# Optimizing a Trainium2 kernel written in Bass

```python
import numpy as np
import jax
import jax.numpy as jnp

def _softmax(x, axis=-1):
    return jax.nn.softmax(x, axis=axis)

def _gelu(x):
    return jax.nn.gelu(x, approximate=True)

def _silu(x):
    return jax.nn.silu(x)

def _sigmoid(x):
    return jax.nn.sigmoid(x)

def _layernorm(x, axis=-1, eps=1e-05):
    m = jnp.mean(x, axis=axis, keepdims=True)
    v = jnp.var(x, axis=axis, keepdims=True)
    return (x - m) / jnp.sqrt(v + eps)

def _scatter_add(tgt, idx, src, axis=0):
    return tgt.at[idx].add(src)

def _segment_sum(src, seg, n):
    return jax.ops.segment_sum(src, seg, n)
kernel_name = 'mk_vit_tower_d1_tok_img768_r4_a71a41'

def setup_inputs(seed: int=0):
    np.random.seed(seed)
    _w = jnp.asarray

    def _rec_inputs():
        import jax
        import jax.numpy as jnp
        _rk = jax.random.key(seed)
        x = -0.00016672 + 0.999947 * jax.random.normal(jax.random.fold_in(_rk, 1), (32, 3, 96, 96), jnp.float32)
        return x
    x = _rec_inputs()

    def _L0_tok_setup():
        import jax, jax.numpy as jnp
        import numpy as np
        PH = PW = 16
        key = jax.random.key(seed)
        k1, k2, k3 = jax.random.split(key, 3)
        B, C, H, W_ = (64, 3, 96, 96)
        embed_dim = 192
        patch_dim = C * PH * PW
        x = jax.random.normal(k1, (B, C, H, W_), dtype=jnp.float32)
        W = jax.random.normal(k2, (embed_dim, patch_dim), dtype=jnp.float32) * 0.02
        b = jax.random.normal(k3, (embed_dim,), dtype=jnp.float32) * 0.02
        return {'x': x, 'W': W, 'b': b}
    _L0_tok_all = _L0_tok_setup()
    _L0_tok_in = {k: v for k, v in _L0_tok_all.items() if k in ('W', 'b')}
    del _L0_tok_all

    def _L0_attn_setup():
        import jax, jax.numpy as jnp
        import numpy as np
        EPS = 1e-05
        B, T, C = (8, 512, 192)
        H = 4 * C
        LAYER_ID, N_LAYER = (4, 12)

        def _ln(x, w, b):
            mu = x.mean(-1, keepdims=True)
            var = ((x - mu) ** 2).mean(-1, keepdims=True)
            return (x - mu) / jnp.sqrt(var + EPS) * w + b

        def _wkv_scan(w, k, v):
            a0 = jnp.zeros(k.shape[1:], k.dtype)
            b0 = jnp.zeros_like(a0)
            m0 = jnp.full_like(a0, -1e+38)

            def step(carry, kv):
                a, b, m = carry
                kt, vt = kv
                mm = jnp.maximum(m + w, kt)
                e1 = jnp.exp(m + w - mm)
                e2 = jnp.exp(kt - mm)
                return ((e1 * a + e2 * vt, e1 * b + e2, mm), (a, b, m))
            _, (A, Bd, M) = jax.lax.scan(step, (a0, b0, m0), (k, v))
            return (A, Bd, M)

        def bi_wkv(w, u, k, v):
            kt = jnp.swapaxes(k, 0, 1)
            vt = jnp.swapaxes(v, 0, 1)
            af, bf, mf = _wkv_scan(w, kt, vt)
            ab, bb, mb = _wkv_scan(w, kt[::-1], vt[::-1])
            ab, bb, mb = (ab[::-1], bb[::-1], mb[::-1])
            kk = kt + u
            M = jnp.maximum(jnp.maximum(mf, mb), kk)
            ef = jnp.exp(mf - M)
            eb = jnp.exp(mb - M)
            ec = jnp.exp(kk - M)
            y = (ef * af + eb * ab + ec * vt) / (ef * bf + eb * bb + ec)
            return jnp.swapaxes(y, 0, 1)
        key = jax.random.key(seed)
        ks = jax.random.split(key, 9)
        x = jax.random.normal(ks[0], (B, T, C), jnp.float32)
        r01 = LAYER_ID / (N_LAYER - 1)
        h = np.arange(C, dtype=np.float64)
        decay = (-5.0 + 8.0 * (h / (C - 1)) ** (0.7 + 1.3 * r01)).astype(np.float32)
        zigzag = ((np.arange(C) + 1) % 3 - 1).astype(np.float32) * 0.5
        first = (np.float32(np.log(0.3)) + zigzag).astype(np.float32)
        s = 0.02
        return {'x': x, 'ln1_w': jnp.ones((C,), jnp.float32), 'ln1_b': jnp.zeros((C,), jnp.float32), 'ln2_w': jnp.ones((C,), jnp.float32), 'ln2_b': jnp.zeros((C,), jnp.float32), 'decay': jnp.asarray(decay), 'first': jnp.asarray(first), 'Wk_a': s * jax.random.normal(ks[1], (C, C), jnp.float32), 'Wv_a': s * jax.random.normal(ks[2], (C, C), jnp.float32), 'Wr_a': s * jax.random.normal(ks[3], (C, C), jnp.float32), 'Wo_a': s * jax.random.normal(ks[4], (C, C), jnp.float32), 'Wk_f': s * jax.random.normal(ks[5], (H, C), jnp.float32), 'Wv_f': s * jax.random.normal(ks[6], (C, H), jnp.float32), 'Wr_f': s * jax.random.normal(ks[7], (C, C), jnp.float32)}
    _L0_attn_all = _L0_attn_setup()
    _L0_attn_in = {k: v for k, v in _L0_attn_all.items() if k in ('ln1_w', 'ln1_b', 'ln2_w', 'ln2_b', 'decay', 'first', 'Wk_a', 'Wv_a', 'Wr_a', 'Wo_a', 'Wk_f', 'Wv_f', 'Wr_f')}
    del _L0_attn_all

    def _L0_ffn_setup():
        import jax, jax.numpy as jnp
        import numpy as np
        B, N, D, H, E, HID, TOPK = (8, 197, 192, 12, 8, 768, 2)

        def _layernorm(x, w, b, eps=1e-05):
            mu = jnp.mean(x, axis=-1, keepdims=True)
            var = jnp.mean((x - mu) ** 2, axis=-1, keepdims=True)
            return (x - mu) * jax.lax.rsqrt(var + eps) * w + b
        key = jax.random.key(seed)
        ks = jax.random.split(key, 8)
        s = 0.02
        return {'x': jax.random.normal(ks[0], (B, N, D), jnp.float32), 'norm1_w': jnp.ones((D,), jnp.float32), 'norm1_b': jnp.zeros((D,), jnp.float32), 'qkv_w': jax.random.normal(ks[1], (3 * D, D), jnp.float32) * s, 'qkv_b': jnp.zeros((3 * D,), jnp.float32), 'proj_w': jax.random.normal(ks[2], (D, D), jnp.float32) * s, 'proj_b': jnp.zeros((D,), jnp.float32), 'norm2_w': jnp.ones((D,), jnp.float32), 'norm2_b': jnp.zeros((D,), jnp.float32), 'w_gate': jax.random.normal(ks[3], (D, E), jnp.float32) * s, 'W1': jax.random.normal(ks[4], (E, D, HID), jnp.float32) * s, 'b1': jnp.zeros((E, HID), jnp.float32), 'W2': jax.random.normal(ks[5], (E, HID, D), jnp.float32) * s, 'b2': jnp.zeros((E, D), jnp.float32)}
    _L0_ffn_all = _L0_ffn_setup()
    _L0_ffn_in = {k: v for k, v in _L0_ffn_all.items() if k in ('norm1_w', 'norm1_b', 'qkv_w', 'qkv_b', 'proj_w', 'proj_b', 'norm2_w', 'norm2_b', 'w_gate', 'W1', 'b1', 'W2', 'b2')}
    del _L0_ffn_all
    return {'x': x, 'L0_tok_W': _L0_tok_in['W'], 'L0_tok_b': _L0_tok_in['b'], 'L0_attn_ln1_w': _L0_attn_in['ln1_w'], 'L0_attn_ln1_b': _L0_attn_in['ln1_b'], 'L0_attn_ln2_w': _L0_attn_in['ln2_w'], 'L0_attn_ln2_b': _L0_attn_in['ln2_b'], 'L0_attn_decay': _L0_attn_in['decay'], 'L0_attn_first': _L0_attn_in['first'], 'L0_attn_Wk_a': _L0_attn_in['Wk_a'], 'L0_attn_Wv_a': _L0_attn_in['Wv_a'], 'L0_attn_Wr_a': _L0_attn_in['Wr_a'], 'L0_attn_Wo_a': _L0_attn_in['Wo_a'], 'L0_attn_Wk_f': _L0_attn_in['Wk_f'], 'L0_attn_Wv_f': _L0_attn_in['Wv_f'], 'L0_attn_Wr_f': _L0_attn_in['Wr_f'], 'L0_ffn_norm1_w': _L0_ffn_in['norm1_w'], 'L0_ffn_norm1_b': _L0_ffn_in['norm1_b'], 'L0_ffn_qkv_w': _L0_ffn_in['qkv_w'], 'L0_ffn_qkv_b': _L0_ffn_in['qkv_b'], 'L0_ffn_proj_w': _L0_ffn_in['proj_w'], 'L0_ffn_proj_b': _L0_ffn_in['proj_b'], 'L0_ffn_norm2_w': _L0_ffn_in['norm2_w'], 'L0_ffn_norm2_b': _L0_ffn_in['norm2_b'], 'L0_ffn_w_gate': _L0_ffn_in['w_gate'], 'L0_ffn_W1': _L0_ffn_in['W1'], 'L0_ffn_b1': _L0_ffn_in['b1'], 'L0_ffn_W2': _L0_ffn_in['W2'], 'L0_ffn_b2': _L0_ffn_in['b2']}

def reference(x, L0_tok_W, L0_tok_b, L0_attn_ln1_w, L0_attn_ln1_b, L0_attn_ln2_w, L0_attn_ln2_b, L0_attn_decay, L0_attn_first, L0_attn_Wk_a, L0_attn_Wv_a, L0_attn_Wr_a, L0_attn_Wo_a, L0_attn_Wk_f, L0_attn_Wv_f, L0_attn_Wr_f, L0_ffn_norm1_w, L0_ffn_norm1_b, L0_ffn_qkv_w, L0_ffn_qkv_b, L0_ffn_proj_w, L0_ffn_proj_b, L0_ffn_norm2_w, L0_ffn_norm2_b, L0_ffn_w_gate, L0_ffn_W1, L0_ffn_b1, L0_ffn_W2, L0_ffn_b2):
    import jax
    import jax.numpy as jnp

    def _L0_tok_ref(x, W, b):
        import jax, jax.numpy as jnp
        import numpy as np
        PH = PW = 16
        B, C, H, Wd = x.shape
        Hp, Wp = (H // PH, Wd // PW)
        patches = x.reshape(B, C, Hp, PH, Wp, PW)
        patches = patches.transpose(0, 2, 4, 1, 3, 5).reshape(B, Hp * Wp, C * PH * PW)
        return jnp.einsum('bnp,ep->bne', patches, W) + b

    def _L0_attn_ref(x, ln1_w, ln1_b, ln2_w, ln2_b, decay, first, Wk_a, Wv_a, Wr_a, Wo_a, Wk_f, Wv_f, Wr_f):
        import jax, jax.numpy as jnp
        import numpy as np
        EPS = 1e-05
        B, T, C = (8, 512, 192)
        H = 4 * C
        LAYER_ID, N_LAYER = (4, 12)

        def _ln(x, w, b):
            mu = x.mean(-1, keepdims=True)
            var = ((x - mu) ** 2).mean(-1, keepdims=True)
            return (x - mu) / jnp.sqrt(var + EPS) * w + b

        def _wkv_scan(w, k, v):
            a0 = jnp.zeros(k.shape[1:], k.dtype)
            b0 = jnp.zeros_like(a0)
            m0 = jnp.full_like(a0, -1e+38)

            def step(carry, kv):
                a, b, m = carry
                kt, vt = kv
                mm = jnp.maximum(m + w, kt)
                e1 = jnp.exp(m + w - mm)
                e2 = jnp.exp(kt - mm)
                return ((e1 * a + e2 * vt, e1 * b + e2, mm), (a, b, m))
            _, (A, Bd, M) = jax.lax.scan(step, (a0, b0, m0), (k, v))
            return (A, Bd, M)

        def bi_wkv(w, u, k, v):
            kt = jnp.swapaxes(k, 0, 1)
            vt = jnp.swapaxes(v, 0, 1)
            af, bf, mf = _wkv_scan(w, kt, vt)
            ab, bb, mb = _wkv_scan(w, kt[::-1], vt[::-1])
            ab, bb, mb = (ab[::-1], bb[::-1], mb[::-1])
            kk = kt + u
            M = jnp.maximum(jnp.maximum(mf, mb), kk)
            ef = jnp.exp(mf - M)
            eb = jnp.exp(mb - M)
            ec = jnp.exp(kk - M)
            y = (ef * af + eb * ab + ec * vt) / (ef * bf + eb * bb + ec)
            return jnp.swapaxes(y, 0, 1)
        Bn, Tn, Cn = x.shape
        h = _ln(x, ln1_w, ln1_b)
        k = h @ Wk_a.T
        v = h @ Wv_a.T
        sr = jax.nn.sigmoid(h @ Wr_a.T)
        y = bi_wkv(decay / Tn, first / Tn, k, v)
        x = x + sr * y @ Wo_a.T
        h = _ln(x, ln2_w, ln2_b)
        kf = jnp.square(jax.nn.relu(h @ Wk_f.T))
        x = x + jax.nn.sigmoid(h @ Wr_f.T) * (kf @ Wv_f.T)
        return x

    def _L0_ffn_ref(x, norm1_w, norm1_b, qkv_w, qkv_b, proj_w, proj_b, norm2_w, norm2_b, w_gate, W1, b1, W2, b2):
        import jax, jax.numpy as jnp
        import numpy as np
        B, N, D, H, E, HID, TOPK = (8, 197, 192, 12, 8, 768, 2)

        def _layernorm(x, w, b, eps=1e-05):
            mu = jnp.mean(x, axis=-1, keepdims=True)
            var = jnp.mean((x - mu) ** 2, axis=-1, keepdims=True)
            return (x - mu) * jax.lax.rsqrt(var + eps) * w + b
        Bx, Nx, C = x.shape
        hd = C // H
        scale = hd ** (-0.5)
        xn = _layernorm(x, norm1_w, norm1_b)
        qkv = (xn @ qkv_w.T + qkv_b).reshape(Bx, Nx, 3, H, hd).transpose(2, 0, 3, 1, 4)
        q, k, v = (qkv[0], qkv[1], qkv[2])
        attn = jax.nn.softmax(jnp.einsum('bhqd,bhkd->bhqk', q, k) * scale, axis=-1)
        o = jnp.einsum('bhqk,bhkd->bqhd', attn, v).reshape(Bx, Nx, C)
        x = x + (o @ proj_w.T + proj_b)
        xn2 = _layernorm(x, norm2_w, norm2_b).reshape(-1, C)
        T = xn2.shape[0]
        logits = xn2 @ w_gate
        top_vals, top_idx = jax.lax.top_k(logits, TOPK)
        gates = jax.nn.softmax(top_vals, axis=-1)
        gates_full = jnp.zeros((T, E), xn2.dtype).at[jnp.arange(T)[:, None], top_idx].add(gates)

        def body(acc, p):
            w1, bb1, w2, bb2, g = p
            h = jax.nn.gelu(xn2 @ w1 + bb1, approximate=False)
            return (acc + g[:, None] * (h @ w2 + bb2), None)
        moe_out, _ = jax.lax.scan(body, jnp.zeros_like(xn2), (W1, b1, W2, b2, gates_full.T))
        return x + moe_out.reshape(Bx, Nx, C)
    h = _L0_tok_ref(x, L0_tok_W, L0_tok_b)
    h = h + _L0_attn_ref(_layernorm(h, axis=-1), L0_attn_ln1_w, L0_attn_ln1_b, L0_attn_ln2_w, L0_attn_ln2_b, L0_attn_decay, L0_attn_first, L0_attn_Wk_a, L0_attn_Wv_a, L0_attn_Wr_a, L0_attn_Wo_a, L0_attn_Wk_f, L0_attn_Wv_f, L0_attn_Wr_f)
    h = h + _L0_ffn_ref(_layernorm(h, axis=-1), L0_ffn_norm1_w, L0_ffn_norm1_b, L0_ffn_qkv_w, L0_ffn_qkv_b, L0_ffn_proj_w, L0_ffn_proj_b, L0_ffn_norm2_w, L0_ffn_norm2_b, L0_ffn_w_gate, L0_ffn_W1, L0_ffn_b1, L0_ffn_W2, L0_ffn_b2)
    return h

_drawn_inputs = setup_inputs


def setup_inputs(seed=0):
    import zlib

    import numpy as np

    out = dict(_drawn_inputs(seed))
    spreads = {'L0_attn_ln1_w': (1.0, 0.6),
     'L0_attn_ln1_b': (0.0, 0.8),
     'L0_attn_ln2_w': (1.0, 0.6),
     'L0_attn_ln2_b': (0.0, 0.8),
     'L0_ffn_norm1_w': (1.0, 0.6),
     'L0_ffn_norm1_b': (0.0, 0.8),
     'L0_ffn_qkv_b': (0.0, 0.631),
     'L0_ffn_proj_b': (0.0, 0.581),
     'L0_ffn_norm2_w': (1.0, 0.6),
     'L0_ffn_norm2_b': (0.0, 2.0),
     'L0_ffn_b1': (0.0, 2.0),
     'L0_ffn_b2': (0.0, 0.815)}
    factors = {'L0_attn_decay': 8.0,
     'L0_attn_first': 31.191,
     'L0_attn_Wk_a': 8.0,
     'L0_attn_Wv_a': 8.0,
     'L0_attn_Wr_a': 8.0,
     'L0_attn_Wo_a': 8.0,
     'L0_attn_Wk_f': 3.219,
     'L0_attn_Wv_f': 2.953,
     'L0_attn_Wr_f': 8.0,
     'L0_ffn_qkv_w': 7.914,
     'L0_ffn_proj_w': 3.899,
     'L0_ffn_W1': 3.608}
    for name, (base, spread) in spreads.items():
        noise = np.random.default_rng([zlib.crc32(name.encode()), seed]).standard_normal(out[name].shape)
        drawn = base * np.exp(spread * noise) if base else spread * noise
        out[name] = jnp.asarray(drawn.astype(out[name].dtype))
    for name, factor in factors.items():
        out[name] = (out[name] * factor).astype(out[name].dtype)
    return out
```

```python
from contextlib import ExitStack

import concourse.bass as bass
from concourse import mybir

F32 = mybir.dt.float32
I32 = mybir.dt.int32
U32 = mybir.dt.uint32
ALU = mybir.AluOpType
ACT = mybir.ActivationFunctionType
AX = mybir.AxisListType

B, NT, C = 32, 36, 192
TOK = B * NT
PD = 768
KP = PD // 128
G = 4
GI = B // G
GT = GI * NT
T = 96
GTILES = GT // T
TILES = TOK // T
C1 = C - 128
HID = 768
HB = HID // 128
NH, HD = 12, 16
HS = 3
NS = NH // HS
E = 8
MT = (2 * TOK + E * 127) // 128
EPS = 1e-5
FAR = -1e38

CI = 16
IC = CI + CI // 2
PITCH = NT + 1
WL = IC * PITCH + 1
WS = WL + 1
WN = IC * NT

CONST = [("ident", 128), ("iota", 128), ("before", T), ("ones", T), ("head0", 8), ("head1", 4),
         ("slab", C), ("slot", MT + 1), ("token", TILES), ("spare", 1), ("keep", E * TILES),
         ("tile", TILES), ("power", 6)]
CHAN = ["ln1_w", "ln1_b", "ln2_w", "ln2_b", "n1_w", "n1_b", "n2_w", "n2_b", "decay", "first",
        "q_b", "k_b", "v_b"]


def offsets(parts):
    at, out = 0, {}
    for name, n in parts:
        out[name] = (at, n)
        at += n
    return out, at


CAT, CN = offsets(CONST)
VAT = {name: 2 * i for i, name in enumerate(CHAN)}


def schedule():
    def front(g):
        return [("tok", g), ("stats", "a", g), ("apply", "a", g), ("turn", "a", g), ("kvr", g)]

    def ffn(g):
        return [[("wo", g), ("stats", "2", g)], [("apply", "2", g), ("turn", "2", g)], [("ff", g)],
                [("stats", "b", g)]]

    def keys(g):
        return [[("apply", "b", g)], [("turn", "b", g), ("qk", g)]]

    def attention(g):
        pairs = range(GI // 2 * g, GI // 2 * (g + 1))
        out = [[("score", pairs[0])]]
        for p in pairs[1:]:
            out.append([("score", p), ("value", p - 1)])
        out.append([("value", pairs[-1])])
        return out

    def back(g):
        return [[("proj", g), ("stats", "g", g)], [("apply", "g", g), ("turn", "g", g), ("logits", g)]]

    def weave(*lists):
        out, n = [], max(len(x) for x in lists)
        at = [0] * len(lists)
        for i in range(n):
            for k, x in enumerate(lists):
                while at[k] < (i + 1) * len(x) / n:
                    out += x[at[k]]
                    at[k] += 1
        return out

    def wkv(c):
        return [[("wkv", c, i)] for i in range(WKV_PARTS)]

    s = front(0) + front(1)
    s += weave(wkv(0), [[x] for x in front(2) + front(3)])
    s += weave(wkv(1), ffn(0) + keys(0), ffn(1) + keys(1))
    s += weave(ffn(2), ffn(3), attention(0) + back(0))
    s += weave(keys(2), attention(1) + back(1))
    s += weave(keys(3), attention(2) + back(2))
    s += weave(attention(3) + back(3))
    return s


WKV_PARTS = 7


def jobs_of(step):
    kind, x = step[0], step[-1]
    tiles = range(GTILES * x, GTILES * (x + 1))
    if kind == "tok":
        return [("tok", t) for t in tiles]
    if kind == "turn":
        return [("turn", step[1], x, b) for b in range(2)]
    if kind == "kvr":
        return [("kvr", x, w, b) for w in range(3) for b in range(2)]
    if kind == "wo":
        return [("wo", t) for t in tiles]
    if kind == "ff":
        return [("kf", x, m) for m in range(HB)] + [("rv", t) for t in tiles]
    if kind == "qk":
        return [(n, x, b) for n in ("q", "k") for b in range(2)]
    if kind == "score":
        return [("s", x), ("v", x)]
    if kind == "value":
        return [("pt", x), ("pv", x), ("ot", x)]
    if kind == "proj":
        return [("proj", t) for t in tiles]
    if kind == "logits":
        return [("lg", x)]
    return []


def moe_jobs():
    out = [("rank",), ("gturn",)] + [("b2", t) for t in range(TILES)] + [("list",), ("xt", 0), ("h", 0, 0), ("h", 0, 1)]
    for j in range(MT):
        if j + 1 < MT:
            out += [("xt", j + 1), ("h", j + 1, 0), ("h", j + 1, 1)]
        out += [("ht", j, 0), ("ht", j, 1), ("y", j)]
    return out


def build(nc, xp, chan, const, tokw, tokb, kvrw, wow, kfw, rfw, vfw, qkvw, projw, projb, gatew,
          w1a, w1b, w2, b2, out):
    STEPS = schedule()
    JOBS = [j for s in STEPS for j in jobs_of(s)] + moe_jobs()
    NBANK = 8
    PLACE = {j: (n % NBANK, n // NBANK) for n, j in enumerate(JOBS)}
    LNS = [s[1:] for s in STEPS if s[0] == "stats"]
    APPLIED = [s[1:] for s in STEPS if s[0] == "apply"]
    TURNED = [s[1:] for s in STEPS if s[0] == "turn"]
    assert LNS and len(set(JOBS)) == len(JOBS)

    ctx = ExitStack()
    with ctx:
        def sb(name, shape, dt=F32):
            return ctx.enter_context(nc.sbuf_tensor(name, shape, dt))

        def sem(name):
            return ctx.enter_context(nc.semaphore(name))

        ARENA = 2 * E * HID + E * HB * C
        arena = sb("arena", [128, ARENA])
        at = [0]

        def carve(n):
            at[0] += n
            assert at[0] <= ARENA
            return arena[:, at[0] - n:at[0]]

        K, KU, V, ER = ([carve(WS) for _ in range(2)] for _ in range(4))
        W, MF, MB, E1F, E1B, E2F, E2B, EVF, EVB = (carve(WS) for _ in range(9))
        P3 = carve(3 * WN)
        Z = [carve(WN) for _ in range(2)]
        TOKW = carve(KP * C)
        W1A = arena[:, 0:E * HID].rearrange("p (e n) -> p e n", e=E)
        W1B = arena[:, E * HID:2 * E * HID].rearrange("p (e n) -> p e n", e=E)
        W2 = arena[:, 2 * E * HID:ARENA].rearrange("p (e n) -> p e n", e=E)
        patch = sb("patch", [128, G * KP * GT])
        XP = patch[:, :].rearrange("p (g k t) -> p g k t", g=G, k=KP)
        KE = [patch[:, i * GI * NH * NT:(i + 1) * GI * NH * NT] for i in range(2)]
        ffn = sb("ffn", [128, HB * GT + GTILES * C + 2 * HID])
        KF = ffn[:, 0:HB * GT].rearrange("p (m t) -> p m t", m=HB)
        TH = ffn[:, HB * GT:HB * GT + GTILES * C].rearrange("p (t c) -> p t c", t=GTILES)
        KFW = ffn[:, HB * GT + GTILES * C:].rearrange("p (b n) -> p b n", b=2)
        KVRW = sb("kvrw", [128, 2, 3 * C])
        WOW = sb("wow", [128, 2, C])
        RFW = sb("rfw", [128, 2, C])
        VFW = sb("vfw", [128, HB, C])
        QKVW = sb("qkvw", [128, 2, 3 * C])
        PROJW = sb("projw", [128, 2, C])
        HTB = KVRW[:, :, :].rearrange("p b n -> p (b n)").rearrange("p (r b t) -> p r b t", r=2, b=2)
        GATEW = sb("gatew", [128, 2, E])
        CH = sb("chans", [128, 2 * len(CHAN)])
        WU = sb("wu", [128, 4])
        CO = sb("consts", [128, CN])
        TOKB = sb("tokb_s", [T, C])
        PROJB = sb("projb_s", [T, C])
        B2 = sb("b2_s", [T, C])
        H = sb("h", [T, TILES, C])
        X = sb("x", [T, TILES, C])
        XH = sb("xh", [T, 2 * GTILES, C])
        HT = sb("ht", [128, 2, 2, GT])
        ST = sb("st", [T, TILES, 6])
        MV = sb("mv", [T, TILES, 2])
        VA = sb("va", [T, G, 2, GTILES])
        RS = sb("rs", [T, G, 2, GTILES])
        QT = sb("qt", [128, 2, 2, GT + 32])
        KT = sb("kt", [128, 2, 2, GT])
        HR = sb("hr", [128, 2, 2, 2 * HS * NT])
        VE = sb("ve", [108, 2, 2 * C])
        S = sb("s", [128, 2, NH * NT])
        MX = sb("mx", [128, 2, NH])
        SUM = sb("sum", [128, 2, NH])
        RI = sb("ri", [128, 2, NH])
        PT = sb("pt", [108, 2, 512])
        O = sb("o", [128, 2, C])
        OT = sb("ot", [128, 2, 2, GT])
        LG = sb("lg", [T, TILES, E])
        TOP = sb("top", [T, TILES, E])
        TIX = sb("tix", [T, TILES, E], U32)
        banks = ctx.enter_context(nc.psum_tensor("banks", [128, NBANK, 512], F32))

        names = ["chan", "const", "tokw", "tokb", "kvrw", "wow", "kfw", "rfw", "vfw", "qkvw", "projw",
                 "projb", "gatew", "b2", "w1a", "w1b", "w2"]
        loaded = {n: sem("loaded_" + n) for n in names}
        patch_loaded = [sem(f"patch_loaded{g}") for g in range(G)]
        bank_full = [sem(f"bank_full{b}") for b in range(NBANK)]
        bank_free = [sem(f"bank_free{b}") for b in range(NBANK)]
        cleared = sem("cleared")
        dve_step = sem("dve_step")
        act_step = sem("act_step")
        pool_step = sem("pool_step")
        wu_ready = sem("wu_ready")
        var_ready = sem("var_ready")
        rstd_ready = sem("rstd_ready")
        xh_ready = sem("xh_ready")
        ht_ready = sem("ht_ready")
        kvr_ready = sem("kvr_ready")
        diff_ready = sem("diff_ready")
        exp_ready = sem("exp_ready")
        z_ready = sem("z_ready")
        x1_ready = sem("x1_ready")
        hx_ready = sem("hx_ready")
        kf_ready = sem("kf_ready")
        th_ready = sem("th_ready")
        h_ready = sem("h_ready")
        xb_ready = sem("xb_ready")
        xpb_ready = sem("xpb_ready")
        qk_ready = sem("qk_ready")
        ke_ready = sem("ke_ready")
        ve_ready = sem("ve_ready")
        hr_ready = sem("hr_ready")
        sub_ready = sem("sub_ready")
        p_ready = sem("p_ready")
        ri_ready = sem("ri_ready")
        pt_ready = sem("pt_ready")
        o_ready = sem("o_ready")
        ot_ready = sem("ot_ready")
        x2_ready = sem("x2_ready")
        base_ready = sem("base_ready")
        xh_stored = sem("xh_stored")
        top_ready = sem("top_ready")
        e2_ready = sem("e2_ready")
        mask_ready = sem("mask_ready")
        gf_ready = sem("gf_ready")
        gft_ready = sem("gft_ready")
        gm_ready = sem("gm_ready")
        table_ready = sem("table_ready")
        index_ready = sem("index_ready")
        out_ready = sem("out_ready")
        base_stored = sem("base_stored")
        gathered = sem("gathered")
        xt_ready = sem("xt_ready")
        hs_ready = sem("hs_ready")
        hst_ready = sem("hst_ready")
        yg_ready = sem("yg_ready")
        scattered = sem("scattered")

        def full(eng, job):
            b, n = PLACE[job]
            eng.wait_ge(bank_full[b], n + 1)
            return banks[:, b, :]

        def freed(ins, job):
            ins.then_inc(bank_free[PLACE[job][0]], 1)

        def after_freed(eng, job):
            b, n = PLACE[job]
            eng.wait_ge(bank_free[b], n + 1)

        def const_(name, rows=128):
            a, n = CAT[name]
            return CO[0:rows, a:a + n]

        def chan_(name, b, lo=0, hi=None):
            a = VAT[name] + b
            return CH[lo:(128 if b == 0 else C1) if hi is None else hi, a:a + 1]

        class Chain:

            def __init__(self, eng, s):
                self.eng, self.s, self.n = eng, s, 0

            def then(self, ins):
                self.n += 1
                ins.then_inc(self.s, 1)

            def settle(self):
                self.eng.wait_ge(self.s, self.n)

            def step(self, ins):
                self.then(ins)
                self.settle()

        def bc(ap, shape):
            return ap.to_broadcast(shape)

        def here(x):
            return x[:, 1:1 + IC * PITCH].rearrange("p (i t) -> p i t", t=PITCH)[:, :, 0:NT]

        def before(x):
            return x[:, 0:IC * PITCH].rearrange("p (i t) -> p i t", t=PITCH)[:, :, 0:NT]

        def behind(x):
            return x[:, 2:2 + IC * PITCH].rearrange("p (i t) -> p i t", t=PITCH)[:, :, 0:NT]

        def dense(x):
            return x.rearrange("p (i t) -> p i t", t=NT)

        def group_tiles(g):
            return range(GTILES * g, GTILES * (g + 1))

        rat = [0]

        def rcarve(n):
            rat[0] += n
            assert rat[0] <= G * KP * GT
            return patch[0:T, rat[0] - n:rat[0]]

        NC2 = 2 * TILES
        ONEB = rcarve(NC2 * 128).rearrange("p (i b) -> p i b", b=128)
        RT = rcarve(NC2 * 2 * MT).rearrange("p (i a) -> p i a", a=2 * MT)
        GE = rcarve(NC2 * (MT + 1)).rearrange("p (i a) -> p i a", a=MT + 1)
        AA = rcarve(NC2 * MT).rearrange("p (i a) -> p i a", a=MT)
        GM = rcarve(TILES * T).rearrange("p (t k) -> p t k", t=TILES)
        qat = {"q": 0, "k": 0}

        def qcarve(n, where="q"):
            whole = (QT if where == "q" else KT)[:, :, :, :].rearrange("p a b t -> p (a b t)")
            qat[where] += n
            assert qat[where] <= whole.shape[1]
            return whole[:, qat[where] - n:qat[where]]

        M1, M2, M12, GF, TOTC, CUM, SF, TMP = (qcarve(TILES * E)[0:T] for _ in range(8))
        GFT = qcarve(T)[0:T]
        IXF, DD, GG, NE8, TE8, END, BASE, SL, AQ, BB = (qcarve(NC2)[0:T] for _ in range(10))
        CMP = qcarve(E * TILES)[0:T].rearrange("p (e t) -> p e t", e=E)
        EJC = qcarve(MT * E, "k")[0:T].rearrange("p (j e) -> p j e", e=E)
        EJ = qcarve(MT, "k")[0:T]
        assert MT <= 32 and 128 * 9 >= TOK

        fat = [0]

        def fcarve(n):
            fat[0] += n
            assert fat[0] <= ffn.shape[1]
            return ffn[:, fat[0] - n:fat[0]]

        XG, YG = ([qcarve(C, "k") for _ in range(2)] for _ in range(2))
        XT = [fcarve(256).rearrange("p (b t) -> p b t", b=2) for _ in range(2)]
        LST = fcarve(2 * MT)
        LT2 = fcarve(2 * MT).rearrange("p (a j) -> p a j", a=2)
        IG, IS, EJI = (fcarve(MT).bitcast(I32) for _ in range(3))
        HSB = [fcarve(HID) for _ in range(2)]
        HST = [fcarve(HID) for _ in range(2)]

        xh_dram = nc.dram_tensor("xh_scratch", [TOK, C], F32).ap()

        block = ctx.enter_context(nc.Block())

        @block.sync
        def _(sp):
            def load(name, dst, src):
                sp.dma_start(dst, src).then_inc(loaded[name], 16)

            load("tokw", TOKW, tokw)
            for g in range(G):
                sp.dma_start(XP[:, g], xp[:, g]).then_inc(patch_loaded[g], 16)
                if g == 0:
                    load("tokb", TOKB[:, :], tokb)
                    load("const", CO[:, :], const)
                    load("chan", CH[:, :], chan)
                    load("kvrw", KVRW[:, :, :], kvrw)
            load("wow", WOW[:, :, :], wow)
            load("kfw", KFW, kfw)
            load("rfw", RFW[:, :, :], rfw)
            load("vfw", VFW[:, :, :], vfw)
            load("qkvw", QKVW[:, :, :], qkvw)
            load("projw", PROJW[:, :, :], projw)
            load("projb", PROJB[:, :], projb)
            load("gatew", GATEW[:, :, :], gatew)
            load("b2", B2[:, :], b2)
            full(sp, ("wo", TILES - 1))
            full(sp, ("wo", TILES - GTILES - 1))
            load("w1a", W1A, w1a)
            load("w1b", W1B[0:C1 + 1], w1b)
            load("w2", W2, w2)
            for n, (kind, g) in enumerate(APPLIED):
                if kind == "g":
                    sp.wait_ge(xh_ready, n + 1)
                    sp.dma_start(xh_dram[GT * g:GT * (g + 1), :].rearrange("(t p) c -> p t c", p=T),
                                 XH[:, GTILES * (g % 2):GTILES * (g % 2 + 1), :]).then_inc(xh_stored, 16)
            sp.wait_ge(out_ready, TILES + 1)
            sp.dma_start(out[0:TOK, :].rearrange("(t p) c -> p t c", p=T), H[:, :, :]).then_inc(base_stored, 16)
            sp.dma_start(out[TOK:TOK + 128, :], O[:, 0, :]).then_inc(base_stored, 16)
            sp.wait_ge(base_stored, 32)
            sp.wait_ge(scattered, 16 * MT)

        @block.gpsimd
        def _(pool):
            ch = Chain(pool, pool_step)
            for x in (E1F, E1B, E2F, E2B, EVF, EVB):
                ch.then(pool.memset(x, 0.0))
            for x in K:
                ch.then(pool.memset(x, FAR))
            ch.then(pool.memset(W, 2 * FAR))
            ch.then(pool.memset(QT[:, :, :, GT:GT + 32], 0.0))
            ch.settle()
            pool.sem_inc(cleared, 1)
            pool.wait_ge(loaded["const"], 16)
            pool.wait_ge(loaded["projb"], 16)

            nstat = nx1 = nxb = nqk = nx2 = 0
            for step in STEPS:
                kind, g = step[0], step[-1]
                if kind == "stats":
                    n = 2 if step[1] in "ab" else 1
                    pool.wait_ge(var_ready, nstat + 1)
                    src = VA[:, g, 0:n, :].rearrange("p a t -> p (a t)")
                    dst = RS[:, g, 0:n, :].rearrange("p a t -> p (a t)")
                    pool.tensor_tensor(dst, src, const_("power", T)[:, 0:n * GTILES], ALU.pow).then_inc(rstd_ready, 1)
                    nstat += 1
                if kind == "stats" and step[1] == "2":
                    pool.wait_ge(x1_ready, nx1 + 1)
                    nx1 += 1
                    sl = slice(GTILES * g, GTILES * (g + 1))
                    pool.tensor_tensor(H[:, sl, :], H[:, sl, :], X[:, sl, :], ALU.add).then_inc(hx_ready, 1)
                if kind == "apply" and step[1] == "b":
                    pool.wait_ge(xb_ready, nxb + 1)
                    nxb += 1
                    sl = slice(GTILES * g, GTILES * (g + 1))
                    pool.tensor_tensor(X[:, sl, :], X[:, sl, :], bc(PROJB[:, :].unsqueeze(1), [T, GTILES, C]),
                                       ALU.add).then_inc(xpb_ready, 1)
                if kind == "qk":
                    pool.wait_ge(qk_ready, 2 * (nqk + 1))
                    nqk += 1
                    if g == 0:
                        full(pool, ("tok", TILES - 1))
                    if g >= 2:
                        full(pool, ("s", (g - 1) * GI // 2 - 1))
                    for b, heads in ((0, 8), (1, 4)):
                        rows = 128 if b == 0 else C1
                        at_ = 0 if b == 0 else GI * 8 * NT
                        ke = KE[g % 2][0:rows, at_:at_ + GI * heads * NT].rearrange("p (i h t) -> p i h t", i=GI, h=heads)
                        src = KT[0:rows, g % 2, b, :].rearrange("p (i t) -> p i t", i=GI)
                        for h in range(heads):
                            m = const_(f"head{b}", rows)[:, h:h + 1]
                            ch.then(pool.tensor_scalar(ke[:, :, h, :], src, m, None, ALU.mult))
                    ch.settle()
                    pool.sem_inc(ke_ready, 1)
                if kind == "score":
                    gg, q = divmod(g, GI // 2)
                    pool.wait_ge(ht_ready, 2 * (TURNED.index(("b", gg)) + 1))
                    if g >= 2:
                        full(pool, ("v", g - 2))
                    for b in range(2):
                        rows = 128 if b == 0 else C1
                        src = HTB[0:rows, gg % 2, b, 2 * NT * q:2 * NT * (q + 1)].rearrange("p (a t) -> p a t", a=2)
                        dst = HR[0:rows, g % 2, b, :].rearrange("p (a s t) -> p a s t", a=2, s=HS)
                        pool.tensor_copy(dst, bc(src.unsqueeze(2), [rows, 2, HS, NT])).then_inc(hr_ready, 1)
                if kind == "stats" and step[1] == "g":
                    pool.wait_ge(x2_ready, nx2 + 1)
                    nx2 += 1
                    sl = slice(GTILES * g, GTILES * (g + 1))
                    pool.tensor_tensor(H[:, sl, :], H[:, sl, :], X[:, sl, :], ALU.add).then_inc(base_ready, 1)

            pool.wait_ge(index_ready, 1)
            pool.wait_ge(xh_stored, 16 * G)

            def gather(j):
                if j >= 2:
                    full(pool, ("xt", j - 2))
                pool.indirect_dma_start(XG[j % 2], None, xh_dram[:, :],
                                        bass.IndirectOffsetOnAxis(ap=IG[:, j:j + 1], axis=0)).then_inc(gathered, 16)
                pool.wait_ge(gathered, 16 * (j + 1))

            def scatter(j):
                pool.wait_ge(yg_ready, j + 1)
                if j == 0:
                    pool.wait_ge(base_stored, 32)
                else:
                    pool.wait_ge(scattered, 16 * j)
                pool.indirect_dma_start(out[:, :], bass.IndirectOffsetOnAxis(ap=IS[:, j:j + 1], axis=0),
                                        YG[j % 2], None, compute_op=ALU.add).then_inc(scattered, 16)

            gather(0)
            gather(1)
            for j in range(MT):
                if j + 2 < MT:
                    gather(j + 2)
                scatter(j)
            pool.wait_ge(scattered, 16 * MT)

        @block.scalar
        def _(act):
            ch = Chain(act, act_step)
            A = act.activation
            act.wait_ge(loaded["chan"], 16)
            act.wait_ge(cleared, 1)
            nturn = nexp = 0
            affine = {"a": ("ln1_w", "ln1_b"), "2": ("ln2_w", "ln2_b"), "b": ("n1_w", "n1_b"), "g": ("n2_w", "n2_b")}

            for step in STEPS:
                kind, g = step[0], step[-1]
                if kind == "turn":
                    w, b_ = affine[step[1]]
                    for job in ht_readers(STEPS, step):
                        full(act, job)
                    for b in range(2):
                        rows = 128 if b == 0 else C1
                        job = ("turn", step[1], g, b)
                        ps = full(act, job)
                        ht = HTB if step[1] == "b" else HT
                        ins = A(ht[0:rows, g % 2, b, :], ps[0:rows, 0:GT], ACT.Identity, bias=chan_(b_, b), scale=chan_(w, b))
                        freed(ins, job)
                        after_freed(act, job)
                        act.sem_inc(ht_ready, 1)
                    nturn += 1
                if kind == "kvr":
                    c, half = divmod(g, 2)
                    if g == 0:
                        act.wait_ge(wu_ready, 1)
                    for w in range(3):
                        for b in range(2):
                            job = ("kvr", g, w, b)
                            ps = full(act, job)
                            lo, hi = (0, 128) if b == 0 else (C1 * half, C1 * half + C1)
                            cols = slice(GI * half, GI * half + GI) if b == 0 else slice(CI, IC)
                            src = ps[lo:hi, 0:GT].rearrange("p (i t) -> p i t", t=NT)

                            def dst(x):
                                return here(x)[lo:hi, cols, :]

                            if w == 0:
                                ch.then(A(dst(K[c]), src, ACT.Identity))
                                ins = A(dst(KU[c]), src, ACT.Identity, bias=WU[lo:hi, 2 + b:3 + b])
                            elif w == 1:
                                ins = A(dst(V[c]), src, ACT.Identity)
                            else:
                                ins = A(dst(ER[c]), src, ACT.Exp, scale=-1.0)
                            freed(ins, job)
                            after_freed(act, job)
                    ch.settle()
                    act.sem_inc(kvr_ready, 1)
                if kind == "wkv" and step[2] in EXPS:
                    for what in EXPS[step[2]]:
                        act.wait_ge(diff_ready, nexp + 1)
                        nexp += 1
                        if what == "p":
                            A(P3, P3, ACT.Exp).then_inc(exp_ready, 1)
                        elif what in ("e2f", "e2b"):
                            x = here(E2F if what == "e2f" else E2B)
                            A(x, x, ACT.Exp).then_inc(exp_ready, 1)
                        else:
                            x = here(E1F if what == "e1f" else E1B)
                            ch.step(A(x[:, 0:CI, :], x[:, 0:CI, :], ACT.Exp, bias=WU[:, 0:1]))
                            A(x[:, CI:IC, :], x[:, CI:IC, :], ACT.Exp, bias=WU[:, 1:2]).then_inc(exp_ready, 1)
                if kind == "ff":
                    if ffs(STEPS, g):
                        full(act, ("rv", GTILES * ffs(STEPS, g)[0] + GTILES - 1))
                    for m in range(HB):
                        job = ("kf", g, m)
                        ps = full(act, job)
                        freed(A(KF[:, m, :], ps[:, 0:GT], ACT.Relu), job)
                        after_freed(act, job)
                        A(KF[:, m, :], KF[:, m, :], ACT.Square).then_inc(kf_ready, 1)
                    if ffs(STEPS, g):
                        act.wait_ge(h_ready, ffs(STEPS, g)[1])
                    for i, t in enumerate(group_tiles(g)):
                        ps = full(act, ("rv", t))
                        A(TH[0:T, i, :], ps[0:T, 0:C], ACT.Tanh, scale=0.5).then_inc(th_ready, 1)
                if kind == "qk":
                    for n, dst in (("q", QT), ("k", KT)):
                        if n == "q" and g >= 2:
                            full(act, ("s", (g - 1) * GI // 2 - 1))
                        if n == "k" and g >= 2:
                            act.wait_ge(ke_ready, g - 1)
                        for b in range(2):
                            rows = 128 if b == 0 else C1
                            job = (n, g, b)
                            ps = full(act, job)
                            ins = A(dst[0:rows, g % 2, b, 0:GT], ps[0:rows, 0:GT], ACT.Identity, bias=chan_(n + "_b", b))
                            freed(ins, job)
                            after_freed(act, job)
                        act.sem_inc(qk_ready, 1)
                if kind == "score":
                    p = step[1]
                    act.wait_ge(sub_ready, p + 1)
                    A(S[:, p % 2, :], S[:, p % 2, :], ACT.Exp, scale=HD ** -0.5).then_inc(p_ready, 1)
                if kind == "value":
                    p = step[1]
                    job = ("pt", p)
                    ps = full(act, job)
                    if p >= 2:
                        full(act, ("pv", p - 2))
                    freed(A(PT[:, p % 2, :], ps[0:108, :], ACT.Copy), job)
                    after_freed(act, job)
                    act.sem_inc(pt_ready, 1)
                    job = ("ot", p)
                    ps = full(act, job)
                    gg, q = divmod(p, GI // 2)
                    if q == 0 and gg >= 2:
                        full(act, ("proj", GTILES * (gg - 1) - 1))
                    for b in range(2):
                        rows = 128 if b == 0 else C1
                        src = ps[0:rows, 128 * b:128 * b + 128].rearrange("p (a q) -> p a q", a=2)[:, :, 0:NT]
                        dst = OT[0:rows, gg % 2, b, 2 * NT * q:2 * NT * (q + 1)].rearrange("p (a q) -> p a q", a=2)
                        ins = A(dst, src, ACT.Identity, bias=chan_("v_b", b))
                        if b == 0:
                            ch.step(ins)
                        else:
                            freed(ins, job)
                    after_freed(act, job)
                    act.sem_inc(ot_ready, 1)

            act.wait_ge(top_ready, 1)
            A(DD[:, 0:TILES], DD[:, 0:TILES], ACT.Exp).then_inc(e2_ready, 1)
            act.wait_ge(out_ready, TILES + 1)
            def turned(j):
                job = ("xt", j)
                ps = full(act, job)
                if j >= 2:
                    full(act, ("h", j - 2, 1))
                ch.step(A(XT[j % 2][:, 0, :], ps[:, 0:128], ACT.Identity, bias=chan_("n2_b", 0), scale=chan_("n2_w", 0)))
                freed(A(XT[j % 2][0:C1, 1, :], ps[0:C1, 128:256], ACT.Identity, bias=chan_("n2_b", 1), scale=chan_("n2_w", 1)), job)
                after_freed(act, job)
                act.sem_inc(xt_ready, 1)

            def gelu(j):
                if j >= 2:
                    full(act, ("ht", j - 2, 1))
                for i in range(2):
                    job = ("h", j, i)
                    ps = full(act, job)
                    freed(A(HSB[j % 2][:, 384 * i:384 * (i + 1)], ps[:, 0:384], ACT.Gelu), job)
                    after_freed(act, job)
                    act.sem_inc(hs_ready, 1)

            turned(0)
            gelu(0)
            for j in range(MT):
                if j + 1 < MT:
                    turned(j + 1)
                    gelu(j + 1)

        @block.vector
        def _(dve):
            ch = Chain(dve, dve_step)
            TTR, TS, STT, CP, RED = dve.tensor_tensor, dve.tensor_scalar, dve.scalar_tensor_tensor, dve.tensor_copy, dve.tensor_reduce
            dve.wait_ge(loaded["chan"], 16)
            dve.wait_ge(loaded["const"], 16)
            dve.wait_ge(cleared, 1)
            ch.step(TS(WU[:, 0:4], CH[:, VAT["decay"]:VAT["decay"] + 4], 1.0 / NT, None, ALU.mult))
            ch.step(dve.memset(here(W), 0.0))
            ch.step(TS(here(W)[:, 0:CI, :], here(W)[:, 0:CI, :], WU[:, 0:1], None, ALU.add))
            ch.step(TS(here(W)[:, CI:IC, :], here(W)[:, CI:IC, :], WU[:, 1:2], None, ALU.add))
            dve.sem_inc(wu_ready, 1)
            dve.wait_ge(loaded["tokb"], 16)

            def tok(g):
                for t in group_tiles(g):
                    ps = full(dve, ("tok", t))
                    freed(TTR(H[:, t, :], ps[0:T, 0:C], TOKB[:, :], ALU.add), ("tok", t))
                for t in group_tiles(g):
                    after_freed(dve, ("tok", t))

            def stats(kind, g):
                src = H if kind in "ab" else X
                for t in group_tiles(g):
                    ch.then(dve.bn_stats(ST[:, t, :], src[:, t, :]))
                ch.settle()
                for t in group_tiles(g):
                    ch.then(dve.bn_aggr(MV[:, t, :], ST[:, t, :]))
                ch.settle()
                var = MV[:, GTILES * g:GTILES * (g + 1), 1]
                ins = TS(VA[:, g, 0, :], var, EPS, None, ALU.add)
                if kind in "ab":
                    ch.then(ins)
                    ins = TS(VA[:, g, 1, :], var, 1.0 + EPS, EPS * EPS, ALU.mult, ALU.add)
                    ch.step(ins)
                    dve.sem_inc(var_ready, 1)
                else:
                    ins.then_inc(var_ready, 1)

            def apply(kind, g):
                n = LNS.index((kind, g))
                k = APPLIED.index((kind, g))
                dve.wait_ge(rstd_ready, n + 1)
                earlier = [i for i in range(k) if APPLIED[i][1] % 2 == g % 2]
                if earlier:
                    kk, gg = APPLIED[earlier[-1]]
                    full(dve, ("turn", kk, gg, 1))
                    stored = sum(APPLIED[i][0] == "g" for i in range(k) if APPLIED[i][1] % 2 == g % 2)
                    if stored:
                        dve.wait_ge(xh_stored, 16 * sum(APPLIED[i][0] == "g" for i in range(earlier[-1] + 1)))
                src = H if kind in "ab" else X
                for i, t in enumerate(group_tiles(g)):
                    xh = XH[:, GTILES * (g % 2) + i, :]
                    m = MV[:, t, 0:1]
                    s = RS[:, g, 1 if kind in "ab" else 0, i:i + 1]
                    ch.then(TS(xh, src[:, t, :], m, s, ALU.subtract, ALU.mult))
                ch.settle()
                dve.sem_inc(xh_ready, 1)
                if kind in "ab":
                    for i, t in enumerate(group_tiles(g)):
                        ch.then(TS(X[:, t, :], H[:, t, :], MV[:, t, 0:1], RS[:, g, 0, i:i + 1], ALU.subtract, ALU.mult))
                    ch.settle()
                    if kind == "b":
                        dve.sem_inc(xb_ready, 1)

            nexp = [0]

            def ready(ins):
                ins.then_inc(diff_ready, 1)

            def exped(n):
                dve.wait_ge(exp_ready, n)

            def wkv(c, part):
                k, ku, v, er = K[c], KU[c], V[c], ER[c]
                e0 = 5 * c
                p = [dense(P3[:, i * WN:(i + 1) * WN]) for i in range(3)]
                t1, t2 = dense(MF[:, 0:WN]), dense(MB[:, 0:WN])
                rev = slice(None, None, -1)
                if part == 0:
                    dve.wait_ge(kvr_ready, 2 * (c + 1))
                    ch.then(dve.tensor_tensor_scan(MF[:, 0:WL], W[:, 0:WL], k[:, 0:WL], FAR, ALU.add, ALU.max))
                    ch.step(dve.tensor_tensor_scan(MB[:, 0:WL][:, rev], W[:, 0:WL][:, rev], k[:, 0:WL][:, rev], FAR, ALU.add, ALU.max))
                if part == 1:
                    ready(TTR(here(E1F), before(MF), here(MF), ALU.subtract))
                    ready(TTR(here(E2F), here(k), here(MF), ALU.subtract))
                    ready(TTR(here(E1B), behind(MB), here(MB), ALU.subtract))
                    ready(TTR(here(E2B), here(k), here(MB), ALU.subtract))
                if part == 2:
                    ch.step(TTR(p[0], here(ku), before(MF), ALU.max))
                    ch.step(TTR(p[2], p[0], behind(MB), ALU.max))
                    ch.then(TTR(p[0], before(MF), p[2], ALU.subtract))
                    ch.then(TTR(p[1], behind(MB), p[2], ALU.subtract))
                    ch.settle()
                    ready(TTR(p[2], here(ku), p[2], ALU.subtract))
                if part == 3:
                    exped(e0 + 2)
                    ch.step(TTR(here(EVF), here(E2F), here(v), ALU.mult))
                    ch.then(dve.tensor_tensor_scan(EVF[:, 0:WL], E1F[:, 0:WL], EVF[:, 0:WL], 0.0, ALU.mult, ALU.add))
                    ch.step(dve.tensor_tensor_scan(E2F[:, 0:WL], E1F[:, 0:WL], E2F[:, 0:WL], 0.0, ALU.mult, ALU.add))
                if part == 4:
                    exped(e0 + 4)
                    ch.step(TTR(here(EVB), here(E2B), here(v), ALU.mult))
                    ch.then(dve.tensor_tensor_scan(EVB[:, 0:WL][:, rev], E1B[:, 0:WL][:, rev], EVB[:, 0:WL][:, rev], 0.0, ALU.mult, ALU.add))
                    ch.step(dve.tensor_tensor_scan(E2B[:, 0:WL][:, rev], E1B[:, 0:WL][:, rev], E2B[:, 0:WL][:, rev], 0.0, ALU.mult, ALU.add))
                if part == 5:
                    exped(e0 + 5)
                    ch.then(TTR(t1, p[0], before(EVF), ALU.mult))
                    ch.step(TTR(t2, p[1], behind(EVB), ALU.mult))
                    ch.step(TTR(t1, t1, t2, ALU.add))
                    ch.step(TTR(t2, p[2], here(v), ALU.mult))
                    ch.then(TTR(t1, t1, t2, ALU.add))
                    ch.then(TTR(p[0], p[0], before(E2F), ALU.mult))
                    ch.step(TTR(p[1], p[1], behind(E2B), ALU.mult))
                    ch.step(TTR(p[0], p[0], p[1], ALU.add))
                    ch.step(TTR(p[0], p[0], p[2], ALU.add))
                if part == 6:
                    ch.step(STT(p[1], here(er), 1.0, p[0], ALU.add, ALU.mult))
                    ch.step(dve.reciprocal(p[0], p[1]))
                    TTR(dense(Z[c]), t1, p[0], ALU.mult).then_inc(z_ready, 1)
                    dve.wait_ge(z_ready, c + 1)

            def wo(g):
                for t in group_tiles(g):
                    ps = full(dve, ("wo", t))
                    freed(TTR(X[:, t, :], ps[0:T, 0:C], X[:, t, :], ALU.add), ("wo", t))
                for t in group_tiles(g):
                    after_freed(dve, ("wo", t))
                dve.sem_inc(x1_ready, 1)

            nth, nff, nproj = [0], [0], [0]

            def ff(g):
                for i, t in enumerate(group_tiles(g)):
                    ps = full(dve, ("rv", t))
                    dve.wait_ge(th_ready, nth[0] + i + 1)
                    freed(STT(TH[0:T, i, :], TH[0:T, i, :], 1.0, ps[0:T, C:2 * C], ALU.add, ALU.mult), ("rv", t))
                nth[0] += GTILES
                nff[0] += 1
                dve.wait_ge(hx_ready, nff[0])
                for i, t in enumerate(group_tiles(g)):
                    after_freed(dve, ("rv", t))
                    ch.then(STT(H[:, t, :], TH[0:T, i, :], 0.5, H[:, t, :], ALU.mult, ALU.add))
                ch.settle()
                dve.sem_inc(h_ready, 1)

            def score(p):
                ps = full(dve, ("s", p))[:, 0:NH * NT].rearrange("p (h k) -> p h k", h=NH)
                e = S[:, p % 2, :].rearrange("p (h k) -> p h k", h=NH)
                ch.step(RED(MX[:, p % 2, :], ps, AX.X, ALU.max))
                if p >= 2:
                    full(dve, ("pt", p - 2))
                    full(dve, ("pv", p - 2))
                freed(TTR(e, ps, bc(MX[:, p % 2, :].unsqueeze(2), [128, NH, NT]), ALU.subtract), ("s", p))
                after_freed(dve, ("s", p))
                dve.sem_inc(sub_ready, 1)
                pv = full(dve, ("v", p))[0:108, 0:2 * C].rearrange("p (a c) -> p a c", a=2)
                freed(TTR(VE[:, p % 2, :].rearrange("p (a c) -> p a c", a=2), pv,
                          bc(const_("slab", 108).unsqueeze(1), [108, 2, C]), ALU.mult), ("v", p))
                after_freed(dve, ("v", p))
                dve.sem_inc(ve_ready, 1)
                dve.wait_ge(p_ready, p + 1)
                ch.step(RED(SUM[:, p % 2, :], e, AX.X, ALU.add))
                ch.step(dve.reciprocal(RI[:, p % 2, :], SUM[:, p % 2, :]))

            def value(p):
                ps = full(dve, ("pv", p))[:, 0:C].rearrange("p (h d) -> p h d", h=NH)
                if p >= 2:
                    full(dve, ("ot", p - 2))
                freed(TTR(O[:, p % 2, :].rearrange("p (h d) -> p h d", h=NH), ps,
                          bc(RI[:, p % 2, :].unsqueeze(2), [128, NH, HD]), ALU.mult), ("pv", p))
                after_freed(dve, ("pv", p))
                dve.sem_inc(o_ready, 1)

            def proj(g):
                nproj[0] += 1
                dve.wait_ge(xpb_ready, projs(STEPS, g))
                for t in group_tiles(g):
                    ps = full(dve, ("proj", t))
                    freed(TTR(X[:, t, :], ps[0:T, 0:C], X[:, t, :], ALU.add), ("proj", t))
                for t in group_tiles(g):
                    after_freed(dve, ("proj", t))
                dve.sem_inc(x2_ready, 1)

            def logits(g):
                ps = full(dve, ("lg", g))[0:T, 0:GTILES * E].rearrange("p (t e) -> p t e", e=E)
                freed(CP(LG[:, GTILES * g:GTILES * (g + 1), :], ps), ("lg", g))
                after_freed(dve, ("lg", g))
                for t in group_tiles(g):
                    ch.then(dve.max(TOP[:, t, :], LG[:, t, :]))
                ch.settle()
                for t in group_tiles(g):
                    ch.then(dve.max_index(TIX[:, t, :], TOP[:, t, :], LG[:, t, :]))
                ch.settle()

            for step in STEPS:
                kind, x = step[0], step[-1]
                if kind == "tok":
                    tok(x)
                elif kind == "stats":
                    stats(step[1], x)
                elif kind == "apply":
                    apply(step[1], x)
                elif kind == "wkv":
                    wkv(step[1], step[2])
                elif kind == "wo":
                    wo(x)
                elif kind == "ff":
                    ff(x)
                elif kind == "score":
                    score(x)
                elif kind == "value":
                    value(x)
                elif kind == "proj":
                    proj(x)
                elif kind == "logits":
                    logits(x)

            def te(x):
                return x.rearrange("p (t e) -> p t e", e=E)

            iota = const_("iota", T)
            ch.step(TTR(DD[:, 0:TILES], TOP[:, :, 1], TOP[:, :, 0], ALU.subtract))
            dve.sem_inc(top_ready, 1)
            ixf = IXF.rearrange("p (c t) -> p c t", c=2)
            ch.step(CP(ixf, TIX[:, :, 0:2].rearrange("p t c -> p c t")))
            m1, m2, m12, gf, sf, tmp = (te(x[:, :]) for x in (M1, M2, M12, GF, SF, TMP))
            i8 = bc(iota[:, 0:E].unsqueeze(1), [T, TILES, E])
            ch.then(TTR(m1, i8, bc(ixf[:, 0, :].unsqueeze(2), [T, TILES, E]), ALU.is_equal))
            ch.step(TTR(m2, i8, bc(ixf[:, 1, :].unsqueeze(2), [T, TILES, E]), ALU.is_equal))
            ch.step(TTR(m12, m1, m2, ALU.add))
            dve.sem_inc(mask_ready, 1)
            dve.wait_ge(e2_ready, 1)
            g12 = GG.rearrange("p (c t) -> p c t", c=2)
            ch.step(TS(DD[:, TILES:NC2], DD[:, 0:TILES], 1.0, None, ALU.add))
            ch.step(dve.reciprocal(g12[:, 0, :], DD[:, TILES:NC2]))
            ch.step(TTR(g12[:, 1, :], g12[:, 0, :], DD[:, 0:TILES], ALU.mult))
            ch.then(TTR(gf, m1, bc(g12[:, 0, :].unsqueeze(2), [T, TILES, E]), ALU.mult))
            ch.step(TTR(tmp, m2, bc(g12[:, 1, :].unsqueeze(2), [T, TILES, E]), ALU.mult))
            ch.step(TTR(gf, gf, tmp, ALU.add))
            dve.sem_inc(gf_ready, 1)
            ps = full(dve, ("rank",))
            et = lambda x: x.rearrange("p (e t) -> p e t", e=E)
            ch.step(CP(et(TOTC[:, :]), ps[0:T, T:2 * T].rearrange("p (t e) -> p e t", e=E)))
            ch.step(dve.tensor_tensor_scan(CUM[:, :], const_("keep", T), TOTC[:, :], 0.0, ALU.mult, ALU.add))
            ch.then(CP(NE8[:, 0:E], et(CUM[:, :])[:, :, TILES - 1]))
            ch.step(TTR(TOTC[:, :], CUM[:, :], TOTC[:, :], ALU.subtract))
            slot = const_("slot", T)
            n9 = TOK // 128
            ch.step(TTR(CMP[:, :, 0:n9], bc(NE8[:, 0:E].unsqueeze(2), [T, E, n9]), bc(slot[:, 0:n9].unsqueeze(1), [T, E, n9]), ALU.is_gt))
            ch.step(RED(TE8[:, 0:E], CMP[:, :, 0:n9], AX.X, ALU.add))
            ch.step(dve.tensor_tensor_scan(END[:, 0:E], const_("ones", T)[:, 0:E], TE8[:, 0:E], 0.0, ALU.mult, ALU.add))
            ch.step(TTR(BASE[:, 0:E], END[:, 0:E], TE8[:, 0:E], ALU.subtract))
            ch.step(TS(BASE[:, 0:E], BASE[:, 0:E], 128.0, None, ALU.mult))
            freed(TTR(sf, ps[0:T, 0:T].rearrange("p (t e) -> p t e", e=E), et(TOTC[:, :]).rearrange("p e t -> p t e"), ALU.add), ("rank",))
            after_freed(dve, ("rank",))
            ch.step(TTR(sf, sf, bc(BASE[:, 0:E].unsqueeze(1), [T, TILES, E]), ALU.add))
            for c, m in enumerate((m1, m2)):
                ch.step(TTR(tmp, m, sf, ALU.mult))
                ch.step(RED(SL[:, TILES * c:TILES * (c + 1)], tmp, AX.X, ALU.add))
            ch.step(TTR(GE, bc(SL.unsqueeze(2), [T, NC2, MT + 1]), bc(slot[:, 0:MT + 1].unsqueeze(1), [T, NC2, MT + 1]), ALU.is_ge))
            ch.then(TTR(AA, GE[:, :, 0:MT], GE[:, :, 1:MT + 1], ALU.subtract))
            ch.step(RED(AQ, GE[:, :, 1:MT + 1], AX.X, ALU.add))
            ch.step(STT(BB, AQ, -128.0, SL, ALU.mult, ALU.add))
            token = const_("token", T)
            for c in range(2):
                sl = slice(TILES * c, TILES * (c + 1))
                ch.then(TTR(RT[:, sl, 0:MT], AA[:, sl, :], bc(token.unsqueeze(2), [T, TILES, MT]), ALU.mult))
                ch.then(TTR(RT[:, sl, MT:2 * MT], AA[:, sl, :], bc(g12[:, c, :].unsqueeze(2), [T, TILES, MT]), ALU.mult))
            for i in range(NC2):
                ch.then(TS(ONEB[:, i, :], iota, BB[:, i:i + 1], None, ALU.is_equal))
            ch.settle()
            dve.sem_inc(table_ready, 1)
            ch.step(TTR(EJC[:, :, :], bc(iota[:, 0:MT].unsqueeze(2), [T, MT, E]), bc(END[:, 0:E].unsqueeze(1), [T, MT, E]), ALU.is_ge))
            ch.step(RED(EJ[:, :], EJC[:, :, :], AX.X, ALU.add))
            ch.step(TS(EJI[0:T, :], EJ[:, :], float(E - 1), None, ALU.min))
            ps = full(dve, ("gturn",))
            freed(CP(GFT[:, :], ps[0:T, 0:T]), ("gturn",))
            after_freed(dve, ("gturn",))
            for t in range(TILES):
                ch.then(TS(GM[:, t, :], GFT[:, :], const_("tile", T)[:, t:t + 1], None, ALU.mult))
            ch.then(dve.memset(O[:, 0, :], 0.0))
            for j in range(2):
                ch.then(dve.memset(XT[j][C1:C1 + 1, 1, :], 1.0))
            ch.settle()
            dve.sem_inc(gm_ready, 1)
            dve.wait_ge(base_ready, G)
            for t in range(TILES):
                ps = full(dve, ("b2", t))
                freed(TTR(H[:, t, :], ps[0:T, 0:C], H[:, t, :], ALU.add), ("b2", t))
                after_freed(dve, ("b2", t))
                dve.sem_inc(out_ready, 1)
            dve.sem_inc(out_ready, 1)
            ps = full(dve, ("list",))
            freed(CP(LST[:, :], ps[:, 0:2 * MT]), ("list",))
            after_freed(dve, ("list",))
            ch.then(TS(LT2[:, 0, :], LST[:, 0:MT], -1.0, 0.0, ALU.add, ALU.max))
            ch.then(TS(LT2[:, 1, :], LST[:, 0:MT], 0.0, const_("spare"), ALU.is_equal, ALU.mult))
            ch.settle()
            ch.then(CP(IG[:, :], LT2[:, 0, :]))
            ch.then(STT(IS[:, :], LST[:, 0:MT], -1.0, LT2[:, 1, :], ALU.add, ALU.add))
            ch.settle()
            dve.sem_inc(index_ready, 1)

            def hst(j):
                if j >= 2:
                    full(dve, ("y", j - 2))
                for i in range(2):
                    job = ("ht", j, i)
                    ps = full(dve, job)
                    freed(CP(HST[j % 2][:, 384 * i:384 * (i + 1)], ps[:, 0:384]), job)
                    after_freed(dve, job)
                    dve.sem_inc(hst_ready, 1)

            for j in range(MT):
                hst(j)
                if j >= 2:
                    dve.wait_ge(scattered, 16 * (j - 1))
                ps = full(dve, ("y", j))
                freed(TS(YG[j % 2], ps[:, 0:C], LST[:, MT + j:MT + j + 1], None, ALU.mult), ("y", j))
                after_freed(dve, ("y", j))
                dve.sem_inc(yg_ready, 1)

        @block.tensor
        def _(pe):
            ident = const_("ident")
            mm = pe.matmul

            def begin(job):
                b, n = PLACE[job]
                if n:
                    pe.wait_ge(bank_free[b], n)
                return banks[:, b, :]

            def end(ins, job):
                ins.then_inc(bank_full[PLACE[job][0]], 1)

            for n in ("tokw", "const"):
                pe.wait_ge(loaded[n], 16)
            tw = TOKW.rearrange("p (k c) -> p k c", k=KP)

            def over_channels(dst, wt, act_, cols, base=0, moving=None):
                mm(dst, act_[0], wt[0], start=True, stop=False)
                return mm(dst, act_[1], wt[1], start=False, stop=True)

            def w_(wt, lo, hi, base=0):
                return wt[:, 0, lo:hi], wt[base:base + C1, 1, lo:hi]

            def h_(g, lo, hi, ht=HT):
                return ht[:, g % 2, 0, lo:hi], ht[0:C1, g % 2, 1, lo:hi]

            seen = set()

            def need(*ns):
                for n in ns:
                    if n not in seen:
                        pe.wait_ge(loaded[n], 16)
                        seen.add(n)

            nqk = [0]
            for step in STEPS:
                kind, g = step[0], step[-1]
                if kind == "tok":
                    pe.wait_ge(patch_loaded[g], 16)
                    for i, t in enumerate(group_tiles(g)):
                        ps = begin(("tok", t))
                        for k in range(KP):
                            ins = mm(ps[0:T, 0:C], XP[:, g, k, T * i:T * (i + 1)], tw[:, k, :], start=(k == 0), stop=(k == KP - 1))
                        end(ins, ("tok", t))
                elif kind == "turn":
                    pe.wait_ge(xh_ready, APPLIED.index(step[1:]) + 1)
                    for b in range(2):
                        job = ("turn", step[1], g, b)
                        ps = begin(job)
                        rows = 128 if b == 0 else C1
                        for i in range(GTILES):
                            ins = pe.transpose(ps[0:rows, T * i:T * (i + 1)], XH[:, GTILES * (g % 2) + i, 128 * b:128 * b + rows], ident[0:T, 0:T])
                        end(ins, job)
                elif kind == "kvr":
                    need("kvrw")
                    pe.wait_ge(ht_ready, 2 * (TURNED.index(("a", g)) + 1))
                    for w in range(3):
                        for b in range(2):
                            ps = begin(("kvr", g, w, b))
                            lo, n = C * w + 128 * b, 128 if b == 0 else C1
                            base = 0 if b == 0 else C1 * (g % 2)
                            end(over_channels(ps[base:base + n, 0:GT], h_(g, 0, GT), w_(KVRW, lo, lo + n), None), ("kvr", g, w, b))
                elif kind == "wo":
                    need("wow")
                    c, half = divmod(g, 2)
                    pe.wait_ge(z_ready, c + 1)
                    base = C1 * half
                    for i, t in enumerate(group_tiles(g)):
                        ps = begin(("wo", t))
                        z0 = Z[c][:, GT * half + T * i:GT * half + T * (i + 1)]
                        z1 = Z[c][base:base + C1, CI * NT + T * i:CI * NT + T * (i + 1)]
                        end(over_channels(ps[0:T, 0:C], w_(WOW, 0, C, base), (z0, z1), None), ("wo", t))
                elif kind == "ff":
                    need("kfw", "rfw", "vfw")
                    pe.wait_ge(ht_ready, 2 * (TURNED.index(("2", g)) + 1))
                    for m in range(HB):
                        ps = begin(("kf", g, m))
                        end(over_channels(ps[:, 0:GT], h_(g, 0, GT), w_(KFW, 128 * m, 128 * (m + 1)), None), ("kf", g, m))
                    nth = ffs(STEPS, g)[1] if ffs(STEPS, g) else 0
                    for i, t in enumerate(group_tiles(g)):
                        ps = begin(("rv", t))
                        over_channels(ps[0:T, 0:C], w_(RFW, 0, C), h_(g, T * i, T * (i + 1)), None)
                        if i == 0:
                            pe.wait_ge(kf_ready, HB * (nth + 1))
                        for m in range(HB):
                            ins = mm(ps[0:T, C:2 * C], KF[:, m, T * i:T * (i + 1)], VFW[:, m, :], start=(m == 0), stop=(m == HB - 1))
                        end(ins, ("rv", t))
                elif kind == "qk":
                    need("qkvw")
                    pe.wait_ge(ht_ready, 2 * (TURNED.index(("b", g)) + 1))
                    for w, n in enumerate("qk"):
                        for b in range(2):
                            ps = begin((n, g, b))
                            rows = 128 if b == 0 else C1
                            lo = C * w + 128 * b
                            end(over_channels(ps[0:rows, 0:GT], h_(g, 0, GT, HTB), w_(QKVW, lo, lo + rows), None), (n, g, b))
                elif kind == "score":
                    p = g
                    gg, q = divmod(p, GI // 2)
                    pe.wait_ge(ke_ready, qks(STEPS, gg))
                    ps = begin(("s", p))
                    for a in range(2):
                        i = 2 * q + a
                        ke0 = KE[gg % 2][:, 0:GI * 8 * NT].rearrange("p (i n) -> p i n", i=GI)
                        ke1 = KE[gg % 2][0:C1, GI * 8 * NT:].rearrange("p (i n) -> p i n", i=GI)
                        mm(ps[64 * a:64 * a + 64, 0:8 * NT], QT[:, gg % 2, 0, NT * i:NT * i + 64], ke0[:, i, :], start=True, stop=True)
                        ins = mm(ps[64 * a:64 * a + 64, 8 * NT:NH * NT], QT[0:C1, gg % 2, 1, NT * i:NT * i + 64], ke1[:, i, :], start=True, stop=True)
                    end(ins, ("s", p))
                    ps = begin(("v", p))
                    pe.wait_ge(hr_ready, 2 * (p + 1))
                    for a in range(2):
                        h01 = (HR[:, p % 2, 0, 108 * a:108 * (a + 1)], HR[0:C1, p % 2, 1, 108 * a:108 * (a + 1)])
                        ins = over_channels(ps[0:108, C * a:C * (a + 1)], w_(QKVW, 2 * C, 3 * C), h01, None)
                    end(ins, ("v", p))
                elif kind == "value":
                    p = g
                    gg, q = divmod(p, GI // 2)
                    pe.wait_ge(p_ready, p + 1)
                    ps = begin(("pt", p))
                    for s in range(NS):
                        ins = pe.transpose(ps[0:108, 128 * s:128 * (s + 1)], S[:, p % 2, 108 * s:108 * (s + 1)], ident)
                    end(ins, ("pt", p))
                    ps = begin(("pv", p))
                    pe.wait_ge(pt_ready, p + 1)
                    pe.wait_ge(ve_ready, p + 1)
                    for a in range(2):
                        for s in range(NS):
                            ins = mm(ps[64 * a:64 * a + 64, 48 * s:48 * (s + 1)], PT[:, p % 2, 128 * s + 64 * a:128 * s + 64 * a + 64],
                                     VE[:, p % 2, C * a + 48 * s:C * a + 48 * (s + 1)], start=True, stop=True)
                    end(ins, ("pv", p))
                    pe.wait_ge(o_ready, p + 1)
                    ps = begin(("ot", p))
                    pe.transpose(ps[:, 0:128], O[:, p % 2, 0:128], ident)
                    end(pe.transpose(ps[0:C1, 128:256], O[:, p % 2, 128:C], ident), ("ot", p))
                elif kind == "proj":
                    need("projw")
                    pe.wait_ge(ot_ready, GI // 2 * (g + 1))
                    for i, t in enumerate(group_tiles(g)):
                        ps = begin(("proj", t))
                        o0 = OT[:, g % 2, 0, T * i:T * (i + 1)]
                        o1 = OT[0:C1, g % 2, 1, T * i:T * (i + 1)]
                        end(over_channels(ps[0:T, 0:C], w_(PROJW, 0, C), (o0, o1), None), ("proj", t))
                elif kind == "logits":
                    need("gatew")
                    pe.wait_ge(ht_ready, 2 * (TURNED.index(("g", g)) + 1))
                    ps = begin(("lg", g))
                    for i in range(GTILES):
                        ins = over_channels(ps[0:T, E * i:E * (i + 1)], w_(GATEW, 0, E), h_(g, T * i, T * (i + 1)), None)
                    end(ins, ("lg", g))

            pe.wait_ge(mask_ready, 1)
            ps = begin(("rank",))
            mm(ps[0:T, 0:T], const_("before", T), M12[:, :], start=True, stop=True)
            end(mm(ps[0:T, T:2 * T], const_("ones", T), M12[:, :], start=True, stop=True), ("rank",))
            pe.wait_ge(gf_ready, 1)
            ps = begin(("gturn",))
            end(pe.transpose(ps[0:T, 0:T], GF[:, :], ident[0:T, 0:T]), ("gturn",))
            pe.wait_ge(gm_ready, 1)
            need("b2")
            for t in range(TILES):
                ps = begin(("b2", t))
                end(mm(ps[0:T, 0:C], GM[:, t, :], B2[:, :], start=True, stop=True), ("b2", t))
            pe.wait_ge(table_ready, 1)
            ps = begin(("list",))
            for i in range(NC2):
                ins = mm(ps[:, 0:2 * MT], ONEB[:, i, :], RT[:, i, :], start=(i == 0), stop=(i == NC2 - 1))
            end(ins, ("list",))

            need("w1a", "w1b", "w2")

            def up(j, e):
                pe.wait_ge(gathered, 16 * (j + 1))
                ps = begin(("xt", j))
                pe.transpose(ps[:, 0:128], XG[j % 2][:, 0:128], ident)
                end(pe.transpose(ps[0:C1, 128:256], XG[j % 2][:, 128:C], ident), ("xt", j))
                pe.wait_ge(xt_ready, j + 1)
                for i in range(2):
                    ps = begin(("h", j, i))
                    mm(ps[:, 0:384], XT[j % 2][:, 0, :], W1A[:, bass.ds(e, 1), 384 * i:384 * (i + 1)], start=True, stop=False)
                    end(mm(ps[:, 0:384], XT[j % 2][0:C1 + 1, 1, :], W1B[0:C1 + 1, bass.ds(e, 1), 384 * i:384 * (i + 1)],
                           start=False, stop=True), ("h", j, i))

            def down(j, e):
                for i in range(2):
                    pe.wait_ge(hs_ready, 2 * j + i + 1)
                    ps = begin(("ht", j, i))
                    for k in range(3):
                        at_ = 384 * i + 128 * k
                        ins = pe.transpose(ps[:, 128 * k:128 * (k + 1)], HSB[j % 2][:, at_:at_ + 128], ident)
                    end(ins, ("ht", j, i))
                ps = begin(("y", j))
                for k in range(HB):
                    if k % 3 == 0:
                        pe.wait_ge(hst_ready, 2 * j + k // 3 + 1)
                    ins = mm(ps[:, 0:C], HST[j % 2][:, 128 * k:128 * (k + 1)], W2[:, bass.ds(e, 1), C * k:C * (k + 1)],
                             start=(k == 0), stop=(k == HB - 1))
                end(ins, ("y", j))

            def expert(j):
                return pe.value_load(EJI[0:1, j:j + 1], min_val=0, max_val=E - 1)

            e_next = expert(0)
            up(0, e_next)
            for j in range(MT):
                e_now = e_next
                if j + 1 < MT:
                    e_next = expert(j + 1)
                    up(j + 1, e_next)
                down(j, e_now)


EXPS = {1: ("e1f", "e2f", "e1b", "e2b"), 2: ("p",)}


def ffs(steps, g):
    order = [s[-1] for s in steps if s[0] == "ff"]
    n = order.index(g)
    return (order[n - 1], n) if n else None


def qks(steps, g):
    return [s[-1] for s in steps if s[0] == "qk"].index(g) + 1


def projs(steps, g):
    return [s[-1] for s in steps if s[0] == "apply" and s[1] == "b"].index(g) + 1


def ht_readers(steps, step):
    n, kind, g = steps.index(step), step[1], step[2]
    if kind == "b":
        return [("v", (g - 1) * GI // 2 - 1)] if g >= 2 else [("kvr", G - 1, 2, 1)]
    for s in reversed(steps[:n]):
        if s[0] in ("kvr", "ff", "logits") and s[-1] % 2 == g % 2:
            return [jobs_of(s)[-1]]
    return []


def kernel(**inputs):
    import numpy as np
    import concourse.bacc as bacc
    from concourse.bass_utils import run_bass_kernel_spmd

    a = {k: np.asarray(v) for k, v in inputs.items()}

    def blocks(w):
        return np.stack([w[0:128], np.concatenate([w[128:192], w[128:192]])], 1)

    def rows(v, n):
        return np.broadcast_to(v, (n, len(v)))

    qb = a["L0_ffn_qkv_b"]
    vectors = {"ln1_w": a["L0_attn_ln1_w"], "ln1_b": a["L0_attn_ln1_b"], "ln2_w": a["L0_attn_ln2_w"], "ln2_b": a["L0_attn_ln2_b"],
               "n1_w": a["L0_ffn_norm1_w"], "n1_b": a["L0_ffn_norm1_b"], "n2_w": a["L0_ffn_norm2_w"], "n2_b": a["L0_ffn_norm2_b"],
               "decay": a["L0_attn_decay"], "first": a["L0_attn_first"], "q_b": qb[0:C], "k_b": qb[C:2 * C], "v_b": qb[2 * C:]}
    chan = np.concatenate([blocks(vectors[n][:, None])[:, :, 0] for n in CHAN], 1)

    p = np.arange(128)[:, None]
    parts = {
        "ident": np.eye(128), "iota": np.arange(128) + 0 * p, "before": p < np.arange(T), "ones": np.ones((128, T)),
        "head0": p // HD == np.arange(8), "head1": p // HD == np.arange(4),
        "slab": p // NT == (np.arange(C) // HD) % HS, "slot": 128 * np.arange(MT + 1) + 0 * p,
        "token": T * np.arange(TILES) + p + 1, "spare": TOK + 1 + p, "keep": (np.arange(E * TILES) % TILES > 0) + 0 * p,
        "tile": p // E == np.arange(TILES), "power": np.full((128, 6), -0.5)}
    const = np.concatenate([parts[n].astype(np.float32) for n, _ in CONST], 1)

    x = a["x"].reshape(G, GI, 3, 6, 16, 6, 16)
    xp = x.transpose(2, 4, 6, 0, 1, 3, 5).reshape(KP, 128, G, GT).transpose(1, 2, 0, 3)
    w1 = a["L0_ffn_W1"].transpose(1, 0, 2)
    arrays = {
        "xp": xp, "chan": chan, "const": const,
        "tokw": a["L0_tok_W"].T.reshape(KP, 128, C).transpose(1, 0, 2).reshape(128, KP * C), "tokb": rows(a["L0_tok_b"], T),
        "kvrw": blocks(np.concatenate([a["L0_attn_Wk_a"].T, a["L0_attn_Wv_a"].T, a["L0_attn_Wr_a"].T], 1)),
        "wow": blocks(a["L0_attn_Wo_a"].T), "kfw": blocks(a["L0_attn_Wk_f"].T), "rfw": blocks(a["L0_attn_Wr_f"].T),
        "vfw": a["L0_attn_Wv_f"].T.reshape(HB, 128, C).transpose(1, 0, 2),
        "qkvw": blocks(a["L0_ffn_qkv_w"].T), "projw": blocks(a["L0_ffn_proj_w"].T), "projb": rows(a["L0_ffn_proj_b"], T),
        "gatew": blocks(a["L0_ffn_w_gate"]), "w1a": w1[0:128], "w1b": np.concatenate([w1[128:192], a["L0_ffn_b1"][None]]),
        "w2": a["L0_ffn_W2"].reshape(E, HB, 128, C).transpose(2, 0, 1, 3).reshape(128, E, HB * C),
        "b2": np.tile(a["L0_ffn_b2"], (TILES, 1)),
    }
    nc = bacc.Bacc("TRN2", target_bir_lowering=False, num_devices=1)
    data, args = {}, {}
    for name, v in arrays.items():
        data["in_" + name] = np.ascontiguousarray(v)
        args[name] = nc.dram_tensor("in_" + name, v.shape, F32, kind="ExternalInput").ap()
    args["out"] = nc.dram_tensor("out_0", (TOK + 128, C), F32, kind="ExternalOutput").ap()
    build(nc, **args)
    r = run_bass_kernel_spmd(nc, [data], core_ids=[0])
    return r.results[0]["out_0"][0:TOK].reshape(B, NT, C)
```

```python
from contextlib import ExitStack

import concourse.bass as bass
from concourse import mybir

F32 = mybir.dt.float32
I32 = mybir.dt.int32
U32 = mybir.dt.uint32
ALU = mybir.AluOpType
ACT = mybir.ActivationFunctionType
AX = mybir.AxisListType

B, NT, C = 32, 36, 192
TOK = B * NT
PD = 768
KP = PD // 128
G = 4
GI = B // G
GT = GI * NT
T = 96
GTILES = GT // T
TILES = TOK // T
C1 = C - 128
HID = 768
HB = HID // 128
NH, HD = 12, 16
HS = 3
NS = NH // HS
E = 8
MT = (2 * TOK + E * 127) // 128
FULL = 2 * TOK // 128
EPS = 1e-5
FAR = -1e38

CI = 16
IC = CI + CI // 2
PITCH = NT + 1
WL = IC * PITCH + 1
WS = WL + 1
WN = IC * NT

CONST = [("ident", 128), ("iota", 128), ("before", T), ("ones", T), ("head0", 8), ("head1", 4),
         ("slab", C), ("slot", MT + 1), ("token", TILES), ("spare", 1), ("keep", E * TILES),
         ("tile", TILES), ("power", 6)]
CHAN = ["ln1_w", "ln1_b", "ln2_w", "ln2_b", "n1_w", "n1_b", "n2_w", "n2_b", "decay", "first",
        "q_b", "k_b", "v_b"]


def offsets(parts):
    at, out = 0, {}
    for name, n in parts:
        out[name] = (at, n)
        at += n
    return out, at


CAT, CN = offsets(CONST)
VAT = {name: 2 * i for i, name in enumerate(CHAN)}


ORDER = """
tok:0 tok:1 tok:2 tok:3 tok:4 stats:a:0 tok:5 apply:a:0 tok:6 tok:7 resid:a:0 stats:a:1 turn:a:0 tok:8 kvr:2:0
kvr:0:0 apply:a:1 turn:a:1 stats:a:2 resid:a:1 kvr:1:0 kvr:0:1 wkv:0:0 apply:a:2 tok:9 wkv:0:1 tok:10 wexp:0:0
wexp:0:1 turn:a:2 wexp:0:2 tok:11 resid:a:2 wexp:0:3 kvr:1:1 kvr:2:1 evb:0 stats:a:3 wkv:0:2 wexp:0:4 kvr:0:2
apply:a:3 kvr:2:2 turn:a:3 kvr:0:3 resid:a:3 wkv:0:3 wkv:0:4 kvr:1:3 den:0 kvr:1:2 wkv:0:5 wkv:0:6 wkv:1:0 wo:0
stats:2:0 wkv:1:1 apply:2:0 kvr:2:3 wexp:1:0 wkv:1:2 wexp:1:1 turn:2:0 wexp:1:2 wo:1 stats:2:1 kf:0:0 apply:2:1
wkv:1:3 kf:1:0 hx:0 wexp:1:3 evb:1 rv:0 wkv:1:4 turn:2:1 wexp:1:4 rv:1 rv:2 ff:0 kf:0:1 den:1 hx:1 kf:1:1
stats:b:0 wkv:1:5 apply:b:0 rv:3 rv:4 rv:5 turn:b:0 wkv:1:6 ff:1 qk:0 stats:b:1 apply:b:1 wo:3 spread:0 turn:b:1
wo:2 triple:0 s:0 hx:2 resid:b:0 s:1 v:0 stats:2:2 exp:0 triple:1 apply:2:2 v:1 triple:2 hx:3 pt:0 qk:1
stats:2:3 turn:2:2 s:2 exp:1 kf:0:2 apply:2:3 resid:b:1 spread:1 pv:0 pt:1 kf:1:2 pv:1 triple:3 exp:2 rv:6 s:3
turn:2:3 rv:7 ot:0 v:2 exp:3 ot:1 pt:2 v:3 rv:8 s:4 triple:4 pv:2 pt:3 ot:2 pv:3 kf:0:3 ot:3 kf:1:3 ff:2 proj:0
stats:g:0 apply:g:0 rv:9 base:0 rv:10 turn:g:0 exp:4 s:5 stats:b:2 apply:b:2 v:4 logits:0 rv:11 pt:4 exp:5
turn:b:2 pv:4 s:6 ff:3 resid:b:2 triple:5 triple:6 ot:4 pt:5 v:5 v:6 qk:2 exp:6 triple:7 s:7 exp:7 pv:5 ot:5
triple:8 spread:2 v:7 pt:6 pv:6 pt:7 stats:b:3 v:8 triple:9 pv:7 s:8 apply:b:3 triple:10 ot:6 ot:7 s:9 proj:1
stats:g:1 exp:8 exp:9 turn:b:3 resid:b:3 pt:8 apply:g:1 base:1 qk:3 s:10 exp:10 pt:9 pv:8 v:9 v:10 triple:11
s:11 pt:10 pv:9 turn:g:1 ot:8 exp:11 pv:10 pt:11 v:11 logits:1 ot:9 ot:10 pv:11 triple:12 spread:3 v:12 ot:11
proj:2 triple:13 s:12 exp:12 s:13 stats:g:2 exp:13 v:13 apply:g:2 pt:12 triple:14 s:14 pv:12 triple:15 pt:13
turn:g:2 base:2 pv:13 s:15 v:14 exp:14 exp:15 logits:2 ot:12 v:15 pt:14 pt:15 ot:13 pv:14 pv:15 ot:14 ot:15
proj:3 stats:g:3 apply:g:3 turn:g:3 base:3 logits:3
"""


def schedule():
    return [tuple(int(x) if x.isdigit() and not (i == 1 and s[:5] in ("stats", "apply", "resid") or s[:4] == "turn" and i == 1) else x
                  for i, x in enumerate(s.split(":"))) for s in ORDER.split()]


WKV_PARTS = 7


def kf_blocks(half):
    return range(HB // 2 * half, HB // 2 * (half + 1))


def jobs_of(step):
    kind, x = step[0], step[-1]
    tiles = range(GTILES * x, GTILES * (x + 1))
    if kind in ("tok", "rv"):
        return [(kind, x)]
    if kind == "turn":
        return [("turn", step[1], x, b) for b in range(2)]
    if kind == "kvr":
        return [("kvr", x, step[1], b) for b in range(2)]
    if kind == "wo":
        return [("wo", t) for t in tiles]
    if kind == "kf":
        return [("kf", x, m) for m in kf_blocks(step[1])]
    if kind == "qk":
        return [(n, x, b) for n in ("q", "k") for b in range(2)]
    if kind in ("s", "v", "pt", "pv", "ot"):
        return [(kind, x)]
    if kind == "proj":
        return [("proj", t) for t in tiles]
    if kind == "logits":
        return [("lg", x)]
    return []


def moe_jobs():
    out = [("rank",), ("gturn",)] + [("b2", t) for t in range(0, TILES, 2)] + [("list",)]
    out += [("xt", 0), ("xt", 1), ("h", 0, 0), ("h", 0, 1)]
    for j in range(MT):
        if j + 1 < MT:
            out += [("h", j + 1, 0), ("h", j + 1, 1)]
        if j + 2 < MT:
            out.append(("xt", j + 2))
        out.append(("y", j))
    return out


def build(nc, xp, chan, const, tokw, tokb, kvrw, wow, kfw, rfw, vfw, qkvw, projw, projb, gatew,
          w1a, w1b, w2, b2, out):
    STEPS = schedule()
    JOBS = [j for s in STEPS for j in jobs_of(s)] + moe_jobs()
    NBANK = 8
    PLACE = {j: (n % NBANK, n // NBANK) for n, j in enumerate(JOBS)}
    LNS = [s[1:] for s in STEPS if s[0] == "stats"]
    APPLIED = [s[1:] for s in STEPS if s[0] == "apply"]
    TURNED = [s[1:] for s in STEPS if s[0] == "turn"]
    assert LNS and len(set(JOBS)) == len(JOBS)

    ctx = ExitStack()
    with ctx:
        def sb(name, shape, dt=F32):
            return ctx.enter_context(nc.sbuf_tensor(name, shape, dt))

        def sem(name):
            return ctx.enter_context(nc.semaphore(name))

        ARENA = 2 * E * HID + E * HB * C
        arena = sb("arena", [128, ARENA])
        at = [0]

        def carve(n):
            at[0] += n
            assert at[0] <= ARENA
            return arena[:, at[0] - n:at[0]]

        K, KU, V, ER = ([carve(WS) for _ in range(2)] for _ in range(4))
        W, MF, MB, E1F, E1B, E2F, E2B, EVF, EVB = (carve(WS) for _ in range(9))
        P3 = carve(3 * WN)
        Z = [carve(WN) for _ in range(2)]
        TOKW = carve(KP * C)
        W1A = arena[:, 0:E * HID].rearrange("p (e n) -> p e n", e=E)
        W1B = arena[:, E * HID:2 * E * HID].rearrange("p (e n) -> p e n", e=E)
        W2 = arena[:, 2 * E * HID:ARENA].rearrange("p (e n) -> p e n", e=E)
        patch = sb("patch", [128, G * KP * GT])
        XP = patch[:, :].rearrange("p (g k t) -> p g k t", g=G, k=KP)
        KE = [patch[:, i * GI * NH * NT:(i + 1) * GI * NH * NT] for i in range(2)]
        ffn = sb("ffn", [128, HB * GT + GTILES * C + 2 * HID])
        KF = ffn[:, 0:HB * GT].rearrange("p (m t) -> p m t", m=HB)
        TH = ffn[:, HB * GT:HB * GT + GTILES * C].rearrange("p (t c) -> p t c", t=GTILES)
        KFW = ffn[:, HB * GT + GTILES * C:].rearrange("p (b n) -> p b n", b=2)
        KVRW = sb("kvrw", [128, 2, 3 * C])
        WOW = sb("wow", [128, 2, C])
        rvw = sb("rvw", [128, 2 * HID])
        RFW = rvw[:, 0:2 * C].rearrange("p (b n) -> p b n", b=2)
        VFW = rvw[:, 2 * C:2 * C + HB * C].rearrange("p (m n) -> p m n", m=HB)
        QKVW = sb("qkvw", [128, 2, 3 * C])
        PROJW = sb("projw", [128, 2, C])
        HTB = KVRW[:, :, :].rearrange("p b n -> p (b n)").rearrange("p (r b t) -> p r b t", r=2, b=2)
        GATEW = sb("gatew", [128, 2, E])
        CH = sb("chans", [128, 2 * len(CHAN)])
        WU = sb("wu", [128, 4])
        CO = sb("consts", [128, CN])
        TOKB = sb("tokb_s", [T, C])
        PROJB = sb("projb_s", [T, C])
        B2 = sb("b2_s", [T, C])
        H = sb("h", [T, TILES, C])
        X = sb("x", [T, TILES, C])
        XH = sb("xh", [T, 2 * GTILES, C])
        HT = sb("ht", [128, 2, 2, GT])
        ST = sb("st", [T, TILES, 6])
        MV = sb("mv", [T, TILES, 2])
        VA = sb("va", [T, G, 2, GTILES])
        RS = sb("rs", [T, G, 2, GTILES])
        QT = sb("qt", [128, 2, 2, GT + 32])
        KT = sb("kt", [128, 2, 2, GT])
        HR = sb("hr", [128, 2, 2, 2 * HS * NT])
        VE = sb("ve", [108, 2, 2 * C])
        S = sb("s", [128, 2, NH * NT])
        MX = sb("mx", [128, 2, NH])
        SUM = sb("sum", [128, 2, NH])
        RI = sb("ri", [128, 2, NH])
        PT = sb("pt", [108, 2, 512])
        O = sb("o", [128, 2, C])
        OT = sb("ot", [128, 2, 2, GT])
        LG = sb("lg", [T, TILES, E])
        TOP = sb("top", [T, TILES, E])
        TIX = sb("tix", [T, TILES, E], U32)
        banks = ctx.enter_context(nc.psum_tensor("banks", [128, NBANK, 512], F32))

        names = ["chan", "const", "tokw", "tokb", "kvrw", "wow", "kfw", "rfw", "vfw", "qkvw", "projw",
                 "projb", "gatew", "b2", "w1a", "w1b", "w2"]
        loaded = {n: sem("loaded_" + n) for n in names}
        patch_loaded = [sem(f"patch_loaded{g}") for g in range(G)]
        bank_full = [sem(f"bank_full{b}") for b in range(NBANK)]
        bank_free = [sem(f"bank_free{b}") for b in range(NBANK)]
        cleared = sem("cleared")
        dve_step = sem("dve_step")
        act_step = sem("act_step")
        pool_step = sem("pool_step")
        wu_ready = sem("wu_ready")
        var_ready = sem("var_ready")
        rstd_ready = sem("rstd_ready")
        xh_ready = sem("xh_ready")
        diff_ready = sem("diff_ready")
        scan_ready = sem("scan_ready")
        diffb_ready = sem("diffb_ready")
        exp_ready = sem("exp_ready")
        evb_ready = sem("evb_ready")
        den_ready = sem("den_ready")
        z_ready = sem("z_ready")
        hx_ready = sem("hx_ready")
        kf_ready = sem("kf_ready")
        th_ready = sem("th_ready")
        h_ready = sem("h_ready")
        xb_ready = sem("xb_ready")
        xpb_ready = sem("xpb_ready")
        ke_ready = sem("ke_ready")
        hr_ready = sem("hr_ready")
        p_ready = sem("p_ready")
        base_ready = sem("base_ready")
        xh_stored = [sem(f"xh_stored{g}") for g in range(G)]
        top_ready = sem("top_ready")
        e2_ready = sem("e2_ready")
        mask_ready = sem("mask_ready")
        gf_ready = sem("gf_ready")
        gm_ready = sem("gm_ready")
        ge_ready = sem("ge_ready")
        bb_ready = sem("bb_ready")
        aa_ready = sem("aa_ready")
        rt_ready = sem("rt_ready")
        table_ready = sem("table_ready")
        table2_ready = sem("table2_ready")
        index_ready = sem("index_ready")
        base_stored = sem("base_stored")
        gathered = [sem(f"gathered{i}") for i in range(3)]
        scattered = sem("scattered")
        all_added = sem("all_added")
        we_ready = sem("we_ready")

        def full(eng, job):
            b, n = PLACE[job]
            eng.wait_ge(bank_full[b], n + 1)
            return banks[:, b, :]

        def freed(ins, job):
            ins.then_inc(bank_free[PLACE[job][0]], 1)

        def taken(eng, job):
            b, n = PLACE[job]
            eng.wait_ge(bank_free[b], n + 1)

        def const_(name, rows=128):
            a, n = CAT[name]
            return CO[0:rows, a:a + n]

        def chan_(name, b, lo=0, hi=None):
            a = VAT[name] + b
            return CH[lo:(128 if b == 0 else C1) if hi is None else hi, a:a + 1]

        def turned_(eng, kind, g):
            for b in range(2):
                taken(eng, ("turn", kind, g, b))

        class Chain:

            def __init__(self, eng, s):
                self.eng, self.s, self.n = eng, s, 0

            def then(self, ins):
                self.n += 1
                ins.then_inc(self.s, 1)

            def settle(self):
                self.eng.wait_ge(self.s, self.n)

            def step(self, ins):
                self.then(ins)
                self.settle()

        def used(eng):
            return eng.value_load(USED[0:1, 0:1], min_val=FULL, max_val=MT)

        def pair(a):
            return range(a, min(a + 2, MT))

        def bc(ap, shape):
            return ap.to_broadcast(shape)

        def here(x):
            return x[:, 1:1 + IC * PITCH].rearrange("p (i t) -> p i t", t=PITCH)[:, :, 0:NT]

        def before(x):
            return x[:, 0:IC * PITCH].rearrange("p (i t) -> p i t", t=PITCH)[:, :, 0:NT]

        def behind(x):
            return x[:, 2:2 + IC * PITCH].rearrange("p (i t) -> p i t", t=PITCH)[:, :, 0:NT]

        def dense(x):
            return x.rearrange("p (i t) -> p i t", t=NT)

        def group_tiles(g):
            return range(GTILES * g, GTILES * (g + 1))

        rat = [0]

        def rcarve(n):
            rat[0] += n
            assert rat[0] <= G * KP * GT
            return patch[0:T, rat[0] - n:rat[0]]

        NC2 = 2 * TILES
        NDVE = NC2 - 6
        ONEB = rcarve(NC2 * 128).rearrange("p (i b) -> p i b", b=128)
        RT = rcarve(NC2 * 2 * MT).rearrange("p (i a) -> p i a", a=2 * MT)
        GE = rcarve(NC2 * (MT + 1)).rearrange("p (i a) -> p i a", a=MT + 1)
        AA = rcarve(NC2 * MT).rearrange("p (i a) -> p i a", a=MT)
        GM = rcarve(TILES * T).rearrange("p (t k) -> p t k", t=TILES)
        qat = {"q": 0, "k": 0}

        def qcarve(n, where="q"):
            whole = (QT if where == "q" else KT)[:, :, :, :].rearrange("p a b t -> p (a b t)")
            qat[where] += n
            assert qat[where] <= whole.shape[1]
            return whole[:, qat[where] - n:qat[where]]

        M1, M2, M12, GF, TOTC, CUM, SF, TMP = (qcarve(TILES * E)[0:T] for _ in range(8))
        GFT = qcarve(T)[0:T]
        IXF, DD, GG, NE8, TE8, END, BASE, SL, AQ, BB = (qcarve(NC2)[0:T] for _ in range(10))
        CMP = qcarve(E * TILES)[0:T].rearrange("p (e t) -> p e t", e=E)
        EJC = qcarve(MT * E, "k")[0:T].rearrange("p (j e) -> p j e", e=E)
        EJ = qcarve(MT, "k")[0:T]
        assert MT <= 32 and 128 * 9 >= TOK

        fat = [0]

        def fcarve(n):
            fat[0] += n
            assert fat[0] <= ffn.shape[1]
            return ffn[:, fat[0] - n:fat[0]]

        XG = [qcarve(C, "k") for _ in range(3)]
        YG = [S[:, i, 0:C] for i in range(2)]
        XT = [fcarve(256).rearrange("p (b t) -> p b t", b=2) for _ in range(2)]
        LST = fcarve(2 * MT)
        LT2 = fcarve(2 * MT).rearrange("p (a j) -> p a j", a=2)
        IG, IS, EJI = (fcarve(MT).bitcast(I32) for _ in range(3))
        USED = fcarve(1).bitcast(I32)
        HST = [fcarve(HID) for _ in range(2)]
        WE = [x.rearrange("p (b n) -> p b n", b=2) for x in (rvw[:, :], fcarve(2 * HID))]

        xh_dram = nc.dram_tensor("xh_scratch", [TOK, C], F32).ap()

        block = ctx.enter_context(nc.Block())

        @block.sync
        def _(sp):
            def load(name, dst, src):
                sp.dma_start(dst, src).then_inc(loaded[name], 16)

            load("tokw", TOKW, tokw)
            for g in range(G):
                sp.dma_start(XP[:, g], xp[:, g]).then_inc(patch_loaded[g], 16)
                if g == 0:
                    load("tokb", TOKB[:, :], tokb)
                    load("const", CO[:, :], const)
                    load("chan", CH[:, :], chan)
                    load("kvrw", KVRW[:, :, :], kvrw)
            load("wow", WOW[:, :, :], wow)
            load("kfw", KFW, kfw)
            load("rfw", RFW, rfw)
            load("vfw", VFW, vfw)
            load("qkvw", QKVW[:, :, :], qkvw)
            load("projw", PROJW[:, :, :], projw)
            load("projb", PROJB[:, :], projb)
            load("gatew", GATEW[:, :, :], gatew)
            load("b2", B2[:, :], b2)
            full(sp, ("wo", TILES - 1))
            full(sp, ("wo", TILES - GTILES - 1))
            load("w1a", W1A, w1a)
            load("w1b", W1B[0:C1 + 1], w1b)
            load("w2", W2, w2)
            for n, (kind, g) in enumerate(APPLIED):
                if kind == "g":
                    sp.wait_ge(xh_ready, n + 1)
                    sp.dma_start(xh_dram[GT * g:GT * (g + 1), :].rearrange("(t p) c -> p t c", p=T),
                                 XH[:, GTILES * (g % 2):GTILES * (g % 2 + 1), :]).then_inc(xh_stored[g], 16)
            sp.wait_ge(index_ready, 1)
            for t in range(0, TILES, 2):
                taken(sp, ("b2", t))
            sp.dma_start(out[0:TOK, :].rearrange("(t p) c -> p t c", p=T), H[:, :, :]).then_inc(base_stored, 16)
            sp.dma_start(out[TOK:TOK + 128, :], O[:, 0, :]).then_inc(base_stored, 16)
            sp.wait_ge(base_stored, 32)
            sp.wait_ge(all_added, 1)

        @block.gpsimd
        def _(pool):
            ch = Chain(pool, pool_step)
            for x in (E1F, E1B, E2F, E2B, EVF, EVB):
                ch.then(pool.memset(x, 0.0))
            for x in K:
                ch.then(pool.memset(x, FAR))
            ch.then(pool.memset(W, 2 * FAR))
            ch.then(pool.memset(QT[:, :, :, GT:GT + 32], 0.0))
            ch.settle()
            pool.sem_inc(cleared, 1)
            pool.wait_ge(loaded["const"], 16)
            pool.wait_ge(loaded["projb"], 16)

            PTT = pool.tensor_tensor
            nstat = nxb = 0
            for step in STEPS:
                kind, g = step[0], step[-1]
                if kind in ("wkv", "evb", "den"):
                    c = step[1]
                    p = [dense(P3[:, i * WN:(i + 1) * WN]) for i in range(3)]
                if kind == "wkv" and step[2] == 1:
                    pool.wait_ge(scan_ready, 2 * c + 1)
                    PTT(here(E1B), behind(MB), here(MB), ALU.subtract).then_inc(diffb_ready, 1)
                    PTT(here(E2B), here(K[c]), here(MB), ALU.subtract).then_inc(diffb_ready, 1)
                if kind == "evb":
                    pool.wait_ge(exp_ready, 5 * c + 4)
                    for gg in (2 * c, 2 * c + 1):
                        for b in range(2):
                            taken(pool, ("kvr", gg, 1, b))
                    PTT(here(EVB), here(E2B), here(V[c]), ALU.mult).then_inc(evb_ready, 1)
                if kind == "den":
                    pool.wait_ge(exp_ready, 5 * c + 5)
                    pool.wait_ge(scan_ready, 2 * c + 2)
                    ch.then(PTT(here(E1F), p[0], before(E2F), ALU.mult))
                    ch.step(PTT(here(E1B), p[1], behind(E2B), ALU.mult))
                    PTT(here(E1F), here(E1F), here(E1B), ALU.add).then_inc(den_ready, 1)
                if kind == "stats":
                    n = 2 if step[1] in "ab" else 1
                    pool.wait_ge(var_ready, nstat + 1)
                    src = VA[:, g, 0:n, :].rearrange("p a t -> p (a t)")
                    dst = RS[:, g, 0:n, :].rearrange("p a t -> p (a t)")
                    pool.tensor_tensor(dst, src, const_("power", T)[:, 0:n * GTILES], ALU.pow).then_inc(rstd_ready, 1)
                    nstat += 1
                if kind == "hx":
                    for t in group_tiles(g):
                        taken(pool, ("wo", t))
                    sl = slice(GTILES * g, GTILES * (g + 1))
                    pool.tensor_tensor(H[:, sl, :], H[:, sl, :], X[:, sl, :], ALU.add).then_inc(hx_ready, 1)
                if kind == "resid" and step[1] == "b":
                    pool.wait_ge(xb_ready, nxb + 1)
                    nxb += 1
                    sl = slice(GTILES * g, GTILES * (g + 1))
                    pool.tensor_tensor(X[:, sl, :], X[:, sl, :], bc(PROJB[:, :].unsqueeze(1), [T, GTILES, C]),
                                       ALU.add).then_inc(xpb_ready, 1)
                if kind == "base":
                    for t in group_tiles(g):
                        taken(pool, ("proj", t))
                    sl = slice(GTILES * g, GTILES * (g + 1))
                    pool.tensor_tensor(H[:, sl, :], H[:, sl, :], X[:, sl, :], ALU.add).then_inc(base_ready, 1)

            pool.wait_ge(ge_ready, 1)
            pool.tensor_tensor(AA, GE[:, :, 0:MT], GE[:, :, 1:MT + 1], ALU.subtract).then_inc(aa_ready, 1)
            pool.wait_ge(aa_ready, 1)
            token = const_("token", T)
            for c in range(2):
                sl = slice(TILES * c, TILES * (c + 1))
                pool.tensor_tensor(RT[:, sl, 0:MT], AA[:, sl, :], bc(token.unsqueeze(2), [T, TILES, MT]), ALU.mult).then_inc(rt_ready, 1)
            pool.wait_ge(bb_ready, 1)
            for i in range(NDVE, NC2):
                pool.tensor_scalar(ONEB[:, i, :], const_("iota", T), BB[:, i:i + 1], None, ALU.is_equal).then_inc(table2_ready, 1)

            pool.wait_ge(index_ready, 1)
            for g in range(G):
                pool.wait_ge(xh_stored[g], 16)

            def gather(j):
                if j >= 3:
                    full(pool, ("xt", j - 3))
                pool.indirect_dma_start(XG[j % 3], None, xh_dram[:, :],
                                        bass.IndirectOffsetOnAxis(ap=IG[:, j:j + 1], axis=0)).then_inc(gathered[j % 3], 16)

            def scatter(j):
                taken(pool, ("y", j))
                if j == 0:
                    pool.wait_ge(base_stored, 32)
                else:
                    pool.wait_ge(scattered, 16 * j)
                pool.indirect_dma_start(out[:, :], bass.IndirectOffsetOnAxis(ap=IS[:, j:j + 1], axis=0),
                                        YG[j % 2], None, compute_op=ALU.add).then_inc(scattered, 16)

            for j in range(3):
                gather(j)
            for j in range(FULL - 2):
                if j + 3 <= min(FULL, MT - 1):
                    gather(j + 3)
                scatter(j)
            n_used = used(pool)

            def gathers(a):
                if a < MT:
                    with pool.If(n_used > a):
                        for j in (a + 1, a + 2):
                            if j < MT:
                                gather(j)

            def done(n):
                pool.wait_ge(scattered, 16 * n)
                pool.sem_inc(all_added, 1)

            def rest(a):
                if a >= MT:
                    return done(MT)
                with pool.If(n_used > a):
                    gathers(a + 2)
                    for j in pair(a):
                        scatter(j)
                    rest(a + 2)
                with pool.Else():
                    done(a)

            gathers(FULL)
            scatter(FULL - 2)
            scatter(FULL - 1)
            rest(FULL)

        @block.scalar
        def _(act):
            ch = Chain(act, act_step)
            A = act.activation
            act.wait_ge(loaded["chan"], 16)
            act.wait_ge(cleared, 1)
            affine = {"a": ("ln1_w", "ln1_b"), "2": ("ln2_w", "ln2_b"), "b": ("n1_w", "n1_b"), "g": ("n2_w", "n2_b")}

            for step in STEPS:
                kind, g = step[0], step[-1]
                if kind == "turn":
                    w, b_ = affine[step[1]]
                    for job in ht_readers(STEPS, step):
                        full(act, job)
                    for b in range(2):
                        rows = 128 if b == 0 else C1
                        job = ("turn", step[1], g, b)
                        ps = full(act, job)
                        ht = HTB if step[1] == "b" else HT
                        ins = A(ht[0:rows, g % 2, b, :], ps[0:rows, 0:GT], ACT.Identity, bias=chan_(b_, b), scale=chan_(w, b))
                        freed(ins, job)
                if kind == "kvr":
                    c, half = divmod(g, 2)
                    if g == 0:
                        act.wait_ge(wu_ready, 1)
                    for w in step[1:2]:
                        for b in range(2):
                            job = ("kvr", g, w, b)
                            ps = full(act, job)
                            lo, hi = (0, 128) if b == 0 else (C1 * half, C1 * half + C1)
                            cols = slice(GI * half, GI * half + GI) if b == 0 else slice(CI, IC)
                            src = ps[lo:hi, 0:GT].rearrange("p (i t) -> p i t", t=NT)

                            def dst(x):
                                return here(x)[lo:hi, cols, :]

                            if w == 0:
                                ch.then(A(dst(K[c]), src, ACT.Identity))
                                ins = A(dst(KU[c]), src, ACT.Identity, bias=WU[lo:hi, 2 + b:3 + b])
                            elif w == 1:
                                ins = A(dst(V[c]), src, ACT.Identity)
                            else:
                                ins = A(dst(ER[c]), src, ACT.Exp, scale=-1.0)
                            freed(ins, job)
                if kind == "wexp":
                    for what in EXPS[step[2]:step[2] + 1]:
                        c = step[1]
                        if what in ("e1b", "e2b"):
                            act.wait_ge(diffb_ready, 2 * c + step[2] - 1)
                        else:
                            act.wait_ge(diff_ready, 3 * c + min(step[2], 2) + 1)
                        if what == "p":
                            A(P3, P3, ACT.Exp).then_inc(exp_ready, 1)
                        elif what in ("e2f", "e2b"):
                            x = here(E2F if what == "e2f" else E2B)
                            A(x, x, ACT.Exp).then_inc(exp_ready, 1)
                        else:
                            x = here(E1F if what == "e1f" else E1B)
                            ch.step(A(x[:, 0:CI, :], x[:, 0:CI, :], ACT.Exp, bias=WU[:, 0:1]))
                            A(x[:, CI:IC, :], x[:, CI:IC, :], ACT.Exp, bias=WU[:, 1:2]).then_inc(exp_ready, 1)
                if kind == "kf":
                    if ffs(STEPS, g):
                        full(act, ("rv", GTILES * ffs(STEPS, g)[0] + GTILES - 1))
                    lo, *_, hi = kf_blocks(step[1])
                    for m in range(lo, hi + 2):
                        if m <= hi:
                            ps = full(act, ("kf", g, m))
                            freed(A(KF[:, m, :], ps[:, 0:GT], ACT.Relu), ("kf", g, m))
                        if m > lo:
                            taken(act, ("kf", g, m - 1))
                            A(KF[:, m - 1, :], KF[:, m - 1, :], ACT.Square).then_inc(kf_ready, 1)
                if kind == "rv":
                    t = step[1]
                    gg, i = divmod(t, GTILES)
                    if ffs(STEPS, gg):
                        act.wait_ge(h_ready, ffs(STEPS, gg)[1])
                    ps = full(act, ("rv", t))
                    A(TH[0:T, i, :], ps[0:T, 0:C], ACT.Tanh, scale=0.5).then_inc(th_ready, 1)
                if kind == "qk":
                    for n, dst in (("q", QT), ("k", KT)):
                        if n == "q" and g >= 2:
                            full(act, ("s", (g - 1) * GI // 2 - 1))
                        if n == "k" and g >= 2:
                            act.wait_ge(ke_ready, g - 1)
                        for b in range(2):
                            rows = 128 if b == 0 else C1
                            job = (n, g, b)
                            ps = full(act, job)
                            ins = A(dst[0:rows, g % 2, b, 0:GT], ps[0:rows, 0:GT], ACT.Identity, bias=chan_(n + "_b", b))
                            freed(ins, job)
                if kind == "triple":
                    p = step[1]
                    gg, q = divmod(p, GI // 2)
                    turned_(act, "b", gg)
                    if p >= 2:
                        full(act, ("v", p - 2))
                    for b in range(2):
                        rows = 128 if b == 0 else C1
                        src = HTB[0:rows, gg % 2, b, 2 * NT * q:2 * NT * (q + 1)].rearrange("p (a t) -> p a t", a=2)
                        dst = HR[0:rows, p % 2, b, :].rearrange("p (a s t) -> p a s t", a=2, s=HS)
                        A(dst, bc(src.unsqueeze(2), [rows, 2, HS, NT]), ACT.Copy).then_inc(hr_ready, 1)
                if kind == "exp":
                    p = step[1]
                    taken(act, ("s", p))
                    A(S[:, p % 2, :], S[:, p % 2, :], ACT.Exp, scale=HD ** -0.5).then_inc(p_ready, 1)
                if kind == "pt":
                    p = step[1]
                    job = ("pt", p)
                    ps = full(act, job)
                    if p >= 2:
                        full(act, ("pv", p - 2))
                    freed(A(PT[:, p % 2, :], ps[0:108, :], ACT.Copy), job)
                if kind == "ot":
                    p = step[1]
                    job = ("ot", p)
                    ps = full(act, job)
                    gg, q = divmod(p, GI // 2)
                    if q == 0 and gg >= 2:
                        full(act, ("proj", GTILES * (gg - 1) - 1))
                    for b in range(2):
                        rows = 128 if b == 0 else C1
                        src = ps[0:rows, 128 * b:128 * b + 128].rearrange("p (a q) -> p a q", a=2)[:, :, 0:NT]
                        dst = OT[0:rows, gg % 2, b, 2 * NT * q:2 * NT * (q + 1)].rearrange("p (a q) -> p a q", a=2)
                        ins = A(dst, src, ACT.Identity, bias=chan_("v_b", b))
                        if b == 1:
                            freed(ins, job)

            act.wait_ge(top_ready, 1)
            A(DD[:, 0:TILES], DD[:, 0:TILES], ACT.Exp).then_inc(e2_ready, 1)
            ps = full(act, ("gturn",))
            freed(A(GFT[:, :], ps[0:T, 0:T], ACT.Copy), ("gturn",))
            taken(act, ("gturn",))
            for t in range(TILES):
                A(GM[:, t, :], GFT[:, :], ACT.Copy, scale=const_("tile", T)[:, t:t + 1]).then_inc(gm_ready, 1)
            act.wait_ge(index_ready, 1)

            def turned(j):
                job = ("xt", j)
                ps = full(act, job)
                if j >= 2:
                    full(act, ("h", j - 2, 1))
                A(XT[j % 2][:, 0, :], ps[:, 0:128], ACT.Identity, bias=chan_("n2_b", 0), scale=chan_("n2_w", 0))
                freed(A(XT[j % 2][0:C1, 1, :], ps[0:C1, 128:256], ACT.Identity, bias=chan_("n2_b", 1), scale=chan_("n2_w", 1)), job)

            def gelu(j):
                if j >= 2:
                    full(act, ("y", j - 2))
                for i in range(2):
                    job = ("h", j, i)
                    ps = full(act, job)
                    freed(A(HST[j % 2][:, 384 * i:384 * (i + 1)], ps[:, 0:384], ACT.Gelu), job)

            turned(0)
            turned(1)
            gelu(0)
            for j in range(1, FULL):
                gelu(j)
                if j + 1 < MT:
                    turned(j + 1)
            n_used = used(act)

            def rest(a):
                if a < MT:
                    with act.If(n_used > a):
                        for j in pair(a):
                            gelu(j)
                            if j + 1 < MT:
                                turned(j + 1)
                        rest(a + 2)

            rest(FULL)

        @block.vector
        def _(dve):
            ch = Chain(dve, dve_step)
            TTR, TS, STT, CP, RED = dve.tensor_tensor, dve.tensor_scalar, dve.scalar_tensor_tensor, dve.tensor_copy, dve.tensor_reduce
            dve.wait_ge(loaded["chan"], 16)
            dve.wait_ge(loaded["const"], 16)
            dve.wait_ge(cleared, 1)
            ch.step(TS(WU[:, 0:4], CH[:, VAT["decay"]:VAT["decay"] + 4], 1.0 / NT, None, ALU.mult))
            ch.step(dve.memset(here(W), 0.0))
            ch.step(TS(here(W)[:, 0:CI, :], here(W)[:, 0:CI, :], WU[:, 0:1], None, ALU.add))
            ch.step(TS(here(W)[:, CI:IC, :], here(W)[:, CI:IC, :], WU[:, 1:2], None, ALU.add))
            dve.sem_inc(wu_ready, 1)
            dve.wait_ge(loaded["tokb"], 16)

            def tok(t):
                ps = full(dve, ("tok", t))
                freed(TTR(H[:, t, :], ps[0:T, 0:C], TOKB[:, :], ALU.add), ("tok", t))

            def stats(kind, g):
                if kind == "a":
                    for t in group_tiles(g):
                        taken(dve, ("tok", t))
                src = H if kind in "ab" else X
                for t in group_tiles(g):
                    ch.then(dve.bn_stats(ST[:, t, :], src[:, t, :]))
                ch.settle()
                for t in group_tiles(g):
                    ch.then(dve.bn_aggr(MV[:, t, :], ST[:, t, :]))
                ch.settle()
                var = MV[:, GTILES * g:GTILES * (g + 1), 1]
                ins = TS(VA[:, g, 0, :], var, EPS, None, ALU.add)
                if kind in "ab":
                    ch.then(ins)
                    ins = TS(VA[:, g, 1, :], var, 1.0 + EPS, EPS * EPS, ALU.mult, ALU.add)
                    ch.step(ins)
                    dve.sem_inc(var_ready, 1)
                else:
                    ins.then_inc(var_ready, 1)

            def apply(kind, g):
                n = LNS.index((kind, g))
                k = APPLIED.index((kind, g))
                dve.wait_ge(rstd_ready, n + 1)
                earlier = [i for i in range(k) if APPLIED[i][1] % 2 == g % 2]
                if earlier:
                    kk, gg = APPLIED[earlier[-1]]
                    full(dve, ("turn", kk, gg, 1))
                    if kk == "g":
                        dve.wait_ge(xh_stored[gg], 16)
                src = H if kind in "ab" else X
                for i, t in enumerate(group_tiles(g)):
                    xh = XH[:, GTILES * (g % 2) + i, :]
                    m = MV[:, t, 0:1]
                    s = RS[:, g, 1 if kind in "ab" else 0, i:i + 1]
                    ch.then(TS(xh, src[:, t, :], m, s, ALU.subtract, ALU.mult))
                ch.settle()
                dve.sem_inc(xh_ready, 1)

            def resid(kind, g):
                dve.wait_ge(rstd_ready, LNS.index((kind, g)) + 1)
                for i, t in enumerate(group_tiles(g)):
                    ch.then(TS(X[:, t, :], H[:, t, :], MV[:, t, 0:1], RS[:, g, 0, i:i + 1], ALU.subtract, ALU.mult))
                ch.settle()
                if kind == "b":
                    dve.sem_inc(xb_ready, 1)

            def ready(ins):
                ins.then_inc(diff_ready, 1)

            def exped(n):
                dve.wait_ge(exp_ready, n)

            def wkv(c, part):
                k, ku, v, er = K[c], KU[c], V[c], ER[c]
                e0 = 5 * c
                p = [dense(P3[:, i * WN:(i + 1) * WN]) for i in range(3)]
                t1, t2 = dense(MF[:, 0:WN]), dense(MB[:, 0:WN])
                rev = slice(None, None, -1)
                for w in range(3):
                    if part == (0, 3, 6)[w]:
                        for g in (2 * c, 2 * c + 1):
                            for b in range(2):
                                taken(dve, ("kvr", g, w, b))
                if part == 0:
                    ch.then(dve.tensor_tensor_scan(MF[:, 0:WL], W[:, 0:WL], k[:, 0:WL], FAR, ALU.add, ALU.max))
                    ch.step(dve.tensor_tensor_scan(MB[:, 0:WL][:, rev], W[:, 0:WL][:, rev], k[:, 0:WL][:, rev], FAR, ALU.add, ALU.max))
                    dve.sem_inc(scan_ready, 1)
                if part == 1:
                    ready(TTR(here(E1F), before(MF), here(MF), ALU.subtract))
                    ready(TTR(here(E2F), here(k), here(MF), ALU.subtract))
                if part == 2:
                    ch.step(TTR(p[0], here(ku), before(MF), ALU.max))
                    ch.step(TTR(p[2], p[0], behind(MB), ALU.max))
                    ch.then(TTR(p[0], before(MF), p[2], ALU.subtract))
                    ch.then(TTR(p[1], behind(MB), p[2], ALU.subtract))
                    ch.settle()
                    ready(TTR(p[2], here(ku), p[2], ALU.subtract))
                if part == 3:
                    exped(e0 + 2)
                    ch.step(TTR(here(EVF), here(E2F), here(v), ALU.mult))
                    ch.then(dve.tensor_tensor_scan(EVF[:, 0:WL], E1F[:, 0:WL], EVF[:, 0:WL], 0.0, ALU.mult, ALU.add))
                    ch.step(dve.tensor_tensor_scan(E2F[:, 0:WL], E1F[:, 0:WL], E2F[:, 0:WL], 0.0, ALU.mult, ALU.add))
                if part == 4:
                    exped(e0 + 4)
                    dve.wait_ge(evb_ready, c + 1)
                    ch.then(dve.tensor_tensor_scan(EVB[:, 0:WL][:, rev], E1B[:, 0:WL][:, rev], EVB[:, 0:WL][:, rev], 0.0, ALU.mult, ALU.add))
                    ch.step(dve.tensor_tensor_scan(E2B[:, 0:WL][:, rev], E1B[:, 0:WL][:, rev], E2B[:, 0:WL][:, rev], 0.0, ALU.mult, ALU.add))
                    dve.sem_inc(scan_ready, 1)
                if part == 5:
                    exped(e0 + 5)
                    ch.then(TTR(t1, p[0], before(EVF), ALU.mult))
                    ch.step(TTR(t2, p[1], behind(EVB), ALU.mult))
                    ch.step(TTR(t1, t1, t2, ALU.add))
                    ch.step(TTR(t2, p[2], here(v), ALU.mult))
                    ch.step(TTR(t1, t1, t2, ALU.add))
                if part == 6:
                    dve.wait_ge(den_ready, c + 1)
                    ch.step(TTR(p[0], here(E1F), p[2], ALU.add))
                    ch.step(STT(p[1], here(er), 1.0, p[0], ALU.add, ALU.mult))
                    ch.step(dve.reciprocal(p[0], p[1]))
                    TTR(dense(Z[c]), t1, p[0], ALU.mult).then_inc(z_ready, 1)
                    dve.wait_ge(z_ready, c + 1)

            def wo(g):
                for t in group_tiles(g):
                    ps = full(dve, ("wo", t))
                    freed(TTR(X[:, t, :], ps[0:T, 0:C], X[:, t, :], ALU.add), ("wo", t))
                for t in group_tiles(g):
                    taken(dve, ("wo", t))

            nth, nff, nproj = [0], [0], [0]

            def rv(t):
                ps = full(dve, ("rv", t))
                nth[0] += 1
                dve.wait_ge(th_ready, nth[0])
                freed(STT(TH[0:T, t % GTILES, :], TH[0:T, t % GTILES, :], 1.0, ps[0:T, C:2 * C], ALU.add, ALU.mult), ("rv", t))

            def ff(g):
                nff[0] += 1
                dve.wait_ge(hx_ready, nff[0])
                for i, t in enumerate(group_tiles(g)):
                    taken(dve, ("rv", t))
                    ch.then(STT(H[:, t, :], TH[0:T, i, :], 0.5, H[:, t, :], ALU.mult, ALU.add))
                ch.settle()
                dve.sem_inc(h_ready, 1)

            def spread(g):
                if g == 0:
                    full(dve, ("tok", TILES - 1))
                if g >= 2:
                    full(dve, ("s", (g - 1) * GI // 2 - 1))
                for b, heads in ((0, 8), (1, 4)):
                    taken(dve, ("k", g, b))
                    rows = 128 if b == 0 else C1
                    at_ = 0 if b == 0 else GI * 8 * NT
                    ke = KE[g % 2][0:rows, at_:at_ + GI * heads * NT].rearrange("p (i h t) -> p i h t", i=GI, h=heads)
                    src = KT[0:rows, g % 2, b, :].rearrange("p (i t) -> p i t", i=GI)
                    for h in range(heads):
                        ins = TS(ke[:, :, h, :], src, const_(f"head{b}", rows)[:, h:h + 1], None, ALU.mult)
                        if (b, h) == (1, 3):
                            ins.then_inc(ke_ready, 1)

            def score(p):
                ps = full(dve, ("s", p))[:, 0:NH * NT].rearrange("p (h k) -> p h k", h=NH)
                e = S[:, p % 2, :].rearrange("p (h k) -> p h k", h=NH)
                ch.step(RED(MX[:, p % 2, :], ps, AX.X, ALU.max))
                if p >= 2:
                    full(dve, ("pt", p - 2))
                freed(TTR(e, ps, bc(MX[:, p % 2, :].unsqueeze(2), [128, NH, NT]), ALU.subtract), ("s", p))

            def values(p):
                if p >= 2:
                    full(dve, ("pv", p - 2))
                pv = full(dve, ("v", p))[0:108, 0:2 * C].rearrange("p (a c) -> p a c", a=2)
                freed(TTR(VE[:, p % 2, :].rearrange("p (a c) -> p a c", a=2), pv,
                          bc(const_("slab", 108).unsqueeze(1), [108, 2, C]), ALU.mult), ("v", p))

            def sums(p):
                e = S[:, p % 2, :].rearrange("p (h k) -> p h k", h=NH)
                dve.wait_ge(p_ready, p + 1)
                ch.step(RED(SUM[:, p % 2, :], e, AX.X, ALU.add))
                ch.step(dve.reciprocal(RI[:, p % 2, :], SUM[:, p % 2, :]))

            def weighted(p):
                ps = full(dve, ("pv", p))
                if p >= 2:
                    full(dve, ("ot", p - 2))
                for a in range(2):
                    r = slice(64 * a, 64 * a + 64)
                    ins = TTR(O[r, p % 2, :].rearrange("p (h d) -> p h d", h=NH), ps[r, C * a:C * (a + 1)].rearrange("p (h d) -> p h d", h=NH),
                              bc(RI[r, p % 2, :].unsqueeze(2), [64, NH, HD]), ALU.mult)
                freed(ins, ("pv", p))

            def proj(g):
                nproj[0] += 1
                dve.wait_ge(xpb_ready, projs(STEPS, g))
                for t in group_tiles(g):
                    ps = full(dve, ("proj", t))
                    freed(TTR(X[:, t, :], ps[0:T, 0:C], X[:, t, :], ALU.add), ("proj", t))
                for t in group_tiles(g):
                    taken(dve, ("proj", t))

            def logits(g):
                ps = full(dve, ("lg", g))[0:T, 0:GTILES * E].rearrange("p (t e) -> p t e", e=E)
                freed(CP(LG[:, GTILES * g:GTILES * (g + 1), :], ps), ("lg", g))
                taken(dve, ("lg", g))
                for t in group_tiles(g):
                    ch.then(dve.max(TOP[:, t, :], LG[:, t, :]))
                ch.settle()
                for t in group_tiles(g):
                    ch.then(dve.max_index(TIX[:, t, :], TOP[:, t, :], LG[:, t, :]))
                ch.settle()

            for step in STEPS:
                kind, x = step[0], step[-1]
                if kind == "tok":
                    tok(x)
                elif kind == "stats":
                    stats(step[1], x)
                elif kind == "apply":
                    apply(step[1], x)
                elif kind == "wkv":
                    wkv(step[1], step[2])
                elif kind == "wo":
                    wo(x)
                elif kind == "resid":
                    resid(step[1], x)
                elif kind == "rv":
                    rv(x)
                elif kind == "ff":
                    ff(x)
                elif kind == "spread":
                    spread(x)
                elif kind == "s":
                    score(x)
                elif kind == "v":
                    values(x)
                elif kind == "pt":
                    sums(x)
                elif kind == "pv":
                    weighted(x)
                elif kind == "proj":
                    proj(x)
                elif kind == "logits":
                    logits(x)

            def te(x):
                return x.rearrange("p (t e) -> p t e", e=E)

            iota = const_("iota", T)
            ch.step(TTR(DD[:, 0:TILES], TOP[:, :, 1], TOP[:, :, 0], ALU.subtract))
            dve.sem_inc(top_ready, 1)
            ixf = IXF.rearrange("p (c t) -> p c t", c=2)
            ch.step(CP(ixf, TIX[:, :, 0:2].rearrange("p t c -> p c t")))
            m1, m2, m12, gf, sf, tmp = (te(x[:, :]) for x in (M1, M2, M12, GF, SF, TMP))
            i8 = bc(iota[:, 0:E].unsqueeze(1), [T, TILES, E])
            ch.then(TTR(m1, i8, bc(ixf[:, 0, :].unsqueeze(2), [T, TILES, E]), ALU.is_equal))
            ch.step(TTR(m2, i8, bc(ixf[:, 1, :].unsqueeze(2), [T, TILES, E]), ALU.is_equal))
            ch.step(TTR(m12, m1, m2, ALU.add))
            dve.sem_inc(mask_ready, 1)
            dve.wait_ge(e2_ready, 1)
            g12 = GG.rearrange("p (c t) -> p c t", c=2)
            ch.step(TS(DD[:, TILES:NC2], DD[:, 0:TILES], 1.0, None, ALU.add))
            ch.step(dve.reciprocal(g12[:, 0, :], DD[:, TILES:NC2]))
            ch.step(TTR(g12[:, 1, :], g12[:, 0, :], DD[:, 0:TILES], ALU.mult))
            ch.then(TTR(gf, m1, bc(g12[:, 0, :].unsqueeze(2), [T, TILES, E]), ALU.mult))
            ch.step(TTR(tmp, m2, bc(g12[:, 1, :].unsqueeze(2), [T, TILES, E]), ALU.mult))
            ch.step(TTR(gf, gf, tmp, ALU.add))
            dve.sem_inc(gf_ready, 1)
            ps = full(dve, ("rank",))
            et = lambda x: x.rearrange("p (e t) -> p e t", e=E)
            ch.step(CP(et(TOTC[:, :]), ps[0:T, T:2 * T].rearrange("p (t e) -> p e t", e=E)))
            ch.step(dve.tensor_tensor_scan(CUM[:, :], const_("keep", T), TOTC[:, :], 0.0, ALU.mult, ALU.add))
            ch.then(CP(NE8[:, 0:E], et(CUM[:, :])[:, :, TILES - 1]))
            ch.step(TTR(TOTC[:, :], CUM[:, :], TOTC[:, :], ALU.subtract))
            slot = const_("slot", T)
            n9 = TOK // 128
            ch.step(TTR(CMP[:, :, 0:n9], bc(NE8[:, 0:E].unsqueeze(2), [T, E, n9]), bc(slot[:, 0:n9].unsqueeze(1), [T, E, n9]), ALU.is_gt))
            ch.step(RED(TE8[:, 0:E], CMP[:, :, 0:n9], AX.X, ALU.add))
            ch.step(dve.tensor_tensor_scan(END[:, 0:E], const_("ones", T)[:, 0:E], TE8[:, 0:E], 0.0, ALU.mult, ALU.add))
            ch.step(TTR(BASE[:, 0:E], END[:, 0:E], TE8[:, 0:E], ALU.subtract))
            ch.step(TS(BASE[:, 0:E], BASE[:, 0:E], 128.0, None, ALU.mult))
            freed(TTR(sf, ps[0:T, 0:T].rearrange("p (t e) -> p t e", e=E), et(TOTC[:, :]).rearrange("p e t -> p t e"), ALU.add), ("rank",))
            taken(dve, ("rank",))
            ch.step(TTR(sf, sf, bc(BASE[:, 0:E].unsqueeze(1), [T, TILES, E]), ALU.add))
            for c, m in enumerate((m1, m2)):
                ch.step(TTR(tmp, m, sf, ALU.mult))
                ch.step(RED(SL[:, TILES * c:TILES * (c + 1)], tmp, AX.X, ALU.add))
            ch.step(TTR(GE, bc(SL.unsqueeze(2), [T, NC2, MT + 1]), bc(slot[:, 0:MT + 1].unsqueeze(1), [T, NC2, MT + 1]), ALU.is_ge))
            dve.sem_inc(ge_ready, 1)
            ch.step(RED(AQ, GE[:, :, 1:MT + 1], AX.X, ALU.add))
            ch.step(STT(BB, AQ, -128.0, SL, ALU.mult, ALU.add))
            dve.sem_inc(bb_ready, 1)
            for i in range(NDVE):
                if i == 2:
                    dve.wait_ge(aa_ready, 1)
                    for c in range(2):
                        sl = slice(TILES * c, TILES * (c + 1))
                        ch.then(TTR(RT[:, sl, MT:2 * MT], AA[:, sl, :], bc(g12[:, c, :].unsqueeze(2), [T, TILES, MT]), ALU.mult))
                    ch.settle()
                    dve.sem_inc(rt_ready, 1)
                TS(ONEB[:, i, :], iota, BB[:, i:i + 1], None, ALU.is_equal).then_inc(table_ready, 1)
            ch.step(TTR(EJC[:, :, :], bc(iota[:, 0:MT].unsqueeze(2), [T, MT, E]), bc(END[:, 0:E].unsqueeze(1), [T, MT, E]), ALU.is_ge))
            ch.step(RED(EJ[:, :], EJC[:, :, :], AX.X, ALU.add))
            ch.then(TS(EJI[0:T, :], EJ[:, :], float(E - 1), None, ALU.min))
            ch.step(CP(USED[0:T, :], END[:, E - 1:E]))
            ch.then(dve.memset(O[:, 0, :], 0.0))
            for j in range(2):
                ch.then(dve.memset(XT[j][C1:C1 + 1, 1, :], 1.0))
            ps = full(dve, ("list",))
            freed(CP(LST[:, :], ps[:, 0:2 * MT]), ("list",))
            taken(dve, ("list",))
            ch.then(TS(LT2[:, 0, :], LST[:, 0:MT], -1.0, 0.0, ALU.add, ALU.max))
            ch.then(TS(LT2[:, 1, :], LST[:, 0:MT], 0.0, const_("spare"), ALU.is_equal, ALU.mult))
            ch.settle()
            ch.then(CP(IG[:, :], LT2[:, 0, :]))
            ch.then(STT(IS[:, :], LST[:, 0:MT], -1.0, LT2[:, 1, :], ALU.add, ALU.add))
            ch.settle()
            dve.sem_inc(index_ready, 1)

            dve.wait_ge(base_ready, G)
            for t in range(0, TILES, 2):
                ps = full(dve, ("b2", t))[0:T, 0:2 * C].rearrange("p (t c) -> p t c", t=2)
                freed(TTR(H[:, t:t + 2, :], ps, H[:, t:t + 2, :], ALU.add), ("b2", t))

            def weights(j):
                if j >= 2:
                    full(dve, ("h", j - 2, 1))
                e = dve.value_load(EJI[0:1, j:j + 1], min_val=0, max_val=E - 1)
                we = WE[j % 2]
                ch.then(CP(we[:, 0:1, :], W1A[:, bass.ds(e, 1), :]))
                ch.step(CP(we[0:C1 + 1, 1:2, :], W1B[0:C1 + 1, bass.ds(e, 1), :]))
                dve.sem_inc(we_ready, 1)

            full(dve, ("rv", TILES - 1))
            dve.wait_ge(loaded["w1a"], 16)
            dve.wait_ge(loaded["w1b"], 16)
            weights(0)
            weights(1)

            def gated(j):
                if j + 2 < MT:
                    weights(j + 2)
                if j >= 2:
                    dve.wait_ge(scattered, 16 * (j - 1))
                ps = full(dve, ("y", j))
                freed(TS(YG[j % 2], ps[:, 0:C], LST[:, MT + j:MT + j + 1], None, ALU.mult), ("y", j))

            for j in range(FULL):
                gated(j)
            n_used = used(dve)

            def rest(a):
                if a < MT:
                    with dve.If(n_used > a):
                        for j in pair(a):
                            gated(j)
                        rest(a + 2)

            rest(FULL)

        @block.tensor
        def _(pe):
            ident = const_("ident")
            mm = pe.matmul

            def begin(job):
                b, n = PLACE[job]
                if n:
                    pe.wait_ge(bank_free[b], n)
                return banks[:, b, :]

            def end(ins, job):
                ins.then_inc(bank_full[PLACE[job][0]], 1)

            for n in ("tokw", "const"):
                pe.wait_ge(loaded[n], 16)
            tw = TOKW.rearrange("p (k c) -> p k c", k=KP)

            def over_channels(dst, wt, act_, cols, base=0, moving=None):
                mm(dst, act_[0], wt[0], start=True, stop=False)
                return mm(dst, act_[1], wt[1], start=False, stop=True)

            def w_(wt, lo, hi, base=0):
                return wt[:, 0, lo:hi], wt[base:base + C1, 1, lo:hi]

            def h_(g, lo, hi, ht=HT):
                return ht[:, g % 2, 0, lo:hi], ht[0:C1, g % 2, 1, lo:hi]

            seen = set()

            def need(*ns):
                for n in ns:
                    if n not in seen:
                        pe.wait_ge(loaded[n], 16)
                        seen.add(n)

            nqk = [0]
            for step in STEPS:
                kind, g = step[0], step[-1]
                if kind == "tok":
                    gg, i = divmod(g, GTILES)
                    pe.wait_ge(patch_loaded[gg], 16)
                    ps = begin(("tok", g))
                    for k in range(KP):
                        ins = mm(ps[0:T, 0:C], XP[:, gg, k, T * i:T * (i + 1)], tw[:, k, :], start=(k == 0), stop=(k == KP - 1))
                    end(ins, ("tok", g))
                elif kind == "turn":
                    pe.wait_ge(xh_ready, APPLIED.index(step[1:]) + 1)
                    for b in range(2):
                        job = ("turn", step[1], g, b)
                        ps = begin(job)
                        rows = 128 if b == 0 else C1
                        for i in range(GTILES):
                            ins = pe.transpose(ps[0:rows, T * i:T * (i + 1)], XH[:, GTILES * (g % 2) + i, 128 * b:128 * b + rows], ident[0:T, 0:T])
                        end(ins, job)
                elif kind == "kvr":
                    need("kvrw")
                    turned_(pe, "a", g)
                    for w in step[1:2]:
                        for b in range(2):
                            ps = begin(("kvr", g, w, b))
                            lo, n = C * w + 128 * b, 128 if b == 0 else C1
                            base = 0 if b == 0 else C1 * (g % 2)
                            end(over_channels(ps[base:base + n, 0:GT], h_(g, 0, GT), w_(KVRW, lo, lo + n), None), ("kvr", g, w, b))
                elif kind == "wo":
                    need("wow")
                    c, half = divmod(g, 2)
                    pe.wait_ge(z_ready, c + 1)
                    base = C1 * half
                    for i, t in enumerate(group_tiles(g)):
                        ps = begin(("wo", t))
                        z0 = Z[c][:, GT * half + T * i:GT * half + T * (i + 1)]
                        z1 = Z[c][base:base + C1, CI * NT + T * i:CI * NT + T * (i + 1)]
                        end(over_channels(ps[0:T, 0:C], w_(WOW, 0, C, base), (z0, z1), None), ("wo", t))
                elif kind == "kf":
                    need("kfw", "rfw", "vfw")
                    turned_(pe, "2", g)
                    for m in kf_blocks(step[1]):
                        ps = begin(("kf", g, m))
                        end(over_channels(ps[:, 0:GT], h_(g, 0, GT), w_(KFW, 128 * m, 128 * (m + 1)), None), ("kf", g, m))
                elif kind == "rv":
                    t = step[1]
                    gg, i = divmod(t, GTILES)
                    nth = ffs(STEPS, gg)[1] if ffs(STEPS, gg) else 0
                    ps = begin(("rv", t))
                    over_channels(ps[0:T, 0:C], w_(RFW, 0, C), h_(gg, T * i, T * (i + 1)), None)
                    if i == 0:
                        pe.wait_ge(kf_ready, HB * (nth + 1))
                    for m in range(HB):
                        ins = mm(ps[0:T, C:2 * C], KF[:, m, T * i:T * (i + 1)], VFW[:, m, :], start=(m == 0), stop=(m == HB - 1))
                    end(ins, ("rv", t))
                elif kind == "qk":
                    need("qkvw")
                    turned_(pe, "b", g)
                    for w, n in enumerate("qk"):
                        for b in range(2):
                            ps = begin((n, g, b))
                            rows = 128 if b == 0 else C1
                            lo = C * w + 128 * b
                            end(over_channels(ps[0:rows, 0:GT], h_(g, 0, GT, HTB), w_(QKVW, lo, lo + rows), None), (n, g, b))
                elif kind == "s":
                    p = g
                    gg, q = divmod(p, GI // 2)
                    pe.wait_ge(ke_ready, gg + 1)
                    for b in range(2):
                        taken(pe, ("q", gg, b))
                    ps = begin(("s", p))
                    ke0 = KE[gg % 2][:, 0:GI * 8 * NT].rearrange("p (i n) -> p i n", i=GI)
                    ke1 = KE[gg % 2][0:C1, GI * 8 * NT:].rearrange("p (i n) -> p i n", i=GI)
                    for a in range(2):
                        i = 2 * q + a
                        mm(ps[64 * a:64 * a + 64, 0:8 * NT], QT[:, gg % 2, 0, NT * i:NT * i + 64], ke0[:, i, :], start=True, stop=True)
                    for a in range(2):
                        i = 2 * q + a
                        ins = mm(ps[64 * a:64 * a + 64, 8 * NT:NH * NT], QT[0:C1, gg % 2, 1, NT * i:NT * i + 64], ke1[:, i, :], start=True, stop=True)
                    end(ins, ("s", p))
                elif kind == "v":
                    p = g
                    ps = begin(("v", p))
                    pe.wait_ge(hr_ready, 2 * (p + 1))
                    for a in range(2):
                        h01 = (HR[:, p % 2, 0, 108 * a:108 * (a + 1)], HR[0:C1, p % 2, 1, 108 * a:108 * (a + 1)])
                        ins = over_channels(ps[0:108, C * a:C * (a + 1)], w_(QKVW, 2 * C, 3 * C), h01, None)
                    end(ins, ("v", p))
                elif kind == "pt":
                    p = g
                    pe.wait_ge(p_ready, p + 1)
                    ps = begin(("pt", p))
                    for s in range(NS):
                        ins = pe.transpose(ps[0:108, 128 * s:128 * (s + 1)], S[:, p % 2, 108 * s:108 * (s + 1)], ident)
                    end(ins, ("pt", p))
                elif kind == "pv":
                    p = g
                    ps = begin(("pv", p))
                    taken(pe, ("pt", p))
                    taken(pe, ("v", p))
                    ve = VE[:, p % 2, :].rearrange("p (a c) -> p a c", a=2)
                    po = ps[:, 0:2 * C].rearrange("p (a c) -> p a c", a=2)
                    for s in range(NS):
                        ins = mm(po[:, :, 48 * s:48 * (s + 1)], PT[:, p % 2, 128 * s:128 * (s + 1)],
                                 ve[:, :, 48 * s:48 * (s + 1)], start=True, stop=True)
                    end(ins, ("pv", p))
                elif kind == "ot":
                    p = g
                    taken(pe, ("pv", p))
                    ps = begin(("ot", p))
                    pe.transpose(ps[:, 0:128], O[:, p % 2, 0:128], ident)
                    end(pe.transpose(ps[0:C1, 128:256], O[:, p % 2, 128:C], ident), ("ot", p))
                elif kind == "proj":
                    need("projw")
                    for p in range(GI // 2 * g, GI // 2 * (g + 1)):
                        taken(pe, ("ot", p))
                    for i, t in enumerate(group_tiles(g)):
                        ps = begin(("proj", t))
                        o0 = OT[:, g % 2, 0, T * i:T * (i + 1)]
                        o1 = OT[0:C1, g % 2, 1, T * i:T * (i + 1)]
                        end(over_channels(ps[0:T, 0:C], w_(PROJW, 0, C), (o0, o1), None), ("proj", t))
                elif kind == "logits":
                    need("gatew")
                    turned_(pe, "g", g)
                    ps = begin(("lg", g))
                    for i in range(GTILES):
                        ins = over_channels(ps[0:T, E * i:E * (i + 1)], w_(GATEW, 0, E), h_(g, T * i, T * (i + 1)), None)
                    end(ins, ("lg", g))

            pe.wait_ge(mask_ready, 1)
            ps = begin(("rank",))
            mm(ps[0:T, 0:T], const_("before", T), M12[:, :], start=True, stop=True)
            end(mm(ps[0:T, T:2 * T], const_("ones", T), M12[:, :], start=True, stop=True), ("rank",))
            pe.wait_ge(gf_ready, 1)
            ps = begin(("gturn",))
            end(pe.transpose(ps[0:T, 0:T], GF[:, :], ident[0:T, 0:T]), ("gturn",))
            need("b2")
            for t in range(0, TILES, 2):
                pe.wait_ge(gm_ready, t + 2)
                ps = begin(("b2", t))
                mm(ps[0:T, 0:C], GM[:, t, :], B2[:, :], start=True, stop=True)
                end(mm(ps[0:T, C:2 * C], GM[:, t + 1, :], B2[:, :], start=True, stop=True), ("b2", t))

            ps = begin(("list",))
            pe.wait_ge(rt_ready, 3)
            for i in range(NC2):
                if i < NDVE:
                    pe.wait_ge(table_ready, i + 1)
                else:
                    pe.wait_ge(table2_ready, i - NDVE + 1)
                ins = mm(ps[:, 0:2 * MT], ONEB[:, i, :], RT[:, i, :], start=(i == 0), stop=(i == NC2 - 1))
            end(ins, ("list",))

            need("w1a", "w1b", "w2")

            def tile_expert(j):
                return pe.value_load(EJI[0:1, j:j + 1], min_val=0, max_val=E - 1)

            def turn_tokens(j):
                pe.wait_ge(gathered[j % 3], 16 * (j // 3 + 1))
                ps = begin(("xt", j))
                pe.transpose(ps[:, 0:128], XG[j % 3][:, 0:128], ident)
                end(pe.transpose(ps[0:C1, 128:256], XG[j % 3][:, 128:C], ident), ("xt", j))

            def up(j):
                if j < FULL:
                    expert[j] = tile_expert(j)
                taken(pe, ("xt", j))
                if j == 0:
                    pe.wait_ge(index_ready, 1)
                pe.wait_ge(we_ready, j + 1)
                for i in range(2):
                    ps = begin(("h", j, i))
                    for k in range(3):
                        at_ = 384 * i + 128 * k
                        h = ps[:, 128 * k:128 * (k + 1)]
                        mm(h, WE[j % 2][:, 0, at_:at_ + 128], XT[j % 2][:, 0, :], start=True, stop=False)
                        ins = mm(h, WE[j % 2][0:C1 + 1, 1, at_:at_ + 128], XT[j % 2][0:C1 + 1, 1, :], start=False, stop=True)
                    end(ins, ("h", j, i))

            def down(j):
                e = expert[j] if j < FULL else tile_expert(j)
                ps = begin(("y", j))
                for k in range(HB):
                    if k % 3 == 0:
                        taken(pe, ("h", j, k // 3))
                    ins = mm(ps[:, 0:C], HST[j % 2][:, 128 * k:128 * (k + 1)], W2[:, bass.ds(e, 1), C * k:C * (k + 1)],
                             start=(k == 0), stop=(k == HB - 1))
                end(ins, ("y", j))

            expert = {}
            turn_tokens(0)
            turn_tokens(1)
            up(0)
            n_used = used(pe)

            def ahead(j):
                if j + 1 < MT:
                    up(j + 1)
                if j + 2 < MT:
                    turn_tokens(j + 2)

            for j in range(FULL - 1):
                ahead(j)
                down(j)

            def rest(a):
                if a >= MT:
                    down(MT - 1)
                    return
                with pe.If(n_used > a):
                    ahead(a - 1)
                down(a - 1)
                with pe.If(n_used > a):
                    if a + 1 < MT:
                        ahead(a)
                        down(a)
                    rest(a + 2)

            rest(FULL)


EXPS = ("e1f", "e2f", "e1b", "e2b", "p")


def ffs(steps, g):
    order = [s[-1] for s in steps if s[0] == "ff"]
    n = order.index(g)
    return (order[n - 1], n) if n else None


def projs(steps, g):
    return [s[-1] for s in steps if s[0] == "resid" and s[1] == "b"].index(g) + 1


def ht_readers(steps, step):
    n, kind, g = steps.index(step), step[1], step[2]
    if kind == "b" and g >= 2:
        return [("v", (g - 1) * GI // 2 - 1)]
    for s in reversed(steps[:n]):
        if kind == "b":
            if s[0] == "kvr":
                return [jobs_of(s)[-1]]
        elif s[0] in ("kvr", "rv", "logits"):
            group = s[1] // GTILES if s[0] == "rv" else s[-1]
            if group % 2 == g % 2:
                return [jobs_of(s)[-1]]
    return []


def kernel(**inputs):
    import numpy as np
    import concourse.bacc as bacc
    from concourse.bass_utils import run_bass_kernel_spmd

    a = {k: np.asarray(v) for k, v in inputs.items()}

    def blocks(w):
        return np.stack([w[0:128], np.concatenate([w[128:192], w[128:192]])], 1)

    def rows(v, n):
        return np.broadcast_to(v, (n, len(v)))

    qb = a["L0_ffn_qkv_b"]
    vectors = {"ln1_w": a["L0_attn_ln1_w"], "ln1_b": a["L0_attn_ln1_b"], "ln2_w": a["L0_attn_ln2_w"], "ln2_b": a["L0_attn_ln2_b"],
               "n1_w": a["L0_ffn_norm1_w"], "n1_b": a["L0_ffn_norm1_b"], "n2_w": a["L0_ffn_norm2_w"], "n2_b": a["L0_ffn_norm2_b"],
               "decay": a["L0_attn_decay"], "first": a["L0_attn_first"], "q_b": qb[0:C], "k_b": qb[C:2 * C], "v_b": qb[2 * C:]}
    chan = np.concatenate([blocks(vectors[n][:, None])[:, :, 0] for n in CHAN], 1)

    p = np.arange(128)[:, None]
    parts = {
        "ident": np.eye(128), "iota": np.arange(128) + 0 * p, "before": p < np.arange(T), "ones": np.ones((128, T)),
        "head0": p // HD == np.arange(8), "head1": p // HD == np.arange(4),
        "slab": p // NT == (np.arange(C) // HD) % HS, "slot": 128 * np.arange(MT + 1) + 0 * p,
        "token": T * np.arange(TILES) + p + 1, "spare": TOK + 1 + p, "keep": (np.arange(E * TILES) % TILES > 0) + 0 * p,
        "tile": p // E == np.arange(TILES), "power": np.full((128, 6), -0.5)}
    const = np.concatenate([parts[n].astype(np.float32) for n, _ in CONST], 1)

    x = a["x"].reshape(G, GI, 3, 6, 16, 6, 16)
    xp = x.transpose(2, 4, 6, 0, 1, 3, 5).reshape(KP, 128, G, GT).transpose(1, 2, 0, 3)
    w1 = a["L0_ffn_W1"].transpose(1, 0, 2)
    arrays = {
        "xp": xp, "chan": chan, "const": const,
        "tokw": a["L0_tok_W"].T.reshape(KP, 128, C).transpose(1, 0, 2).reshape(128, KP * C), "tokb": rows(a["L0_tok_b"], T),
        "kvrw": blocks(np.concatenate([a["L0_attn_Wk_a"].T, a["L0_attn_Wv_a"].T, a["L0_attn_Wr_a"].T], 1)),
        "wow": blocks(a["L0_attn_Wo_a"].T), "kfw": blocks(a["L0_attn_Wk_f"].T), "rfw": blocks(a["L0_attn_Wr_f"].T),
        "vfw": a["L0_attn_Wv_f"].T.reshape(HB, 128, C).transpose(1, 0, 2),
        "qkvw": blocks(a["L0_ffn_qkv_w"].T), "projw": blocks(a["L0_ffn_proj_w"].T), "projb": rows(a["L0_ffn_proj_b"], T),
        "gatew": blocks(a["L0_ffn_w_gate"]), "w1a": w1[0:128], "w1b": np.concatenate([w1[128:192], a["L0_ffn_b1"][None]]),
        "w2": a["L0_ffn_W2"].reshape(E, HB, 128, C).transpose(2, 0, 1, 3).reshape(128, E, HB * C),
        "b2": np.tile(a["L0_ffn_b2"], (TILES, 1)),
    }
    nc = bacc.Bacc("TRN2", target_bir_lowering=False, num_devices=1)
    data, args = {}, {}
    for name, v in arrays.items():
        data["in_" + name] = np.ascontiguousarray(v)
        args[name] = nc.dram_tensor("in_" + name, v.shape, F32, kind="ExternalInput").ap()
    args["out"] = nc.dram_tensor("out_0", (TOK + 128, C), F32, kind="ExternalOutput").ap()
    build(nc, **args)
    r = run_bass_kernel_spmd(nc, [data], core_ids=[0])
    return r.results[0]["out_0"][0:TOK].reshape(B, NT, C)
```

```python
from contextlib import ExitStack

import concourse.bass as bass
from concourse import mybir

F32 = mybir.dt.float32
I32 = mybir.dt.int32
U32 = mybir.dt.uint32
ALU = mybir.AluOpType
ACT = mybir.ActivationFunctionType
AX = mybir.AxisListType

B, NT, C = 32, 36, 192
TOK = B * NT
PD = 768
KP = PD // 128
G = 4
GI = B // G
GT = GI * NT
T = 96
GTILES = GT // T
TILES = TOK // T
C1 = C - 128
HID = 768
HB = HID // 128
NH, HD = 12, 16
HS = 3
NS = NH // HS
E = 8
MT = (2 * TOK + E * 127) // 128
FULL = 2 * TOK // 128
EPS = 1e-5
FAR = -1e38

CI = 16
IC = CI + CI // 2
PITCH = NT + 1
WL = IC * PITCH + 1
WS = WL + 1
WN = IC * NT

CONST = [("ident", 128), ("iota", 128), ("before", T), ("ones", T), ("head0", 8), ("head1", 4),
         ("slab", C), ("slot", MT + 1), ("token", TILES), ("spare", 1), ("keep", E * TILES),
         ("tile", TILES), ("power", 6)]
CHAN = ["ln1_w", "ln1_b", "ln2_w", "ln2_b", "n1_w", "n1_b", "n2_w", "n2_b", "decay", "first",
        "q_b", "k_b", "v_b"]


def offsets(parts):
    at, out = 0, {}
    for name, n in parts:
        out[name] = (at, n)
        at += n
    return out, at


CAT, CN = offsets(CONST)
VAT = {name: 2 * i for i, name in enumerate(CHAN)}


ORDER = """
tok:0 tok:1 tok:2 stats:a:0 apply:a:0 tok:3 tok:4 tok:5 tok:6 tok:7 turn:a:0 stats:a:1 tok:8 stats:a:2
kvr:0:0 kvr:2:0 apply:a:1 turn:a:1 kvr:0:1 apply:a:2 resid:a:0 resid:a:2 wkv:0:0 tok:9 wkv:0:1 wexp:0:0
tok:10 wexp:0:1 tok:11 kvr:1:0 kvr:1:1 stats:a:3 wkv:0:2 kvr:2:1 wexp:0:2 resid:a:1 wkv:0:3 apply:a:3
wexp:0:3 evb:0 wexp:0:4 wkv:0:4 wkv:0:5 turn:a:2 resid:a:3 turn:a:3 kvr:2:2 kvr:0:2 kvr:0:3 kvr:1:3 kvr:1:2
kvr:2:3 den:0 wkv:0:6 wkv:1:0 wo:0 stats:2:0 wkv:1:1 apply:2:0 wexp:1:0 turn:2:0 wexp:1:1 wkv:1:2 wexp:1:2
wo:1 wexp:1:3 wexp:1:4 stats:2:1 evb:1 kf:0:0 hx:0 kf:1:0 apply:2:1 wkv:1:3 rv:0 rv:1 turn:2:1 rv:2 wkv:1:4
ff:0 kf:0:1 kf:1:1 den:1 hx:1 wkv:1:5 stats:b:0 apply:b:0 rv:3 rv:4 rv:5 ff:1 wkv:1:6 turn:b:0 qk:0 vt:0
vl:0:0 stats:b:1 spread:0 apply:b:1 wo:2 wo:3 turn:b:1 s:0 s:1 vt:1 exp:0 resid:b:0 pt:0 stats:2:2 vl:1:0
apply:2:2 qk:1 exp:1 stats:2:3 turn:2:2 v:0 v:1 v:2 resid:b:1 apply:2:3 s:2 v:3 spread:1 hx:2 kf:0:2 kf:1:2
pt:1 s:3 rv:6 exp:2 exp:3 pv:0 pv:1 hx:3 vl:0:1 rv:7 turn:2:3 ot:0 pt:2 pt:3 rv:8 pv:2 s:4 ot:1 pv:3 ot:2
vl:1:1 kf:0:3 ot:3 kf:1:3 proj:0 v:4 v:5 stats:g:0 ff:2 exp:4 rv:9 apply:g:0 rv:10 stats:b:2 s:5 v:6
turn:g:0 apply:b:2 base:0 rv:11 pt:4 logits:0 pv:4 exp:5 s:6 pt:5 ot:4 resid:b:2 v:7 s:7 pv:5 ff:3 turn:b:2
stats:b:3 qk:2 exp:6 vt:2 spread:2 ot:5 vl:0:2 exp:7 pt:6 pv:6 pt:7 s:8 exp:8 pv:7 ot:6 apply:b:3 v:8 v:9
vl:1:2 v:10 ot:7 proj:1 stats:g:1 turn:b:3 s:9 v:11 qk:3 apply:g:1 pt:8 resid:b:3 vt:3 s:10 exp:9 exp:10
pv:8 pt:9 s:11 ot:8 pt:10 turn:g:1 exp:11 pv:9 vl:0:3 pv:10 ot:9 pt:11 ot:10 logits:1 pv:11 base:1 spread:3
ot:11 vl:1:3 v:12 proj:2 v:13 s:12 s:13 stats:g:2 exp:12 pt:12 v:14 exp:13 apply:g:2 pt:13 pv:12 s:14
turn:g:2 pv:13 ot:12 v:15 exp:14 logits:2 s:15 pt:14 exp:15 ot:13 pt:15 pv:14 pv:15 ot:14 ot:15 proj:3
base:2 stats:g:3 base:3 apply:g:3 turn:g:3 logits:3
"""


def schedule():
    return [tuple(int(x) if x.isdigit() and not (i == 1 and s[:5] in ("stats", "apply", "resid") or s[:4] == "turn" and i == 1) else x
                  for i, x in enumerate(s.split(":"))) for s in ORDER.split()]


WKV_PARTS = 7


def kf_blocks(half):
    return range(HB // 2 * half, HB // 2 * (half + 1))


def jobs_of(step):
    kind, x = step[0], step[-1]
    tiles = range(GTILES * x, GTILES * (x + 1))
    if kind in ("tok", "rv"):
        return [(kind, x)]
    if kind == "turn":
        return [("turn", step[1], x, b) for b in range(2)]
    if kind == "kvr":
        return [("kvr", x, step[1], b) for b in range(2)]
    if kind == "wo":
        return [("wo", t) for t in tiles]
    if kind == "kf":
        return [("kf", x, m) for m in kf_blocks(step[1])]
    if kind == "qk":
        return [("q", x), ("k", x), ("qk1", x)]
    if kind == "vt":
        return [("vt", t) for t in tiles]
    if kind in ("s", "pt", "pv", "ot"):
        return [(kind, x)]
    if kind == "proj":
        return [("proj", t) for t in tiles]
    if kind == "logits":
        return [("lg", x)]
    return []


def moe_jobs():
    out = [("rank",), ("gturn",)] + [("b2", t) for t in range(0, TILES, 2)] + [("list",)]
    out += [("xt", 0), ("xt", 1), ("h", 0, 0), ("h", 0, 1)]
    for j in range(MT):
        if j + 1 < MT:
            out += [("h", j + 1, 0), ("h", j + 1, 1)]
        if j + 2 < MT:
            out.append(("xt", j + 2))
        out.append(("y", j))
    return out


def build(nc, xp, chan, const, tokw, tokb, kvrw, wow, kfw, rfw, vfw, qkvw, projw, projb, gatew,
          w1a, w1b, w2, b2, out):
    STEPS = schedule()
    JOBS = [j for s in STEPS for j in jobs_of(s)] + moe_jobs()
    NBANK = 8
    PLACE = {j: (n % NBANK, n // NBANK) for n, j in enumerate(JOBS)}
    LNS = [s[1:] for s in STEPS if s[0] == "stats"]
    APPLIED = [s[1:] for s in STEPS if s[0] == "apply"]
    TURNED = [s[1:] for s in STEPS if s[0] == "turn"]
    assert LNS and len(set(JOBS)) == len(JOBS)

    ctx = ExitStack()
    with ctx:
        def sb(name, shape, dt=F32):
            return ctx.enter_context(nc.sbuf_tensor(name, shape, dt))

        def sem(name):
            return ctx.enter_context(nc.semaphore(name))

        ARENA = 2 * E * HID + E * HB * C
        arena = sb("arena", [128, ARENA])
        at = [0]

        def carve(n):
            at[0] += n
            assert at[0] <= ARENA
            return arena[:, at[0] - n:at[0]]

        K, KU, V, ER = ([carve(WS) for _ in range(2)] for _ in range(4))
        W, MF, MB, E1F, E1B, E2F, E2B, EVF, EVB = (carve(WS) for _ in range(9))
        P3 = carve(3 * WN)
        Z = [carve(WN) for _ in range(2)]
        TOKW = carve(KP * C)
        W1A = arena[:, 0:E * HID].rearrange("p (e n) -> p e n", e=E)
        W1B = arena[:, E * HID:2 * E * HID].rearrange("p (e n) -> p e n", e=E)
        W2 = arena[:, 2 * E * HID:ARENA].rearrange("p (e n) -> p e n", e=E)
        patch = sb("patch", [128, G * KP * GT])
        XP = patch[:, :].rearrange("p (n k t) -> p n k t", n=TILES, k=KP)
        KE = [patch[:, i * GI * NH * NT:(i + 1) * GI * NH * NT] for i in range(2)]
        ffn = sb("ffn", [128, HB * GT + GTILES * C + 2 * HID])
        KF = ffn[:, 0:HB * GT].rearrange("p (m t) -> p m t", m=HB)
        TH = ffn[:, HB * GT:HB * GT + GTILES * C].rearrange("p (t c) -> p t c", t=GTILES)
        KFW = ffn[:, HB * GT + GTILES * C:].rearrange("p (b n) -> p b n", b=2)
        KVRW = sb("kvrw", [128, 2, 3 * C])
        WOW = sb("wow", [128, 2, C])
        rvw = sb("rvw", [128, 2 * HID])
        RFW = rvw[:, 0:2 * C].rearrange("p (b n) -> p b n", b=2)
        VFW = rvw[:, 2 * C:2 * C + HB * C].rearrange("p (m n) -> p m n", m=HB)
        QKVW = sb("qkvw", [128, 2, 3 * C])
        PROJW = sb("projw", [128, 2, C])
        HTB = KVRW[:, :, :].rearrange("p b n -> p (b n)").rearrange("p (r b t) -> p r b t", r=2, b=2)
        GATEW = sb("gatew", [128, 2, E])
        CH = sb("chans", [128, 2 * len(CHAN)])
        WU = sb("wu", [128, 4])
        CO = sb("consts", [128, CN])
        TOKB = sb("tokb_s", [T, C])
        PROJB = sb("projb_s", [T, C])
        B2 = sb("b2_s", [T, C])
        H = sb("h", [T, TILES, C])
        X = sb("x", [T, TILES, C])
        XH = sb("xh", [T, 2 * GTILES, C])
        HT = sb("ht", [128, 2, 2, GT])
        ST = sb("st", [T, TILES, 6])
        MV = sb("mv", [T, TILES, 2])
        VA = sb("va", [T, G, 2, GTILES])
        RS = sb("rs", [T, G, 2, GTILES])
        QT = sb("qt", [128, 2, 2, GT + 32])
        KT = sb("kt", [128, 2, GT])
        VT = sb("vt", [T, GTILES, C])
        vs_ = sb("vs", [128, GI * C])
        VS = vs_[0:HS * NT, :].rearrange("p (i c) -> p i c", i=GI)
        S = sb("s", [128, 2, NH * NT])
        MX = sb("mx", [128, 2, NH])
        SUM = sb("sum", [128, 2, NH])
        RI = sb("ri", [128, 2, NH])
        PT = sb("pt", [108, 2, 512])
        O = sb("o", [128, 2, C])
        OT = sb("ot", [128, 2, 2, GT])
        LG = sb("lg", [T, TILES, E])
        TOP = sb("top", [T, TILES, E])
        TIX = sb("tix", [T, TILES, E], U32)
        banks = ctx.enter_context(nc.psum_tensor("banks", [128, NBANK, 512], F32))

        names = ["chan", "const", "tokw", "tokb", "kvrw", "wow", "kfw", "rfw", "vfw", "qkvw", "projw",
                 "projb", "gatew", "b2", "w1a", "w1b", "w2"]
        loaded = {n: sem("loaded_" + n) for n in names}
        patch_loaded = [sem(f"patch_loaded{t}") for t in range(TILES)]
        bank_full = [sem(f"bank_full{b}") for b in range(NBANK)]
        bank_free = [sem(f"bank_free{b}") for b in range(NBANK)]
        cleared = sem("cleared")
        dve_step = sem("dve_step")
        act_step = sem("act_step")
        pool_step = sem("pool_step")
        wu_ready = sem("wu_ready")
        var_ready = sem("var_ready")
        rstd_ready = sem("rstd_ready")
        xh_ready = sem("xh_ready")
        diff_ready = sem("diff_ready")
        scan_ready = sem("scan_ready")
        diffb_ready = sem("diffb_ready")
        exp_ready = sem("exp_ready")
        evb_ready = sem("evb_ready")
        den_ready = sem("den_ready")
        z_ready = sem("z_ready")
        hx_ready = sem("hx_ready")
        kf_ready = sem("kf_ready")
        th_ready = sem("th_ready")
        h_ready = sem("h_ready")
        x_ready = [sem(f"x_ready{g}") for g in range(G)]
        xpb_ready = sem("xpb_ready")
        ke_ready = sem("ke_ready")
        v_stored = [sem(f"v_stored{g}") for g in range(G)]
        v_loaded = [sem(f"v_loaded{i}") for i in range(2 * G)]
        vs_ready = sem("vs_ready")
        p_ready = sem("p_ready")
        base_ready = sem("base_ready")
        xh_stored = [sem(f"xh_stored{g}") for g in range(G)]
        top_ready = sem("top_ready")
        e2_ready = sem("e2_ready")
        mask_ready = sem("mask_ready")
        gf_ready = sem("gf_ready")
        gm_ready = sem("gm_ready")
        ge_ready = sem("ge_ready")
        bb_ready = sem("bb_ready")
        aa_ready = sem("aa_ready")
        rt_ready = sem("rt_ready")
        table_ready = sem("table_ready")
        table2_ready = sem("table2_ready")
        index_ready = sem("index_ready")
        base_stored = sem("base_stored")
        gathered = [sem(f"gathered{i}") for i in range(3)]
        scattered = sem("scattered")
        all_added = sem("all_added")
        we_ready = sem("we_ready")

        def full(eng, job):
            b, n = PLACE[job]
            eng.wait_ge(bank_full[b], n + 1)
            return banks[:, b, :]

        def freed(ins, job):
            ins.then_inc(bank_free[PLACE[job][0]], 1)

        def taken(eng, job):
            b, n = PLACE[job]
            eng.wait_ge(bank_free[b], n + 1)

        def const_(name, rows=128):
            a, n = CAT[name]
            return CO[0:rows, a:a + n]

        def chan_(name, b, lo=0, hi=None):
            a = VAT[name] + b
            return CH[lo:(128 if b == 0 else C1) if hi is None else hi, a:a + 1]

        def turned_(eng, kind, g):
            for b in range(2):
                taken(eng, ("turn", kind, g, b))

        class Chain:

            def __init__(self, eng, s):
                self.eng, self.s, self.n = eng, s, 0

            def then(self, ins):
                self.n += 1
                ins.then_inc(self.s, 1)

            def settle(self):
                self.eng.wait_ge(self.s, self.n)

            def step(self, ins):
                self.then(ins)
                self.settle()

        def used(eng):
            return eng.value_load(USED[0:1, 0:1], min_val=FULL, max_val=MT)

        def pair(a):
            return range(a, min(a + 2, MT))

        def bc(ap, shape):
            return ap.to_broadcast(shape)

        def here(x):
            return x[:, 1:1 + IC * PITCH].rearrange("p (i t) -> p i t", t=PITCH)[:, :, 0:NT]

        def before(x):
            return x[:, 0:IC * PITCH].rearrange("p (i t) -> p i t", t=PITCH)[:, :, 0:NT]

        def behind(x):
            return x[:, 2:2 + IC * PITCH].rearrange("p (i t) -> p i t", t=PITCH)[:, :, 0:NT]

        def dense(x):
            return x.rearrange("p (i t) -> p i t", t=NT)

        def group_tiles(g):
            return range(GTILES * g, GTILES * (g + 1))

        rat = [0]

        def rcarve(n):
            rat[0] += n
            assert rat[0] <= G * KP * GT
            return patch[0:T, rat[0] - n:rat[0]]

        NC2 = 2 * TILES
        NDVE = NC2 - 6
        ONEB = rcarve(NC2 * 128).rearrange("p (i b) -> p i b", b=128)
        RT = rcarve(NC2 * 2 * MT).rearrange("p (i a) -> p i a", a=2 * MT)
        GE = rcarve(NC2 * (MT + 1)).rearrange("p (i a) -> p i a", a=MT + 1)
        AA = rcarve(NC2 * MT).rearrange("p (i a) -> p i a", a=MT)
        GM = rcarve(TILES * T).rearrange("p (t k) -> p t k", t=TILES)
        qat = {"q": 0, "k": 0}

        def qcarve(n, where="q"):
            whole = QT[:, :, :, :].rearrange("p a b t -> p (a b t)") if where == "q" else KT[:, :, :].rearrange("p b t -> p (b t)")
            qat[where] += n
            assert qat[where] <= whole.shape[1]
            return whole[:, qat[where] - n:qat[where]]

        M1, M2, M12, GF, TOTC, CUM, SF, TMP = (qcarve(TILES * E)[0:T] for _ in range(8))
        GFT = qcarve(T)[0:T]
        IXF, DD, GG, NE8, TE8, END, BASE, SL, AQ, BB = (qcarve(NC2)[0:T] for _ in range(10))
        CMP = qcarve(E * TILES)[0:T].rearrange("p (e t) -> p e t", e=E)
        EJC = qcarve(MT * E, "k")[0:T].rearrange("p (j e) -> p j e", e=E)
        EJ = qcarve(MT, "k")[0:T]
        assert MT <= 32 and 128 * 9 >= TOK

        fat = [0]

        def fcarve(n):
            fat[0] += n
            assert fat[0] <= ffn.shape[1]
            return ffn[:, fat[0] - n:fat[0]]

        XG = [vs_[:, C * i:C * (i + 1)] for i in range(3)]
        YG = [S[:, i, 0:C] for i in range(2)]
        XT = [fcarve(256).rearrange("p (b t) -> p b t", b=2) for _ in range(2)]
        LST = fcarve(2 * MT)
        LT2 = fcarve(2 * MT).rearrange("p (a j) -> p a j", a=2)
        IG, IS, EJI = (fcarve(MT).bitcast(I32) for _ in range(3))
        USED = fcarve(1).bitcast(I32)
        HST = [fcarve(HID) for _ in range(2)]
        WE = [x.rearrange("p (b n) -> p b n", b=2) for x in (rvw[:, :], fcarve(2 * HID))]

        v_dram = nc.dram_tensor("v_scratch", [TOK, C], F32).ap()
        xh_dram = nc.dram_tensor("xh_scratch", [TOK, C], F32).ap()

        block = ctx.enter_context(nc.Block())

        @block.sync
        def _(sp):
            def load(name, dst, src):
                sp.dma_start(dst, src).then_inc(loaded[name], 16)

            load("tokw", TOKW, tokw)
            for t in range(TILES):
                sp.dma_start(XP[:, t], xp[t]).then_inc(patch_loaded[t], 16)
                if t == 0:
                    load("tokb", TOKB[:, :], tokb)
                    load("chan", CH[:, :], chan)
                if t == 1:
                    load("const", CO[:, :], const)
                if t == 4:
                    load("kvrw", KVRW[:, :, :], kvrw)
            load("wow", WOW[:, :, :], wow)
            load("kfw", KFW, kfw)
            load("rfw", RFW, rfw)
            load("vfw", VFW, vfw)
            load("qkvw", QKVW[:, :, :], qkvw)
            load("projw", PROJW[:, :, :], projw)
            load("projb", PROJB[:, :], projb)
            load("gatew", GATEW[:, :, :], gatew)
            load("b2", B2[:, :], b2)
            n_applied = wo_seen = n_experts = 0

            def experts(upto):
                nonlocal n_experts
                for e in range(n_experts, upto):
                    load("w1a", W1A[:, e, :], w1a[:, e, :])
                    load("w1b", W1B[0:C1 + 1, e, :], w1b[:, e, :])
                    load("w2", W2[:, e, :], w2[:, e, :])
                n_experts = upto

            for step in STEPS:
                kind, g = step[0], step[-1]
                if kind == "apply":
                    n_applied += 1
                if kind == "apply" and step[1] == "g":
                    sp.wait_ge(xh_ready, n_applied)
                    sp.dma_start(xh_dram[GT * g:GT * (g + 1), :].rearrange("(t p) c -> p t c", p=T),
                                 XH[:, GTILES * (g % 2):GTILES * (g % 2 + 1), :]).then_inc(xh_stored[g], 16)
                if kind == "vt":
                    for t in group_tiles(g):
                        taken(sp, ("vt", t))
                    sp.dma_start(v_dram[GT * g:GT * (g + 1), :].rearrange("(t p) c -> p t c", p=T), VT[:, :, :]).then_inc(v_stored[g], 16)
                if kind == "vl":
                    half = step[1]
                    sp.wait_ge(v_stored[g], 16)
                    if g:
                        full(sp, ("pv", GI // 2 * (g - 1) + 2 * half + 1))
                    images = slice(4 * half, 4 * half + 4)
                    src = v_dram[GT * g:GT * (g + 1), :].rearrange("(i t) c -> t i c", t=NT)[:, images, :]
                    for h in range(HS):
                        sp.dma_start(VS[NT * h:NT * (h + 1), images, :], src).then_inc(v_loaded[2 * g + half], 16)
                if kind == "wo":
                    wo_seen += 1
                if kind == "pt" and wo_seen == G:
                    if n_experts == 0:
                        full(sp, ("wo", TILES - 1))
                        full(sp, ("wo", TILES - GTILES - 1))
                    full(sp, step)
                    experts((g + 1) * E // (G * GI // 2))
            sp.wait_ge(index_ready, 1)
            for t in range(0, TILES, 2):
                taken(sp, ("b2", t))
            sp.dma_start(out[0:TOK, :].rearrange("(t p) c -> p t c", p=T), H[:, :, :]).then_inc(base_stored, 16)
            sp.dma_start(out[TOK:TOK + 128, :], O[:, 0, :]).then_inc(base_stored, 16)
            sp.wait_ge(base_stored, 32)
            sp.wait_ge(all_added, 1)

        @block.gpsimd
        def _(pool):
            ch = Chain(pool, pool_step)
            for x in (E1F, E1B, E2F, E2B, EVF, EVB):
                ch.then(pool.memset(x, 0.0))
            for x in K:
                ch.then(pool.memset(x, FAR))
            ch.then(pool.memset(W, 2 * FAR))
            ch.then(pool.memset(QT[:, :, :, GT:GT + 32], 0.0))
            ch.settle()
            pool.sem_inc(cleared, 1)
            pool.wait_ge(loaded["const"], 16)

            PTT = pool.tensor_tensor
            nstat = 0
            for step in STEPS:
                kind, g = step[0], step[-1]
                if kind in ("wkv", "evb", "den"):
                    c = step[1]
                    p = [dense(P3[:, i * WN:(i + 1) * WN]) for i in range(3)]
                if kind == "wkv" and step[2] == 1:
                    pool.wait_ge(scan_ready, 2 * c + 1)
                    PTT(here(E1B), behind(MB), here(MB), ALU.subtract).then_inc(diffb_ready, 1)
                    PTT(here(E2B), here(K[c]), here(MB), ALU.subtract).then_inc(diffb_ready, 1)
                if kind == "evb":
                    pool.wait_ge(exp_ready, 5 * c + 4)
                    for gg in (2 * c, 2 * c + 1):
                        for b in range(2):
                            taken(pool, ("kvr", gg, 1, b))
                    PTT(here(EVB), here(E2B), here(V[c]), ALU.mult).then_inc(evb_ready, 1)
                if kind == "den":
                    pool.wait_ge(exp_ready, 5 * c + 5)
                    pool.wait_ge(scan_ready, 2 * c + 2)
                    ch.then(PTT(here(E1F), p[0], before(E2F), ALU.mult))
                    ch.step(PTT(here(E1B), p[1], behind(E2B), ALU.mult))
                    PTT(here(E1F), here(E1F), here(E1B), ALU.add).then_inc(den_ready, 1)
                if kind == "stats":
                    n = 2 if step[1] in "ab" else 1
                    pool.wait_ge(var_ready, nstat + 1)
                    src = VA[:, g, 0:n, :].rearrange("p a t -> p (a t)")
                    dst = RS[:, g, 0:n, :].rearrange("p a t -> p (a t)")
                    pool.tensor_tensor(dst, src, const_("power", T)[:, 0:n * GTILES], ALU.pow).then_inc(rstd_ready, 1)
                    nstat += 1
                if kind == "hx":
                    for t in group_tiles(g):
                        taken(pool, ("wo", t))
                    sl = slice(GTILES * g, GTILES * (g + 1))
                    pool.tensor_tensor(H[:, sl, :], H[:, sl, :], X[:, sl, :], ALU.add).then_inc(hx_ready, 1)
                if kind == "resid":
                    pool.wait_ge(rstd_ready, LNS.index(step[1:]) + 1)
                    for i, t in enumerate(group_tiles(g)):
                        ins = pool.tensor_scalar(X[:, t, :], H[:, t, :], MV[:, t, 0:1], RS[:, g, 0, i:i + 1], ALU.subtract, ALU.mult)
                        if step[1] == "a":
                            ins.then_inc(x_ready[g], 1)
                        else:
                            ch.then(ins)
                    if step[1] == "b":
                        pool.wait_ge(loaded["projb"], 16)
                        ch.settle()
                        sl = slice(GTILES * g, GTILES * (g + 1))
                        pool.tensor_tensor(X[:, sl, :], X[:, sl, :], bc(PROJB[:, :].unsqueeze(1), [T, GTILES, C]),
                                           ALU.add).then_inc(xpb_ready, 1)
                if kind == "v":
                    gg, q = divmod(g, GI // 2)
                    pool.wait_ge(v_loaded[2 * gg + q // 2], 16 * HS)
                    vs = VS[:, 2 * q:2 * q + 2, :]
                    PTT(vs, vs, bc(const_("slab", HS * NT).unsqueeze(1), [HS * NT, 2, C]), ALU.mult).then_inc(vs_ready, 1)
                if kind == "base":
                    for t in group_tiles(g):
                        taken(pool, ("proj", t))
                    sl = slice(GTILES * g, GTILES * (g + 1))
                    pool.tensor_tensor(H[:, sl, :], H[:, sl, :], X[:, sl, :], ALU.add).then_inc(base_ready, 1)

            pool.wait_ge(ge_ready, 1)
            pool.tensor_tensor(AA, GE[:, :, 0:MT], GE[:, :, 1:MT + 1], ALU.subtract).then_inc(aa_ready, 1)
            pool.wait_ge(aa_ready, 1)
            token = const_("token", T)
            for c in range(2):
                sl = slice(TILES * c, TILES * (c + 1))
                pool.tensor_tensor(RT[:, sl, 0:MT], AA[:, sl, :], bc(token.unsqueeze(2), [T, TILES, MT]), ALU.mult).then_inc(rt_ready, 1)
            pool.wait_ge(bb_ready, 1)
            for i in range(NDVE, NC2):
                pool.tensor_scalar(ONEB[:, i, :], const_("iota", T), BB[:, i:i + 1], None, ALU.is_equal).then_inc(table2_ready, 1)

            pool.wait_ge(index_ready, 1)
            for g in range(G):
                pool.wait_ge(xh_stored[g], 16)

            def gather(j):
                if j >= 3:
                    full(pool, ("xt", j - 3))
                pool.indirect_dma_start(XG[j % 3], None, xh_dram[:, :],
                                        bass.IndirectOffsetOnAxis(ap=IG[:, j:j + 1], axis=0)).then_inc(gathered[j % 3], 16)

            def scatter(j):
                taken(pool, ("y", j))
                if j == 0:
                    pool.wait_ge(base_stored, 32)
                else:
                    pool.wait_ge(scattered, 16 * j)
                pool.indirect_dma_start(out[:, :], bass.IndirectOffsetOnAxis(ap=IS[:, j:j + 1], axis=0),
                                        YG[j % 2], None, compute_op=ALU.add).then_inc(scattered, 16)

            for j in range(3):
                gather(j)
            for j in range(FULL - 2):
                if j + 3 <= min(FULL, MT - 1):
                    gather(j + 3)
                scatter(j)
            n_used = used(pool)

            def gathers(a):
                if a < MT:
                    with pool.If(n_used > a):
                        for j in (a + 1, a + 2):
                            if j < MT:
                                gather(j)

            def done(n):
                pool.wait_ge(scattered, 16 * n)
                pool.sem_inc(all_added, 1)

            def rest(a):
                if a >= MT:
                    return done(MT)
                with pool.If(n_used > a):
                    gathers(a + 2)
                    for j in pair(a):
                        scatter(j)
                    rest(a + 2)
                with pool.Else():
                    done(a)

            gathers(FULL)
            scatter(FULL - 2)
            scatter(FULL - 1)
            rest(FULL)

        @block.scalar
        def _(act):
            ch = Chain(act, act_step)
            A = act.activation
            act.wait_ge(loaded["chan"], 16)
            act.wait_ge(cleared, 1)
            affine = {"a": ("ln1_w", "ln1_b"), "2": ("ln2_w", "ln2_b"), "b": ("n1_w", "n1_b"), "g": ("n2_w", "n2_b")}

            for step in STEPS:
                kind, g = step[0], step[-1]
                if kind == "turn":
                    w, b_ = affine[step[1]]
                    for job in ht_readers(STEPS, step):
                        full(act, job)
                    for b in range(2):
                        rows = 128 if b == 0 else C1
                        job = ("turn", step[1], g, b)
                        ps = full(act, job)
                        ht = HTB if step[1] == "b" else HT
                        ins = A(ht[0:rows, g % 2, b, :], ps[0:rows, 0:GT], ACT.Identity, bias=chan_(b_, b), scale=chan_(w, b))
                        freed(ins, job)
                if kind == "kvr":
                    c, half = divmod(g, 2)
                    if g == 0:
                        act.wait_ge(wu_ready, 1)
                    for w in step[1:2]:
                        for b in range(2):
                            job = ("kvr", g, w, b)
                            ps = full(act, job)
                            lo, hi = (0, 128) if b == 0 else (C1 * half, C1 * half + C1)
                            cols = slice(GI * half, GI * half + GI) if b == 0 else slice(CI, IC)
                            src = ps[lo:hi, 0:GT].rearrange("p (i t) -> p i t", t=NT)

                            def dst(x):
                                return here(x)[lo:hi, cols, :]

                            if w == 0:
                                ch.then(A(dst(K[c]), src, ACT.Identity))
                                ins = A(dst(KU[c]), src, ACT.Identity, bias=WU[lo:hi, 2 + b:3 + b])
                            elif w == 1:
                                ins = A(dst(V[c]), src, ACT.Identity)
                            else:
                                ins = A(dst(ER[c]), src, ACT.Exp, scale=-1.0)
                            freed(ins, job)
                if kind == "wexp":
                    for what in EXPS[step[2]:step[2] + 1]:
                        c = step[1]
                        if what in ("e1b", "e2b"):
                            act.wait_ge(diffb_ready, 2 * c + step[2] - 1)
                        else:
                            act.wait_ge(diff_ready, 3 * c + min(step[2], 2) + 1)
                        if what == "p":
                            A(P3, P3, ACT.Exp).then_inc(exp_ready, 1)
                        elif what in ("e2f", "e2b"):
                            x = here(E2F if what == "e2f" else E2B)
                            A(x, x, ACT.Exp).then_inc(exp_ready, 1)
                        else:
                            x = here(E1F if what == "e1f" else E1B)
                            ch.step(A(x[:, 0:CI, :], x[:, 0:CI, :], ACT.Exp, bias=WU[:, 0:1]))
                            A(x[:, CI:IC, :], x[:, CI:IC, :], ACT.Exp, bias=WU[:, 1:2]).then_inc(exp_ready, 1)
                if kind == "kf":
                    if ffs(STEPS, g):
                        full(act, ("rv", GTILES * ffs(STEPS, g)[0] + GTILES - 1))
                    lo, *_, hi = kf_blocks(step[1])
                    for m in range(lo, hi + 2):
                        if m <= hi:
                            ps = full(act, ("kf", g, m))
                            freed(A(KF[:, m, :], ps[:, 0:GT], ACT.Relu), ("kf", g, m))
                        if m > lo:
                            taken(act, ("kf", g, m - 1))
                            A(KF[:, m - 1, :], KF[:, m - 1, :], ACT.Square).then_inc(kf_ready, 1)
                if kind == "rv":
                    t = step[1]
                    gg, i = divmod(t, GTILES)
                    if ffs(STEPS, gg):
                        act.wait_ge(h_ready, ffs(STEPS, gg)[1])
                    ps = full(act, ("rv", t))
                    A(TH[0:T, i, :], ps[0:T, 0:C], ACT.Tanh, scale=0.5).then_inc(th_ready, 1)
                if kind == "qk":
                    if g >= 2:
                        full(act, ("s", (g - 1) * GI // 2 - 1))
                    ps = full(act, ("q", g))
                    freed(A(QT[:, g % 2, 0, 0:GT], ps[:, 0:GT], ACT.Identity, bias=chan_("q_b", 0)), ("q", g))
                    if g:
                        act.wait_ge(ke_ready, g)
                    ps = full(act, ("k", g))
                    freed(A(KT[:, 0, :], ps[:, 0:GT], ACT.Identity, bias=chan_("k_b", 0)), ("k", g))
                    ps = full(act, ("qk1", g))
                    A(QT[0:C1, g % 2, 1, 0:GT], ps[0:C1, 0:GT], ACT.Identity, bias=chan_("q_b", 1))
                    freed(A(KT[0:C1, 1, :], ps[C1:2 * C1, 0:GT], ACT.Identity, bias=chan_("k_b", 1)), ("qk1", g))
                if kind == "vt":
                    if g:
                        act.wait_ge(v_stored[g - 1], 16)
                    for i, t in enumerate(group_tiles(g)):
                        ps = full(act, ("vt", t))
                        freed(A(VT[:, i, :], ps[0:T, 0:C], ACT.Copy), ("vt", t))
                if kind == "exp":
                    p = step[1]
                    taken(act, ("s", p))
                    A(S[:, p % 2, :], S[:, p % 2, :], ACT.Exp, scale=HD ** -0.5).then_inc(p_ready, 1)
                if kind == "pt":
                    p = step[1]
                    job = ("pt", p)
                    ps = full(act, job)
                    if p >= 2:
                        full(act, ("pv", p - 2))
                    freed(A(PT[:, p % 2, :], ps[0:108, :], ACT.Copy), job)
                if kind == "ot":
                    p = step[1]
                    job = ("ot", p)
                    ps = full(act, job)
                    gg, q = divmod(p, GI // 2)
                    if q == 0 and gg >= 2:
                        full(act, ("proj", GTILES * (gg - 1) - 1))
                    for b in range(2):
                        rows = 128 if b == 0 else C1
                        src = ps[0:rows, 128 * b:128 * b + 128].rearrange("p (a q) -> p a q", a=2)[:, :, 0:NT]
                        dst = OT[0:rows, gg % 2, b, 2 * NT * q:2 * NT * (q + 1)].rearrange("p (a q) -> p a q", a=2)
                        ins = A(dst, src, ACT.Identity, bias=chan_("v_b", b))
                        if b == 1:
                            freed(ins, job)

            act.wait_ge(top_ready, 1)
            A(DD[:, 0:TILES], DD[:, 0:TILES], ACT.Exp).then_inc(e2_ready, 1)
            ps = full(act, ("gturn",))
            freed(A(GFT[:, :], ps[0:T, 0:T], ACT.Copy), ("gturn",))
            taken(act, ("gturn",))
            for t in range(TILES):
                A(GM[:, t, :], GFT[:, :], ACT.Copy, scale=const_("tile", T)[:, t:t + 1]).then_inc(gm_ready, 1)
            act.wait_ge(index_ready, 1)

            def turned(j):
                job = ("xt", j)
                ps = full(act, job)
                if j >= 2:
                    full(act, ("h", j - 2, 1))
                A(XT[j % 2][:, 0, :], ps[:, 0:128], ACT.Identity, bias=chan_("n2_b", 0), scale=chan_("n2_w", 0))
                freed(A(XT[j % 2][0:C1, 1, :], ps[0:C1, 128:256], ACT.Identity, bias=chan_("n2_b", 1), scale=chan_("n2_w", 1)), job)

            def gelu(j):
                if j >= 2:
                    full(act, ("y", j - 2))
                for i in range(2):
                    job = ("h", j, i)
                    ps = full(act, job)
                    freed(A(HST[j % 2][:, 384 * i:384 * (i + 1)], ps[:, 0:384], ACT.Gelu), job)

            turned(0)
            turned(1)
            gelu(0)
            for j in range(1, FULL):
                gelu(j)
                if j + 1 < MT:
                    turned(j + 1)
            n_used = used(act)

            def rest(a):
                if a < MT:
                    with act.If(n_used > a):
                        for j in pair(a):
                            gelu(j)
                            if j + 1 < MT:
                                turned(j + 1)
                        rest(a + 2)

            rest(FULL)

        @block.vector
        def _(dve):
            ch = Chain(dve, dve_step)
            TTR, TS, STT, CP, RED = dve.tensor_tensor, dve.tensor_scalar, dve.scalar_tensor_tensor, dve.tensor_copy, dve.tensor_reduce
            dve.wait_ge(loaded["chan"], 16)
            dve.wait_ge(cleared, 1)
            ch.step(TS(WU[:, 0:4], CH[:, VAT["decay"]:VAT["decay"] + 4], 1.0 / NT, None, ALU.mult))
            ch.step(dve.memset(here(W), 0.0))
            ch.step(TS(here(W)[:, 0:CI, :], here(W)[:, 0:CI, :], WU[:, 0:1], None, ALU.add))
            ch.step(TS(here(W)[:, CI:IC, :], here(W)[:, CI:IC, :], WU[:, 1:2], None, ALU.add))
            dve.sem_inc(wu_ready, 1)
            dve.wait_ge(loaded["tokb"], 16)

            def tok(t):
                ps = full(dve, ("tok", t))
                freed(TTR(H[:, t, :], ps[0:T, 0:C], TOKB[:, :], ALU.add), ("tok", t))

            def stats(kind, g):
                if kind == "a":
                    for t in group_tiles(g):
                        taken(dve, ("tok", t))
                src = H if kind in "ab" else X
                for t in group_tiles(g):
                    ch.then(dve.bn_stats(ST[:, t, :], src[:, t, :]))
                ch.settle()
                for t in group_tiles(g):
                    ch.then(dve.bn_aggr(MV[:, t, :], ST[:, t, :]))
                ch.settle()
                var = MV[:, GTILES * g:GTILES * (g + 1), 1]
                ins = TS(VA[:, g, 0, :], var, EPS, None, ALU.add)
                if kind in "ab":
                    ch.then(ins)
                    ins = TS(VA[:, g, 1, :], var, 1.0 + EPS, EPS * EPS, ALU.mult, ALU.add)
                    ch.step(ins)
                    dve.sem_inc(var_ready, 1)
                else:
                    ins.then_inc(var_ready, 1)

            def apply(kind, g):
                n = LNS.index((kind, g))
                k = APPLIED.index((kind, g))
                dve.wait_ge(rstd_ready, n + 1)
                earlier = [i for i in range(k) if APPLIED[i][1] % 2 == g % 2]
                if earlier:
                    kk, gg = APPLIED[earlier[-1]]
                    full(dve, ("turn", kk, gg, 1))
                    if kk == "g":
                        dve.wait_ge(xh_stored[gg], 16)
                src = H if kind in "ab" else X
                for i, t in enumerate(group_tiles(g)):
                    xh = XH[:, GTILES * (g % 2) + i, :]
                    m = MV[:, t, 0:1]
                    s = RS[:, g, 1 if kind in "ab" else 0, i:i + 1]
                    ch.then(TS(xh, src[:, t, :], m, s, ALU.subtract, ALU.mult))
                ch.settle()
                dve.sem_inc(xh_ready, 1)

            def ready(ins):
                ins.then_inc(diff_ready, 1)

            def exped(n):
                dve.wait_ge(exp_ready, n)

            def wkv(c, part):
                k, ku, v, er = K[c], KU[c], V[c], ER[c]
                e0 = 5 * c
                p = [dense(P3[:, i * WN:(i + 1) * WN]) for i in range(3)]
                t1, t2 = dense(MF[:, 0:WN]), dense(MB[:, 0:WN])
                rev = slice(None, None, -1)
                for w in range(3):
                    if part == (0, 3, 6)[w]:
                        for g in (2 * c, 2 * c + 1):
                            for b in range(2):
                                taken(dve, ("kvr", g, w, b))
                if part == 0:
                    ch.then(dve.tensor_tensor_scan(MF[:, 0:WL], W[:, 0:WL], k[:, 0:WL], FAR, ALU.add, ALU.max))
                    ch.step(dve.tensor_tensor_scan(MB[:, 0:WL][:, rev], W[:, 0:WL][:, rev], k[:, 0:WL][:, rev], FAR, ALU.add, ALU.max))
                    dve.sem_inc(scan_ready, 1)
                if part == 1:
                    ready(TTR(here(E1F), before(MF), here(MF), ALU.subtract))
                    ready(TTR(here(E2F), here(k), here(MF), ALU.subtract))
                if part == 2:
                    ch.step(TTR(p[0], here(ku), before(MF), ALU.max))
                    ch.step(TTR(p[2], p[0], behind(MB), ALU.max))
                    ch.then(TTR(p[0], before(MF), p[2], ALU.subtract))
                    ch.then(TTR(p[1], behind(MB), p[2], ALU.subtract))
                    ch.settle()
                    ready(TTR(p[2], here(ku), p[2], ALU.subtract))
                if part == 3:
                    exped(e0 + 2)
                    ch.step(TTR(here(EVF), here(E2F), here(v), ALU.mult))
                    ch.then(dve.tensor_tensor_scan(EVF[:, 0:WL], E1F[:, 0:WL], EVF[:, 0:WL], 0.0, ALU.mult, ALU.add))
                    ch.step(dve.tensor_tensor_scan(E2F[:, 0:WL], E1F[:, 0:WL], E2F[:, 0:WL], 0.0, ALU.mult, ALU.add))
                if part == 4:
                    exped(e0 + 4)
                    dve.wait_ge(evb_ready, c + 1)
                    ch.then(dve.tensor_tensor_scan(EVB[:, 0:WL][:, rev], E1B[:, 0:WL][:, rev], EVB[:, 0:WL][:, rev], 0.0, ALU.mult, ALU.add))
                    ch.step(dve.tensor_tensor_scan(E2B[:, 0:WL][:, rev], E1B[:, 0:WL][:, rev], E2B[:, 0:WL][:, rev], 0.0, ALU.mult, ALU.add))
                    dve.sem_inc(scan_ready, 1)
                if part == 5:
                    exped(e0 + 5)
                    ch.then(TTR(t1, p[0], before(EVF), ALU.mult))
                    ch.step(TTR(t2, p[1], behind(EVB), ALU.mult))
                    ch.step(TTR(t1, t1, t2, ALU.add))
                    ch.step(TTR(t2, p[2], here(v), ALU.mult))
                    ch.step(TTR(t1, t1, t2, ALU.add))
                if part == 6:
                    dve.wait_ge(den_ready, c + 1)
                    ch.step(TTR(p[0], here(E1F), p[2], ALU.add))
                    ch.step(STT(p[1], here(er), 1.0, p[0], ALU.add, ALU.mult))
                    ch.step(dve.reciprocal(p[0], p[1]))
                    TTR(dense(Z[c]), t1, p[0], ALU.mult).then_inc(z_ready, 1)
                    dve.wait_ge(z_ready, c + 1)

            def wo(g):
                dve.wait_ge(x_ready[g], GTILES)
                for t in group_tiles(g):
                    ps = full(dve, ("wo", t))
                    freed(TTR(X[:, t, :], ps[0:T, 0:C], X[:, t, :], ALU.add), ("wo", t))
                for t in group_tiles(g):
                    taken(dve, ("wo", t))

            nth, nff, nproj = [0], [0], [0]

            def rv(t):
                ps = full(dve, ("rv", t))
                nth[0] += 1
                dve.wait_ge(th_ready, nth[0])
                freed(STT(TH[0:T, t % GTILES, :], TH[0:T, t % GTILES, :], 1.0, ps[0:T, C:2 * C], ALU.add, ALU.mult), ("rv", t))

            def ff(g):
                nff[0] += 1
                dve.wait_ge(hx_ready, nff[0])
                for i, t in enumerate(group_tiles(g)):
                    taken(dve, ("rv", t))
                    ch.then(STT(H[:, t, :], TH[0:T, i, :], 0.5, H[:, t, :], ALU.mult, ALU.add))
                ch.settle()
                dve.sem_inc(h_ready, 1)

            def spread(g):
                if g == 0:
                    dve.wait_ge(loaded["const"], 16)
                    full(dve, ("tok", TILES - 1))
                if g >= 2:
                    full(dve, ("s", (g - 1) * GI // 2 - 1))
                for b, heads in ((0, 8), (1, 4)):
                    taken(dve, ("k", g) if b == 0 else ("qk1", g))
                    rows = 128 if b == 0 else C1
                    at_ = 0 if b == 0 else GI * 8 * NT
                    ke = KE[g % 2][0:rows, at_:at_ + GI * heads * NT].rearrange("p (i h t) -> p i h t", i=GI, h=heads)
                    src = KT[0:rows, b, :].rearrange("p (i t) -> p i t", i=GI)
                    for h in range(heads):
                        ins = TS(ke[:, :, h, :], src, const_(f"head{b}", rows)[:, h:h + 1], None, ALU.mult)
                        if (b, h) == (1, 3):
                            ins.then_inc(ke_ready, 1)

            def score(p):
                ps = full(dve, ("s", p))[:, 0:NH * NT].rearrange("p (h k) -> p h k", h=NH)
                e = S[:, p % 2, :].rearrange("p (h k) -> p h k", h=NH)
                ch.step(RED(MX[:, p % 2, :], ps, AX.X, ALU.max))
                if p >= 2:
                    full(dve, ("pt", p - 2))
                freed(TTR(e, ps, bc(MX[:, p % 2, :].unsqueeze(2), [128, NH, NT]), ALU.subtract), ("s", p))

            def sums(p):
                e = S[:, p % 2, :].rearrange("p (h k) -> p h k", h=NH)
                dve.wait_ge(p_ready, p + 1)
                ch.step(RED(SUM[:, p % 2, :], e, AX.X, ALU.add))
                ch.step(dve.reciprocal(RI[:, p % 2, :], SUM[:, p % 2, :]))

            def weighted(p):
                ps = full(dve, ("pv", p))
                if p >= 2:
                    full(dve, ("ot", p - 2))
                for a in range(2):
                    r = slice(64 * a, 64 * a + 64)
                    ins = TTR(O[r, p % 2, :].rearrange("p (h d) -> p h d", h=NH), ps[r, C * a:C * (a + 1)].rearrange("p (h d) -> p h d", h=NH),
                              bc(RI[r, p % 2, :].unsqueeze(2), [64, NH, HD]), ALU.mult)
                freed(ins, ("pv", p))

            def proj(g):
                nproj[0] += 1
                dve.wait_ge(xpb_ready, projs(STEPS, g))
                for t in group_tiles(g):
                    ps = full(dve, ("proj", t))
                    freed(TTR(X[:, t, :], ps[0:T, 0:C], X[:, t, :], ALU.add), ("proj", t))
                for t in group_tiles(g):
                    taken(dve, ("proj", t))

            def logits(g):
                ps = full(dve, ("lg", g))[0:T, 0:GTILES * E].rearrange("p (t e) -> p t e", e=E)
                freed(CP(LG[:, GTILES * g:GTILES * (g + 1), :], ps), ("lg", g))
                taken(dve, ("lg", g))
                for t in group_tiles(g):
                    ch.then(dve.max(TOP[:, t, :], LG[:, t, :]))
                ch.settle()
                for t in group_tiles(g):
                    ch.then(dve.max_index(TIX[:, t, :], TOP[:, t, :], LG[:, t, :]))
                ch.settle()

            for step in STEPS:
                kind, x = step[0], step[-1]
                if kind == "tok":
                    tok(x)
                elif kind == "stats":
                    stats(step[1], x)
                elif kind == "apply":
                    apply(step[1], x)
                elif kind == "wkv":
                    wkv(step[1], step[2])
                elif kind == "wo":
                    wo(x)
                elif kind == "rv":
                    rv(x)
                elif kind == "ff":
                    ff(x)
                elif kind == "spread":
                    spread(x)
                elif kind == "s":
                    score(x)
                elif kind == "pt":
                    sums(x)
                elif kind == "pv":
                    weighted(x)
                elif kind == "proj":
                    proj(x)
                elif kind == "logits":
                    logits(x)

            def te(x):
                return x.rearrange("p (t e) -> p t e", e=E)

            iota = const_("iota", T)
            ch.step(TTR(DD[:, 0:TILES], TOP[:, :, 1], TOP[:, :, 0], ALU.subtract))
            dve.sem_inc(top_ready, 1)
            ixf = IXF.rearrange("p (c t) -> p c t", c=2)
            ch.step(CP(ixf, TIX[:, :, 0:2].rearrange("p t c -> p c t")))
            m1, m2, m12, gf, sf, tmp = (te(x[:, :]) for x in (M1, M2, M12, GF, SF, TMP))
            i8 = bc(iota[:, 0:E].unsqueeze(1), [T, TILES, E])
            ch.then(TTR(m1, i8, bc(ixf[:, 0, :].unsqueeze(2), [T, TILES, E]), ALU.is_equal))
            ch.step(TTR(m2, i8, bc(ixf[:, 1, :].unsqueeze(2), [T, TILES, E]), ALU.is_equal))
            ch.step(TTR(m12, m1, m2, ALU.add))
            dve.sem_inc(mask_ready, 1)
            dve.wait_ge(e2_ready, 1)
            g12 = GG.rearrange("p (c t) -> p c t", c=2)
            ch.step(TS(DD[:, TILES:NC2], DD[:, 0:TILES], 1.0, None, ALU.add))
            ch.step(dve.reciprocal(g12[:, 0, :], DD[:, TILES:NC2]))
            ch.step(TTR(g12[:, 1, :], g12[:, 0, :], DD[:, 0:TILES], ALU.mult))
            ch.then(TTR(gf, m1, bc(g12[:, 0, :].unsqueeze(2), [T, TILES, E]), ALU.mult))
            ch.step(TTR(tmp, m2, bc(g12[:, 1, :].unsqueeze(2), [T, TILES, E]), ALU.mult))
            ch.step(TTR(gf, gf, tmp, ALU.add))
            dve.sem_inc(gf_ready, 1)
            ps = full(dve, ("rank",))
            et = lambda x: x.rearrange("p (e t) -> p e t", e=E)
            ch.step(CP(et(TOTC[:, :]), ps[0:T, T:2 * T].rearrange("p (t e) -> p e t", e=E)))
            ch.step(dve.tensor_tensor_scan(CUM[:, :], const_("keep", T), TOTC[:, :], 0.0, ALU.mult, ALU.add))
            ch.then(CP(NE8[:, 0:E], et(CUM[:, :])[:, :, TILES - 1]))
            ch.step(TTR(TOTC[:, :], CUM[:, :], TOTC[:, :], ALU.subtract))
            slot = const_("slot", T)
            n9 = TOK // 128
            ch.step(TTR(CMP[:, :, 0:n9], bc(NE8[:, 0:E].unsqueeze(2), [T, E, n9]), bc(slot[:, 0:n9].unsqueeze(1), [T, E, n9]), ALU.is_gt))
            ch.step(RED(TE8[:, 0:E], CMP[:, :, 0:n9], AX.X, ALU.add))
            ch.step(dve.tensor_tensor_scan(END[:, 0:E], const_("ones", T)[:, 0:E], TE8[:, 0:E], 0.0, ALU.mult, ALU.add))
            ch.step(TTR(BASE[:, 0:E], END[:, 0:E], TE8[:, 0:E], ALU.subtract))
            ch.step(TS(BASE[:, 0:E], BASE[:, 0:E], 128.0, None, ALU.mult))
            freed(TTR(sf, ps[0:T, 0:T].rearrange("p (t e) -> p t e", e=E), et(TOTC[:, :]).rearrange("p e t -> p t e"), ALU.add), ("rank",))
            taken(dve, ("rank",))
            ch.step(TTR(sf, sf, bc(BASE[:, 0:E].unsqueeze(1), [T, TILES, E]), ALU.add))
            for c, m in enumerate((m1, m2)):
                ch.step(TTR(tmp, m, sf, ALU.mult))
                ch.step(RED(SL[:, TILES * c:TILES * (c + 1)], tmp, AX.X, ALU.add))
            ch.step(TTR(GE, bc(SL.unsqueeze(2), [T, NC2, MT + 1]), bc(slot[:, 0:MT + 1].unsqueeze(1), [T, NC2, MT + 1]), ALU.is_ge))
            dve.sem_inc(ge_ready, 1)
            ch.step(RED(AQ, GE[:, :, 1:MT + 1], AX.X, ALU.add))
            ch.step(STT(BB, AQ, -128.0, SL, ALU.mult, ALU.add))
            dve.sem_inc(bb_ready, 1)
            for i in range(NDVE):
                if i == 2:
                    dve.wait_ge(aa_ready, 1)
                    for c in range(2):
                        sl = slice(TILES * c, TILES * (c + 1))
                        ch.then(TTR(RT[:, sl, MT:2 * MT], AA[:, sl, :], bc(g12[:, c, :].unsqueeze(2), [T, TILES, MT]), ALU.mult))
                    ch.settle()
                    dve.sem_inc(rt_ready, 1)
                TS(ONEB[:, i, :], iota, BB[:, i:i + 1], None, ALU.is_equal).then_inc(table_ready, 1)
            ch.step(TTR(EJC[:, :, :], bc(iota[:, 0:MT].unsqueeze(2), [T, MT, E]), bc(END[:, 0:E].unsqueeze(1), [T, MT, E]), ALU.is_ge))
            ch.step(RED(EJ[:, :], EJC[:, :, :], AX.X, ALU.add))
            ch.then(TS(EJI[0:T, :], EJ[:, :], float(E - 1), None, ALU.min))
            ch.step(CP(USED[0:T, :], END[:, E - 1:E]))
            ch.then(dve.memset(O[:, 0, :], 0.0))
            for j in range(2):
                ch.then(dve.memset(XT[j][C1:C1 + 1, 1, :], 1.0))
            def weights(j):
                if j >= 2:
                    full(dve, ("h", j - 2, 1))
                e = dve.value_load(EJI[0:1, j:j + 1], min_val=0, max_val=E - 1)
                we = WE[j % 2]
                ch.then(CP(we[:, 0:1, :], W1A[:, bass.ds(e, 1), :]))
                ch.step(CP(we[0:C1 + 1, 1:2, :], W1B[0:C1 + 1, bass.ds(e, 1), :]))
                dve.sem_inc(we_ready, 1)

            full(dve, ("rv", TILES - 1))
            dve.wait_ge(loaded["w1a"], 16 * E)
            dve.wait_ge(loaded["w1b"], 16 * E)
            weights(0)
            ps = full(dve, ("list",))
            freed(CP(LST[:, :], ps[:, 0:2 * MT]), ("list",))
            taken(dve, ("list",))
            ch.then(TS(LT2[:, 0, :], LST[:, 0:MT], -1.0, 0.0, ALU.add, ALU.max))
            ch.then(TS(LT2[:, 1, :], LST[:, 0:MT], 0.0, const_("spare"), ALU.is_equal, ALU.mult))
            ch.settle()
            ch.then(CP(IG[:, :], LT2[:, 0, :]))
            ch.then(STT(IS[:, :], LST[:, 0:MT], -1.0, LT2[:, 1, :], ALU.add, ALU.add))
            ch.settle()
            dve.sem_inc(index_ready, 1)

            dve.wait_ge(base_ready, G)
            for t in range(0, TILES, 2):
                ps = full(dve, ("b2", t))[0:T, 0:2 * C].rearrange("p (t c) -> p t c", t=2)
                freed(TTR(H[:, t:t + 2, :], ps, H[:, t:t + 2, :], ALU.add), ("b2", t))
                if t == 4:
                    weights(1)


            def gated(j):
                if j + 2 < MT:
                    weights(j + 2)
                if j >= 2:
                    dve.wait_ge(scattered, 16 * (j - 1))
                ps = full(dve, ("y", j))
                freed(TS(YG[j % 2], ps[:, 0:C], LST[:, MT + j:MT + j + 1], None, ALU.mult), ("y", j))

            for j in range(FULL):
                gated(j)
            n_used = used(dve)

            def rest(a):
                if a < MT:
                    with dve.If(n_used > a):
                        for j in pair(a):
                            gated(j)
                        rest(a + 2)

            rest(FULL)

        @block.tensor
        def _(pe):
            ident = const_("ident")
            mm = pe.matmul

            def begin(job):
                b, n = PLACE[job]
                if n:
                    pe.wait_ge(bank_free[b], n)
                return banks[:, b, :]

            def end(ins, job):
                ins.then_inc(bank_full[PLACE[job][0]], 1)

            pe.wait_ge(loaded["tokw"], 16)
            tw = TOKW.rearrange("p (k c) -> p k c", k=KP)

            def over_channels(dst, moving, stationary):
                mm(dst, stationary[0], moving[0], start=True, stop=False)
                return mm(dst, stationary[1], moving[1], start=False, stop=True)

            def w_(wt, lo, hi, base=0):
                return wt[:, 0, lo:hi], wt[base:base + C1, 1, lo:hi]

            def h_(g, lo, hi, ht=HT):
                return ht[:, g % 2, 0, lo:hi], ht[0:C1, g % 2, 1, lo:hi]

            seen = set()

            def need(*ns):
                for n in ns:
                    if n not in seen:
                        pe.wait_ge(loaded[n], 16)
                        seen.add(n)

            for step in STEPS:
                kind, g = step[0], step[-1]
                if kind == "tok":
                    pe.wait_ge(patch_loaded[g], 16)
                    ps = begin(("tok", g))
                    for k in range(KP):
                        ins = mm(ps[0:T, 0:C], XP[:, g, k, :], tw[:, k, :], start=(k == 0), stop=(k == KP - 1))
                    end(ins, ("tok", g))
                elif kind == "turn":
                    need("const")
                    pe.wait_ge(xh_ready, APPLIED.index(step[1:]) + 1)
                    for b in range(2):
                        job = ("turn", step[1], g, b)
                        ps = begin(job)
                        rows = 128 if b == 0 else C1
                        for i in range(GTILES):
                            ins = pe.transpose(ps[0:rows, T * i:T * (i + 1)], XH[:, GTILES * (g % 2) + i, 128 * b:128 * b + rows], ident[0:T, 0:T])
                        end(ins, job)
                elif kind == "kvr":
                    need("kvrw")
                    turned_(pe, "a", g)
                    for w in step[1:2]:
                        for b in range(2):
                            ps = begin(("kvr", g, w, b))
                            lo, n = C * w + 128 * b, 128 if b == 0 else C1
                            base = 0 if b == 0 else C1 * (g % 2)
                            end(over_channels(ps[base:base + n, 0:GT], h_(g, 0, GT), w_(KVRW, lo, lo + n)), ("kvr", g, w, b))
                elif kind == "wo":
                    need("wow")
                    c, half = divmod(g, 2)
                    pe.wait_ge(z_ready, c + 1)
                    base = C1 * half
                    for i, t in enumerate(group_tiles(g)):
                        ps = begin(("wo", t))
                        z0 = Z[c][:, GT * half + T * i:GT * half + T * (i + 1)]
                        z1 = Z[c][base:base + C1, CI * NT + T * i:CI * NT + T * (i + 1)]
                        end(over_channels(ps[0:T, 0:C], w_(WOW, 0, C, base), (z0, z1)), ("wo", t))
                elif kind == "kf":
                    need("kfw", "rfw", "vfw")
                    turned_(pe, "2", g)
                    for m in kf_blocks(step[1]):
                        ps = begin(("kf", g, m))
                        end(over_channels(ps[:, 0:GT], h_(g, 0, GT), w_(KFW, 128 * m, 128 * (m + 1))), ("kf", g, m))
                elif kind == "rv":
                    t = step[1]
                    gg, i = divmod(t, GTILES)
                    nth = ffs(STEPS, gg)[1] if ffs(STEPS, gg) else 0
                    ps = begin(("rv", t))
                    over_channels(ps[0:T, 0:C], w_(RFW, 0, C), h_(gg, T * i, T * (i + 1)))
                    if i == 0:
                        pe.wait_ge(kf_ready, HB * (nth + 1))
                    for m in range(HB):
                        ins = mm(ps[0:T, C:2 * C], KF[:, m, T * i:T * (i + 1)], VFW[:, m, :], start=(m == 0), stop=(m == HB - 1))
                    end(ins, ("rv", t))
                elif kind == "qk":
                    need("qkvw")
                    turned_(pe, "b", g)
                    for w, n in enumerate("qk"):
                        ps = begin((n, g))
                        end(over_channels(ps[:, 0:GT], h_(g, 0, GT, HTB), w_(QKVW, C * w, C * w + 128)), (n, g))
                    ps = begin(("qk1", g))
                    for b in range(2):
                        for w in range(2):
                            rows = 128 if b == 0 else C1
                            lo = C * w + 128
                            ins = mm(ps[C1 * w:C1 * (w + 1), 0:GT], QKVW[0:rows, b, lo:lo + C1], HTB[0:rows, g % 2, b, :], start=(b == 0), stop=(b == 1))
                    end(ins, ("qk1", g))
                elif kind == "s":
                    p = g
                    gg, q = divmod(p, GI // 2)
                    pe.wait_ge(ke_ready, gg + 1)
                    taken(pe, ("q", gg))
                    taken(pe, ("qk1", gg))
                    ps = begin(("s", p))
                    ke0 = KE[gg % 2][:, 0:GI * 8 * NT].rearrange("p (i n) -> p i n", i=GI)
                    ke1 = KE[gg % 2][0:C1, GI * 8 * NT:].rearrange("p (i n) -> p i n", i=GI)
                    for a in range(2):
                        i = 2 * q + a
                        mm(ps[64 * a:64 * a + 64, 0:8 * NT], QT[:, gg % 2, 0, NT * i:NT * i + 64], ke0[:, i, :], start=True, stop=True)
                    for a in range(2):
                        i = 2 * q + a
                        ins = mm(ps[64 * a:64 * a + 64, 8 * NT:NH * NT], QT[0:C1, gg % 2, 1, NT * i:NT * i + 64], ke1[:, i, :], start=True, stop=True)
                    end(ins, ("s", p))
                elif kind == "vt":
                    need("qkvw")
                    turned_(pe, "b", g)
                    for i, t in enumerate(group_tiles(g)):
                        ps = begin(("vt", t))
                        end(over_channels(ps[0:T, 0:C], w_(QKVW, 2 * C, 3 * C), h_(g, T * i, T * (i + 1), HTB)), ("vt", t))
                elif kind == "pt":
                    p = g
                    pe.wait_ge(p_ready, p + 1)
                    ps = begin(("pt", p))
                    for s in range(NS):
                        ins = pe.transpose(ps[0:108, 128 * s:128 * (s + 1)], S[:, p % 2, 108 * s:108 * (s + 1)], ident)
                    end(ins, ("pt", p))
                elif kind == "pv":
                    p = g
                    ps = begin(("pv", p))
                    taken(pe, ("pt", p))
                    pe.wait_ge(vs_ready, p + 1)
                    q = p % (GI // 2)
                    ve = VS[:, 2 * q:2 * q + 2, :]
                    po = ps[:, 0:2 * C].rearrange("p (a c) -> p a c", a=2)
                    for s in range(NS):
                        ins = mm(po[:, :, 48 * s:48 * (s + 1)], PT[:, p % 2, 128 * s:128 * (s + 1)],
                                 ve[:, :, 48 * s:48 * (s + 1)], start=True, stop=True)
                    end(ins, ("pv", p))
                elif kind == "ot":
                    p = g
                    taken(pe, ("pv", p))
                    ps = begin(("ot", p))
                    pe.transpose(ps[:, 0:128], O[:, p % 2, 0:128], ident)
                    end(pe.transpose(ps[0:C1, 128:256], O[:, p % 2, 128:C], ident), ("ot", p))
                elif kind == "proj":
                    need("projw")
                    for p in range(GI // 2 * g, GI // 2 * (g + 1)):
                        taken(pe, ("ot", p))
                    for i, t in enumerate(group_tiles(g)):
                        ps = begin(("proj", t))
                        o0 = OT[:, g % 2, 0, T * i:T * (i + 1)]
                        o1 = OT[0:C1, g % 2, 1, T * i:T * (i + 1)]
                        end(over_channels(ps[0:T, 0:C], w_(PROJW, 0, C), (o0, o1)), ("proj", t))
                elif kind == "logits":
                    need("gatew")
                    turned_(pe, "g", g)
                    ps = begin(("lg", g))
                    for i in range(GTILES):
                        ins = over_channels(ps[0:T, E * i:E * (i + 1)], w_(GATEW, 0, E), h_(g, T * i, T * (i + 1)))
                    end(ins, ("lg", g))

            pe.wait_ge(mask_ready, 1)
            ps = begin(("rank",))
            mm(ps[0:T, 0:T], const_("before", T), M12[:, :], start=True, stop=True)
            end(mm(ps[0:T, T:2 * T], const_("ones", T), M12[:, :], start=True, stop=True), ("rank",))
            pe.wait_ge(gf_ready, 1)
            ps = begin(("gturn",))
            end(pe.transpose(ps[0:T, 0:T], GF[:, :], ident[0:T, 0:T]), ("gturn",))
            need("b2")
            for t in range(0, TILES, 2):
                pe.wait_ge(gm_ready, t + 2)
                ps = begin(("b2", t))
                mm(ps[0:T, 0:C], GM[:, t, :], B2[:, :], start=True, stop=True)
                end(mm(ps[0:T, C:2 * C], GM[:, t + 1, :], B2[:, :], start=True, stop=True), ("b2", t))
            ps = begin(("list",))
            pe.wait_ge(rt_ready, 3)
            for i in range(NC2):
                if i < NDVE:
                    pe.wait_ge(table_ready, i + 1)
                else:
                    pe.wait_ge(table2_ready, i - NDVE + 1)
                ins = mm(ps[:, 0:2 * MT], ONEB[:, i, :], RT[:, i, :], start=(i == 0), stop=(i == NC2 - 1))
            end(ins, ("list",))

            for n in ("w1a", "w1b", "w2"):
                pe.wait_ge(loaded[n], 16 * E)

            def tile_expert(j):
                return pe.value_load(EJI[0:1, j:j + 1], min_val=0, max_val=E - 1)

            def turn_tokens(j):
                pe.wait_ge(gathered[j % 3], 16 * (j // 3 + 1))
                ps = begin(("xt", j))
                pe.transpose(ps[:, 0:128], XG[j % 3][:, 0:128], ident)
                end(pe.transpose(ps[0:C1, 128:256], XG[j % 3][:, 128:C], ident), ("xt", j))

            def up(j):
                if j < FULL:
                    expert[j] = tile_expert(j)
                taken(pe, ("xt", j))
                if j == 0:
                    pe.wait_ge(index_ready, 1)
                pe.wait_ge(we_ready, j + 1)
                for i in range(2):
                    ps = begin(("h", j, i))
                    for k in range(3):
                        at_ = 384 * i + 128 * k
                        h = ps[:, 128 * k:128 * (k + 1)]
                        mm(h, WE[j % 2][:, 0, at_:at_ + 128], XT[j % 2][:, 0, :], start=True, stop=False)
                        ins = mm(h, WE[j % 2][0:C1 + 1, 1, at_:at_ + 128], XT[j % 2][0:C1 + 1, 1, :], start=False, stop=True)
                    end(ins, ("h", j, i))

            def down(j):
                e = expert[j] if j < FULL else tile_expert(j)
                ps = begin(("y", j))
                for k in range(HB):
                    if k % 3 == 0:
                        taken(pe, ("h", j, k // 3))
                    ins = mm(ps[:, 0:C], HST[j % 2][:, 128 * k:128 * (k + 1)], W2[:, bass.ds(e, 1), C * k:C * (k + 1)],
                             start=(k == 0), stop=(k == HB - 1))
                end(ins, ("y", j))

            expert = {}
            turn_tokens(0)
            turn_tokens(1)
            up(0)
            n_used = used(pe)

            def ahead(j):
                if j + 1 < MT:
                    up(j + 1)
                if j + 2 < MT:
                    turn_tokens(j + 2)

            for j in range(FULL - 1):
                ahead(j)
                down(j)

            def rest(a):
                if a >= MT:
                    down(MT - 1)
                    return
                with pe.If(n_used > a):
                    ahead(a - 1)
                down(a - 1)
                with pe.If(n_used > a):
                    if a + 1 < MT:
                        ahead(a)
                        down(a)
                    rest(a + 2)

            rest(FULL)


EXPS = ("e1f", "e2f", "e1b", "e2b", "p")


def ffs(steps, g):
    order = [s[-1] for s in steps if s[0] == "ff"]
    n = order.index(g)
    return (order[n - 1], n) if n else None


def projs(steps, g):
    return [s[-1] for s in steps if s[0] == "resid" and s[1] == "b"].index(g) + 1


def ht_readers(steps, step):
    n, kind, g = steps.index(step), step[1], step[2]
    if kind == "b" and g >= 2:
        return [("vt", GTILES * (g - 1) - 1), ("qk1", g - 2)]
    for s in reversed(steps[:n]):
        if kind == "b":
            if s[0] == "kvr":
                return [jobs_of(s)[-1]]
        elif s[0] in ("kvr", "rv", "logits"):
            group = s[1] // GTILES if s[0] == "rv" else s[-1]
            if group % 2 == g % 2:
                return [jobs_of(s)[-1]]
    return []


def kernel(**inputs):
    import numpy as np
    import concourse.bacc as bacc
    from concourse.bass_utils import run_bass_kernel_spmd

    a = {k: np.asarray(v) for k, v in inputs.items()}

    def blocks(w):
        return np.stack([w[0:128], np.concatenate([w[128:192], w[128:192]])], 1)

    def rows(v, n):
        return np.broadcast_to(v, (n, len(v)))

    qb = a["L0_ffn_qkv_b"]
    vectors = {"ln1_w": a["L0_attn_ln1_w"], "ln1_b": a["L0_attn_ln1_b"], "ln2_w": a["L0_attn_ln2_w"], "ln2_b": a["L0_attn_ln2_b"],
               "n1_w": a["L0_ffn_norm1_w"], "n1_b": a["L0_ffn_norm1_b"], "n2_w": a["L0_ffn_norm2_w"], "n2_b": a["L0_ffn_norm2_b"],
               "decay": a["L0_attn_decay"], "first": a["L0_attn_first"], "q_b": qb[0:C], "k_b": qb[C:2 * C], "v_b": qb[2 * C:]}
    chan = np.concatenate([blocks(vectors[n][:, None])[:, :, 0] for n in CHAN], 1)

    p = np.arange(128)[:, None]
    parts = {
        "ident": np.eye(128), "iota": np.arange(128) + 0 * p, "before": p < np.arange(T), "ones": np.ones((128, T)),
        "head0": p // HD == np.arange(8), "head1": p // HD == np.arange(4),
        "slab": p // NT == (np.arange(C) // HD) % HS, "slot": 128 * np.arange(MT + 1) + 0 * p,
        "token": T * np.arange(TILES) + p + 1, "spare": TOK + 1 + p, "keep": (np.arange(E * TILES) % TILES > 0) + 0 * p,
        "tile": p // E == np.arange(TILES), "power": np.full((128, 6), -0.5)}
    const = np.concatenate([parts[n].astype(np.float32) for n, _ in CONST], 1)

    x = a["x"].reshape(G, GI, 3, 6, 16, 6, 16)
    xp = x.transpose(2, 4, 6, 0, 1, 3, 5).reshape(KP, 128, TILES, T).transpose(2, 1, 0, 3)
    w1 = a["L0_ffn_W1"].transpose(1, 0, 2)
    arrays = {
        "xp": xp, "chan": chan, "const": const,
        "tokw": a["L0_tok_W"].T.reshape(KP, 128, C).transpose(1, 0, 2).reshape(128, KP * C), "tokb": rows(a["L0_tok_b"], T),
        "kvrw": blocks(np.concatenate([a["L0_attn_Wk_a"].T, a["L0_attn_Wv_a"].T, a["L0_attn_Wr_a"].T], 1)),
        "wow": blocks(a["L0_attn_Wo_a"].T), "kfw": blocks(a["L0_attn_Wk_f"].T), "rfw": blocks(a["L0_attn_Wr_f"].T),
        "vfw": a["L0_attn_Wv_f"].T.reshape(HB, 128, C).transpose(1, 0, 2),
        "qkvw": blocks(a["L0_ffn_qkv_w"].T), "projw": blocks(a["L0_ffn_proj_w"].T), "projb": rows(a["L0_ffn_proj_b"], T),
        "gatew": blocks(a["L0_ffn_w_gate"]), "w1a": w1[0:128], "w1b": np.concatenate([w1[128:192], a["L0_ffn_b1"][None]]),
        "w2": a["L0_ffn_W2"].reshape(E, HB, 128, C).transpose(2, 0, 1, 3).reshape(128, E, HB * C),
        "b2": np.tile(a["L0_ffn_b2"], (TILES, 1)),
    }
    nc = bacc.Bacc("TRN2", target_bir_lowering=False, num_devices=1)
    data, args = {}, {}
    for name, v in arrays.items():
        data["in_" + name] = np.ascontiguousarray(v)
        args[name] = nc.dram_tensor("in_" + name, v.shape, F32, kind="ExternalInput").ap()
    args["out"] = nc.dram_tensor("out_0", (TOK + 128, C), F32, kind="ExternalOutput").ap()
    build(nc, **args)
    r = run_bass_kernel_spmd(nc, [data], core_ids=[0])
    return r.results[0]["out_0"][0:TOK].reshape(B, NT, C)
```
